# Optimizing a Trainium2 kernel written in Bass

```python
import numpy as np
import jax
import jax.numpy as jnp

def _softmax(x, axis=-1):
    return jax.nn.softmax(x, axis=axis)

def _gelu(x):
    return jax.nn.gelu(x, approximate=True)

def _silu(x):
    return jax.nn.silu(x)

def _sigmoid(x):
    return jax.nn.sigmoid(x)

def _layernorm(x, axis=-1, eps=1e-05):
    m = jnp.mean(x, axis=axis, keepdims=True)
    v = jnp.var(x, axis=axis, keepdims=True)
    return (x - m) / jnp.sqrt(v + eps)

def _scatter_add(tgt, idx, src, axis=0):
    return tgt.at[idx].add(src)

def _segment_sum(src, seg, n):
    return jax.ops.segment_sum(src, seg, n)
kernel_name = 'mk_hybrid_d1_jaxref_r4_f16a58'

def setup_inputs(seed: int=0):
    np.random.seed(seed)
    _w = jnp.asarray

    def _L0_attn_a_setup():
        import jax, jax.numpy as jnp
        import numpy as np
        H, DK, DV, HID, KSZ, CHUNK = (6, 64, 128, 512, 4, 64)
        EPS = 1e-05

        def _short_conv(x, w):
            C, K = (w.shape[0], w.shape[2])
            y = jax.lax.conv_general_dilated(x.transpose(0, 2, 1), w, window_strides=(1,), padding=[(K - 1, 0)], feature_group_count=C, dimension_numbers=('NCH', 'OIH', 'NCH'))
            return jax.nn.silu(y.transpose(0, 2, 1))

        def _l2norm(x, eps=1e-06):
            return x * jax.lax.rsqrt(jnp.sum(x * x, axis=-1, keepdims=True) + eps)
        key = jax.random.key(seed)
        ks = jax.random.split(key, 16)
        B, T = (2, 512)

        def w(k, shape):
            s = 1.0 / np.sqrt(shape[-1] if len(shape) == 2 else shape[-1] * shape[-2] + 1e-09)
            if len(shape) == 3:
                s = 1.0 / np.sqrt(shape[2])
            return jax.random.uniform(k, shape, jnp.float32, -s, s)
        dt = jnp.exp(jax.random.uniform(ks[7], (H,), jnp.float32) * (np.log(0.1) - np.log(0.001)) + np.log(0.001))
        dt = jnp.clip(dt, 0.0001)
        return {'x': jax.random.normal(ks[0], (B, T, HID), jnp.float32), 'Wq': w(ks[1], (H * DK, HID)), 'Wk': w(ks[2], (H * DK, HID)), 'Wv': w(ks[3], (H * DV, HID)), 'Wa': w(ks[4], (H, HID)), 'Wb': w(ks[5], (H, HID)), 'A_log': jnp.log(jax.random.uniform(ks[6], (H,), jnp.float32, 1.0, 16.0)), 'dt_bias': dt + jnp.log(-jnp.expm1(-dt)), 'conv_q_w': w(ks[8], (H * DK, 1, KSZ)), 'conv_k_w': w(ks[9], (H * DK, 1, KSZ)), 'conv_v_w': w(ks[10], (H * DV, 1, KSZ)), 'Wg': w(ks[11], (H * DV, HID)), 'norm_w': jnp.ones((DV,), jnp.float32), 'Wo': w(ks[12], (HID, H * DV))}
    _L0_attn_a_in = _L0_attn_a_setup()

    def _L0_attn_b_setup():
        import jax, jax.numpy as jnp
        import numpy as np
        import math
        D_MODEL = 512
        D_STATE = 64
        R_MIN = 0.0
        R_MAX = 0.9
        MAX_PHASE = 6.283185307179586
        B_SZ = 4
        T_LEN = 512
        key = jax.random.key(seed)
        k_x, k_bre, k_bim, k_cre, k_cim = jax.random.split(key, 5)
        x = jax.random.normal(k_x, (B_SZ, T_LEN, D_MODEL), dtype=jnp.float32)
        u = np.linspace(0.0, 1.0, D_STATE, dtype=np.float64)
        mag_init = np.clip(R_MIN + (R_MAX - R_MIN) * u, 1e-06, 1.0 - 1e-06)
        nu_init = -np.log(mag_init)
        nu_log = jnp.asarray(np.log(np.clip(np.expm1(nu_init), 1e-06, None)), dtype=jnp.float32)
        theta_log = jnp.asarray(np.linspace(math.log(0.0001), math.log(MAX_PHASE), D_STATE), dtype=jnp.float32)
        B_re = jax.random.normal(k_bre, (D_STATE, D_MODEL), dtype=jnp.float32) / math.sqrt(D_MODEL)
        B_im = jax.random.normal(k_bim, (D_STATE, D_MODEL), dtype=jnp.float32) / math.sqrt(D_MODEL)
        C_re = jax.random.normal(k_cre, (D_MODEL, D_STATE), dtype=jnp.float32) / math.sqrt(D_STATE)
        C_im = jax.random.normal(k_cim, (D_MODEL, D_STATE), dtype=jnp.float32) / math.sqrt(D_STATE)
        D = jnp.ones((D_MODEL,), dtype=jnp.float32)
        return {'x': x, 'nu_log': nu_log, 'theta_log': theta_log, 'B_re': B_re, 'B_im': B_im, 'C_re': C_re, 'C_im': C_im, 'D': D}
    _L0_attn_b_in = _L0_attn_b_setup()

    def _L0_ffn_setup():
        import jax, jax.numpy as jnp
        import numpy as np
        E = 32
        K = 4
        G = 4
        TG = 2
        H = 512
        F = 256
        FS = 512
        SCALE = 2.0
        B, S = (2, 256)
        N = B * S
        CAP = 2 * (N * K // E)

        def _gate(x, gate_w, gate_bias):
            logits = x @ gate_w.T
            scores = jax.nn.sigmoid(logits)
            sc = scores + gate_bias
            n = x.shape[0]
            grp = sc.reshape(n, G, E // G)
            group_scores = jax.lax.top_k(grp, 2)[0].sum(-1)
            _, gidx = jax.lax.top_k(group_scores, TG)
            gmask = jnp.zeros((n, G), sc.dtype).at[jnp.arange(n)[:, None], gidx].set(1.0)
            smask = jnp.repeat(gmask, E // G, axis=1)
            tmp = jnp.where(smask > 0, sc, 0.0)
            _, topk_idx = jax.lax.top_k(tmp, K)
            topk_w = jnp.take_along_axis(scores, topk_idx, axis=1)
            topk_w = topk_w / (topk_w.sum(-1, keepdims=True) + 1e-20)
            return (topk_idx, topk_w * SCALE)

        def _moe(x, topk_idx, topk_w, w1, w2, w3):
            n = x.shape[0]
            flat_e = topk_idx.reshape(-1)
            oh = jax.nn.one_hot(flat_e, E, dtype=jnp.int32)
            pos = (jnp.cumsum(oh, axis=0) * oh).sum(-1) - 1
            keep = pos < CAP
            slot = jnp.where(keep, pos, CAP)
            x_rep = jnp.repeat(x, K, axis=0)
            buf = jnp.zeros((E, CAP, H), x.dtype).at[flat_e, slot].set(x_rep, mode='drop')
            h = jax.nn.silu(jnp.einsum('ech,ehf->ecf', buf, w1)) * jnp.einsum('ech,ehf->ecf', buf, w3)
            ob = jnp.einsum('ecf,efh->ech', h, w2)
            y = ob[flat_e, jnp.minimum(slot, CAP - 1)]
            y = jnp.where(keep[:, None], y, 0.0)
            return (y.reshape(n, K, H) * topk_w[:, :, None]).sum(1)
        key = jax.random.key(seed)
        ks = jax.random.split(key, 9)
        w = 0.02
        return {'hidden_states': jax.random.normal(ks[0], (B, S, H), jnp.float32), 'gate_w': jax.random.normal(ks[1], (E, H), jnp.float32) * w, 'gate_bias': jax.random.normal(ks[2], (E,), jnp.float32) * w, 'w1': jax.random.normal(ks[3], (E, H, F), jnp.float32) * w, 'w2': jax.random.normal(ks[4], (E, F, H), jnp.float32) * w, 'w3': jax.random.normal(ks[5], (E, H, F), jnp.float32) * w, 'shared_gate': jax.random.normal(ks[6], (H, FS), jnp.float32) * w, 'shared_up': jax.random.normal(ks[7], (H, FS), jnp.float32) * w, 'shared_down': jax.random.normal(ks[8], (FS, H), jnp.float32) * w}
    _L0_ffn_in = _L0_ffn_setup()
    _d = {'L0_attn_a_x': _L0_attn_a_in['x'], 'L0_attn_a_Wq': _L0_attn_a_in['Wq'], 'L0_attn_a_Wk': _L0_attn_a_in['Wk'], 'L0_attn_a_Wv': _L0_attn_a_in['Wv'], 'L0_attn_a_Wa': _L0_attn_a_in['Wa'], 'L0_attn_a_Wb': _L0_attn_a_in['Wb'], 'L0_attn_a_A_log': _L0_attn_a_in['A_log'], 'L0_attn_a_dt_bias': _L0_attn_a_in['dt_bias'], 'L0_attn_a_conv_q_w': _L0_attn_a_in['conv_q_w'], 'L0_attn_a_conv_k_w': _L0_attn_a_in['conv_k_w'], 'L0_attn_a_conv_v_w': _L0_attn_a_in['conv_v_w'], 'L0_attn_a_Wg': _L0_attn_a_in['Wg'], 'L0_attn_a_norm_w': _L0_attn_a_in['norm_w'], 'L0_attn_a_Wo': _L0_attn_a_in['Wo'], 'L0_attn_b_nu_log': _L0_attn_b_in['nu_log'], 'L0_attn_b_theta_log': _L0_attn_b_in['theta_log'], 'L0_attn_b_B_re': _L0_attn_b_in['B_re'], 'L0_attn_b_B_im': _L0_attn_b_in['B_im'], 'L0_attn_b_C_re': _L0_attn_b_in['C_re'], 'L0_attn_b_C_im': _L0_attn_b_in['C_im'], 'L0_attn_b_D': _L0_attn_b_in['D'], 'L0_ffn_gate_w': _L0_ffn_in['gate_w'], 'L0_ffn_gate_bias': _L0_ffn_in['gate_bias'], 'L0_ffn_w1': _L0_ffn_in['w1'], 'L0_ffn_w2': _L0_ffn_in['w2'], 'L0_ffn_w3': _L0_ffn_in['w3'], 'L0_ffn_shared_gate': _L0_ffn_in['shared_gate'], 'L0_ffn_shared_up': _L0_ffn_in['shared_up'], 'L0_ffn_shared_down': _L0_ffn_in['shared_down']}
    _x0 = _d['L0_attn_a_x']
    _d['L0_attn_a_x'] = jax.random.normal(jax.random.fold_in(jax.random.key(seed), 1), (1, 2048, 512), dtype=_x0.dtype)
    del _x0
    return _d

def reference(L0_attn_a_x, L0_attn_a_Wq, L0_attn_a_Wk, L0_attn_a_Wv, L0_attn_a_Wa, L0_attn_a_Wb, L0_attn_a_A_log, L0_attn_a_dt_bias, L0_attn_a_conv_q_w, L0_attn_a_conv_k_w, L0_attn_a_conv_v_w, L0_attn_a_Wg, L0_attn_a_norm_w, L0_attn_a_Wo, L0_attn_b_nu_log, L0_attn_b_theta_log, L0_attn_b_B_re, L0_attn_b_B_im, L0_attn_b_C_re, L0_attn_b_C_im, L0_attn_b_D, L0_ffn_gate_w, L0_ffn_gate_bias, L0_ffn_w1, L0_ffn_w2, L0_ffn_w3, L0_ffn_shared_gate, L0_ffn_shared_up, L0_ffn_shared_down):

    def _L0_attn_a_ref(x, Wq, Wk, Wv, Wa, Wb, A_log, dt_bias, conv_q_w, conv_k_w, conv_v_w, Wg, norm_w, Wo):
        import jax, jax.numpy as jnp
        import numpy as np
        H, DK, DV, HID, KSZ, CHUNK = (6, 64, 128, 512, 4, 64)
        EPS = 1e-05

        def _short_conv(x, w):
            C, K = (w.shape[0], w.shape[2])
            y = jax.lax.conv_general_dilated(x.transpose(0, 2, 1), w, window_strides=(1,), padding=[(K - 1, 0)], feature_group_count=C, dimension_numbers=('NCH', 'OIH', 'NCH'))
            return jax.nn.silu(y.transpose(0, 2, 1))

        def _l2norm(x, eps=1e-06):
            return x * jax.lax.rsqrt(jnp.sum(x * x, axis=-1, keepdims=True) + eps)
        B, T, _ = x.shape
        q = _short_conv(x @ Wq.T, conv_q_w).reshape(B, T, H, DK)
        k = _short_conv(x @ Wk.T, conv_k_w).reshape(B, T, H, DK)
        v = _short_conv(x @ Wv.T, conv_v_w).reshape(B, T, H, DV)
        q = _l2norm(q) * DK ** (-0.5)
        k = _l2norm(k)
        g = -jnp.exp(A_log) * jax.nn.softplus(x @ Wa.T + dt_bias)
        beta = jax.nn.sigmoid(x @ Wb.T)

        def tm(a):
            a = jnp.moveaxis(a, 1, 0)
            return a.reshape((T // CHUNK, CHUNK) + a.shape[1:])
        qc, kc, vc, gc, bc = map(tm, (q, k, v, g, beta))

        def step(S, inp):
            q_t, k_t, v_t, g_t, b_t = inp
            S = S * jnp.exp(g_t)[..., None, None]
            delta = (v_t - jnp.einsum('bhk,bhkv->bhv', k_t, S)) * b_t[..., None]
            S = S + k_t[..., None] * delta[:, :, None, :]
            return (S, jnp.einsum('bhk,bhkv->bhv', q_t, S))

        @jax.checkpoint
        def chunk(S, inp):
            return jax.lax.scan(step, S, inp)
        S0 = jnp.zeros((B, H, DK, DV), x.dtype)
        _, o = jax.lax.scan(chunk, S0, (qc, kc, vc, gc, bc))
        o = jnp.moveaxis(o.reshape(T, B, H, DV), 0, 1)
        gate = (x @ Wg.T).reshape(B, T, H, DV)
        og = o * jax.nn.silu(gate)
        og = og * jax.lax.rsqrt(jnp.mean(og * og, axis=-1, keepdims=True) + EPS) * norm_w
        return og.reshape(B, T, H * DV) @ Wo.T

    def _L0_attn_b_ref(x, nu_log, theta_log, B_re, B_im, C_re, C_im, D):
        import jax, jax.numpy as jnp
        import numpy as np
        import math
        D_MODEL = 512
        D_STATE = 64
        R_MIN = 0.0
        R_MAX = 0.9
        MAX_PHASE = 6.283185307179586
        B_SZ = 4
        T_LEN = 512
        nu = jax.nn.softplus(nu_log)
        mag = jnp.exp(-jnp.exp(nu))
        theta = jnp.exp(theta_log)
        A_re = mag * jnp.cos(theta)
        A_im = mag * jnp.sin(theta)
        gamma = jnp.sqrt(jnp.clip(1.0 - mag * mag, 0.0))
        gB_re = gamma[:, None] * B_re
        gB_im = gamma[:, None] * B_im
        Bu_re = jnp.einsum('btd,nd->btn', x, gB_re)
        Bu_im = jnp.einsum('btd,nd->btn', x, gB_im)

        def step(h, bu):
            h_re, h_im = h
            bu_re, bu_im = bu
            new_re = A_re * h_re - A_im * h_im + bu_re
            new_im = A_re * h_im + A_im * h_re + bu_im
            return ((new_re, new_im), (new_re, new_im))
        Bsz = x.shape[0]
        h0 = jnp.zeros((Bsz, A_re.shape[0]), dtype=x.dtype)
        _, (H_re, H_im) = jax.lax.scan(step, (h0, h0), (jnp.swapaxes(Bu_re, 0, 1), jnp.swapaxes(Bu_im, 0, 1)))
        H_re = jnp.swapaxes(H_re, 0, 1)
        H_im = jnp.swapaxes(H_im, 0, 1)
        y = jnp.einsum('btn,dn->btd', H_re, C_re) - jnp.einsum('btn,dn->btd', H_im, C_im) + D * x
        return y

    def _L0_ffn_ref(hidden_states, gate_w, gate_bias, w1, w2, w3, shared_gate, shared_up, shared_down):
        import jax, jax.numpy as jnp
        import numpy as np
        E = 32
        K = 4
        G = 4
        TG = 2
        H = 512
        F = 256
        FS = 512
        SCALE = 2.0
        B, S = (2, 256)
        N = B * S
        CAP = 2 * (N * K // E)

        def _gate(x, gate_w, gate_bias):
            logits = x @ gate_w.T
            scores = jax.nn.sigmoid(logits)
            sc = scores + gate_bias
            n = x.shape[0]
            grp = sc.reshape(n, G, E // G)
            group_scores = jax.lax.top_k(grp, 2)[0].sum(-1)
            _, gidx = jax.lax.top_k(group_scores, TG)
            gmask = jnp.zeros((n, G), sc.dtype).at[jnp.arange(n)[:, None], gidx].set(1.0)
            smask = jnp.repeat(gmask, E // G, axis=1)
            tmp = jnp.where(smask > 0, sc, 0.0)
            _, topk_idx = jax.lax.top_k(tmp, K)
            topk_w = jnp.take_along_axis(scores, topk_idx, axis=1)
            topk_w = topk_w / (topk_w.sum(-1, keepdims=True) + 1e-20)
            return (topk_idx, topk_w * SCALE)

        def _moe(x, topk_idx, topk_w, w1, w2, w3):
            n = x.shape[0]
            flat_e = topk_idx.reshape(-1)
            oh = jax.nn.one_hot(flat_e, E, dtype=jnp.int32)
            pos = (jnp.cumsum(oh, axis=0) * oh).sum(-1) - 1
            keep = pos < CAP
            slot = jnp.where(keep, pos, CAP)
            x_rep = jnp.repeat(x, K, axis=0)
            buf = jnp.zeros((E, CAP, H), x.dtype).at[flat_e, slot].set(x_rep, mode='drop')
            h = jax.nn.silu(jnp.einsum('ech,ehf->ecf', buf, w1)) * jnp.einsum('ech,ehf->ecf', buf, w3)
            ob = jnp.einsum('ecf,efh->ech', h, w2)
            y = ob[flat_e, jnp.minimum(slot, CAP - 1)]
            y = jnp.where(keep[:, None], y, 0.0)
            return (y.reshape(n, K, H) * topk_w[:, :, None]).sum(1)
        b, s, h = hidden_states.shape
        x = hidden_states.reshape(-1, h)
        topk_idx, topk_w = _gate(x, gate_w, gate_bias)
        out = _moe(x, topk_idx, topk_w, w1, w2, w3)
        shared = jax.nn.silu(x @ shared_gate) * (x @ shared_up) @ shared_down
        return (out + shared).reshape(b, s, h)
    x = L0_attn_a_x
    x = x + _L0_attn_a_ref(_layernorm(x, axis=-1), L0_attn_a_Wq, L0_attn_a_Wk, L0_attn_a_Wv, L0_attn_a_Wa, L0_attn_a_Wb, L0_attn_a_A_log, L0_attn_a_dt_bias, L0_attn_a_conv_q_w, L0_attn_a_conv_k_w, L0_attn_a_conv_v_w, L0_attn_a_Wg, L0_attn_a_norm_w, L0_attn_a_Wo)
    x = x + _L0_ffn_ref(_layernorm(x, axis=-1), L0_ffn_gate_w, L0_ffn_gate_bias, L0_ffn_w1, L0_ffn_w2, L0_ffn_w3, L0_ffn_shared_gate, L0_ffn_shared_up, L0_ffn_shared_down)
    x = x + _L0_attn_b_ref(_layernorm(x, axis=-1), L0_attn_b_nu_log, L0_attn_b_theta_log, L0_attn_b_B_re, L0_attn_b_B_im, L0_attn_b_C_re, L0_attn_b_C_im, L0_attn_b_D)
    x = x + _L0_ffn_ref(_layernorm(x, axis=-1), L0_ffn_gate_w, L0_ffn_gate_bias, L0_ffn_w1, L0_ffn_w2, L0_ffn_w3, L0_ffn_shared_gate, L0_ffn_shared_up, L0_ffn_shared_down)
    return x

_drawn_inputs = setup_inputs


def setup_inputs(seed=0):
    import zlib

    import numpy as np

    out = dict(_drawn_inputs(seed))
    spreads = {'L0_attn_a_norm_w': (1.0, 0.2), 'L0_attn_b_D': (1.0, 0.2)}
    factors = {'L0_attn_a_Wa': 3.027,
     'L0_ffn_gate_bias': 34.932,
     'L0_ffn_gate_w': 3.846,
     'L0_ffn_w1': 3.203,
     'L0_ffn_w2': 3.14,
     'L0_ffn_w3': 3.136}
    for name, (base, spread) in spreads.items():
        noise = np.random.default_rng([zlib.crc32(name.encode()), seed]).standard_normal(out[name].shape)
        drawn = base * np.exp(spread * noise) if base else spread * noise
        out[name] = jnp.asarray(drawn.astype(out[name].dtype))
    for name, factor in factors.items():
        out[name] = (out[name] * factor).astype(out[name].dtype)
    return out
```

```python
from contextlib import ExitStack

import numpy as np
import concourse.bass as bass
from concourse import mybir

F32 = mybir.dt.float32
U32 = mybir.dt.uint32
I32 = mybir.dt.int32
ALU = mybir.AluOpType
ACT = mybir.ActivationFunctionType
AX = mybir.AxisListType

T = 2048
D = 512
NT = 16
H = 6
DK = 64
E = 32
CAP = 128
TB = 256
NB = T // TB
MAGIC = 12582912.0
TWO_PI = 6.283185
LEVELS = (1, 2, 4, 8, 16, 32, 64)
C_ID, C_TRI, C_STRI, C_M1T = 0, 128, 256, 384
C_MASK = 512
C_BONE = C_MASK + 6 * 128
C_IOTA = C_BONE + 2
C_SGN = C_IOTA + 32
C_U = C_SGN + 2
C_L = C_U + 16
C_N = C_L + 16


def shape_constants():
    c = np.zeros((128, C_N), np.float32)
    r = np.arange(128)
    s, t = r[:, None], r[None, :]
    c[:, C_ID:C_ID + 128] = s == t
    c[:, C_TRI:C_TRI + 128] = s <= t
    c[:, C_STRI:C_STRI + 128] = s < t

    def level(n, row, col):
        return (row == col) | ((row // (2 * n) == col // (2 * n)) & (row // n % 2 == 1) & (col // n % 2 == 0))

    c[:, C_M1T:C_M1T + 128] = level(1, t, s)
    for i, n in enumerate(LEVELS[1:7]):
        c[:, C_MASK + 128 * i:C_MASK + 128 * i + 128] = level(n, s, t)
    c[:64, C_BONE] = 1
    c[64:, C_BONE + 1] = 1
    c[:, C_IOTA:C_IOTA + 32] = np.arange(32)
    c[:64, C_SGN] = 1
    c[64:, C_SGN] = -1
    c[:, C_SGN + 1] = -1
    i, j = np.arange(16) // 4, np.arange(16) % 4
    c[:, C_U:C_U + 16] = j > i
    c[:, C_L:C_L + 16] = j < i
    return c


class Line:

    def __init__(self, sem, by=1):
        self.sem, self.by, self.n = sem, by, 0

    def up(self):
        self.n += self.by
        return (self, self.n)


def program(nc, a, out, stage=9):
    ctx = ExitStack()
    q = {"sync": [], "scalar": [], "vector": [], "tensor": [], "gpsimd": []}
    lines = []

    def line(name, by=1):
        x = Line(ctx.enter_context(nc.semaphore(name)), by)
        lines.append(x)
        return x

    def op(engine, fn, waits=(), on=None):
        flat = []

        def walk(w):
            if w is None:
                return
            if isinstance(w, tuple) and w and isinstance(w[0], Line):
                flat.append(w)
            else:
                for x in w:
                    walk(x)
        walk(waits)
        q[engine].append((flat, fn, on))
        return on.up() if on is not None else None

    def barrier():
        now = [(x, x.n) for x in lines if x.n]
        for engine in q:
            q[engine].append((now, None, None))

    with ctx:
        L_pe, L_dve, L_act, L_pool = line("pe"), line("dve"), line("act"), line("pool")

        def pe(fn, waits=(), sig=True):
            return op("tensor", fn, waits, L_pe if sig else None)

        def dve(fn, waits=()):
            return op("vector", fn, waits, L_dve)

        def act(fn, waits=()):
            return op("scalar", fn, waits, L_act)

        def pool(fn, waits=()):
            return op("gpsimd", fn, waits, L_pool)

        def dma(fn, on, waits=(), engine="sync"):
            return op(engine, fn, waits, on)

        def mm(o, lhsT, rhs, start=True, stop=True, waits=(), sig=False, skip=False):
            return pe(lambda e: e.matmul(o, lhsT, rhs, start=start, stop=stop, skip_group_check=skip), waits, sig)

        def tr(o, i, waits=(), sig=False):
            n = i.shape[0]
            return pe(lambda e: e.transpose(o, i, ident[0:n, 0:n]), waits, sig)

        def sb(name, shape, dt=F32, c=ctx):
            return c.enter_context(nc.sbuf_tensor(name, shape, dt))

        PS = ctx.enter_context(nc.psum_tensor("PS", [128, 8, 512], F32))
        free = [None] * 8

        X = sb("X", [128, NT, D])
        XNT = sb("XNT", [128, 4, T])
        CON = sb("CON", [128, C_N])
        ones = sb("ones", [128, 128])
        ident = CON[:, C_ID:C_ID + 128]
        triu = CON[:, C_TRI:C_TRI + 128]
        stri = CON[:, C_STRI:C_STRI + 128]
        bst = sb("bst", [128, NT, 6])
        bmv = sb("bmv", [128, NT, 2])
        rstd = sb("rstd", [128, NT])
        pw = sb("pw", [128, 64])

        L_x, L_con, L_xn = line("d_x", 16), line("d_con", 16), line("d_xn", 16)
        L_w = [line(f"d_w{i}", 16) for i in range(8)]
        t_con = dma(lambda e: e.dma_start(CON[:, :], a["consts"]), L_con)
        xv = a["x"].rearrange("b (i p) n -> p (b i) n", p=128)
        t_x = [dma(lambda e, i=i: e.dma_start(X[:, 4 * i:4 * i + 4, :], xv[:, 4 * i:4 * i + 4, :]), L_x)
               for i in range(4)]
        t_x = [t_x[3]] * 4
        t_ones = pool(lambda e: e.memset(ones[:, :], 1.0))
        t_pw = pool(lambda e: e.memset(pw[:, :], -0.5))

        buf = nc.dram_tensor("moe_buf", [E * CAP, D], F32, kind="Internal").ap()
        obd = nc.dram_tensor("moe_out", [E * CAP + 128, D], F32, kind="Internal").ap()
        zero = sb("zero", [128, 128])
        t_z = pool(lambda e: e.memset(zero[:, :], 0.0))
        L_z = line("d_z", 16)
        for j in range(E):
            dma(lambda e, j=j: e.dma_start(buf[j * 128:(j + 1) * 128, :].rearrange("p (a n) -> p a n", n=128), zero[:, :].unsqueeze(1).to_broadcast([128, 4, 128])), L_z, [t_z], "gpsimd")
        dma(lambda e: e.dma_start(obd[E * CAP:E * CAP + 128, :].rearrange("p (a n) -> p a n", n=128), zero[:, :].unsqueeze(1).to_broadcast([128, 4, 128])), L_z, [t_z], "gpsimd")

        def layer_norm(t_in, xn_of, keep=False):
            t_s = []
            for i in range(NT):
                t = dve(lambda e, i=i: e.bn_stats(bst[:, i, :], X[:, i, :]), [t_in[i]])
                t_s.append(dve(lambda e, i=i: e.bn_aggr(bmv[:, i, :], bst[:, i, :]), [t]))
            t = dve(lambda e: e.tensor_scalar(rstd[:, :], bmv[:, :, 1], 1e-5, None, ALU.add), [t_s])
            t_r = pool(lambda e: e.tensor_tensor(rstd[:, :], rstd[:, :], pw[:, 0:NT], ALU.pow), [t, t_pw])
            t_xn, t_xt = [], []
            for i in range(NT):
                xn = xn_of(i)
                w = [] if keep or i < 2 else [t_xt[i - 2]]
                t_xn.append(dve(lambda e, i=i, xn=xn: e.tensor_scalar(
                    xn, X[:, i, :], bmv[:, i, 0:1], rstd[:, i:i + 1], ALU.subtract, ALU.mult), [t_r, w]))
                b = i % 2
                for k in range(4):
                    t = tr(PS[:, b, k * 128:(k + 1) * 128], xn[:, k * 128:(k + 1) * 128],
                           [t_xn[i], free[b], t_con], sig=(k == 3))
                t2 = act(lambda e, i=i, b=b: e.activation(
                    XNT[:, :, i * 128:(i + 1) * 128],
                    PS[:, b, :].rearrange("p (k n) -> p k n", k=4), ACT.Copy), [t])
                free[b] = t2
                t_xt.append(t2)
            return t_xn, t_xt

        def delta_net():
            with ExitStack() as c:
                def s1(name, shape, dt=F32):
                    return sb(name, shape, dt, c)
                W = s1("W", [128, 4, 2304])
                WO = s1("WO", [128, H, D])
                WAB = s1("WAB", [128, 4, 12])
                CW = s1("CW", [128, 12, 4])
                SM = s1("SM", [128, 16])
                xnt2 = s1("xnt2", [128, 2, D])
                t_wab = dma(lambda e: e.dma_start(WAB[:, :, :], a["wab"].rearrange("(c p) n -> p c n", p=128)), L_w[0])
                t_sm = dma(lambda e: e.dma_start(SM[:, :], a["small"]), L_w[1])
                t_cw = dma(lambda e: e.dma_start(CW[:, :, :], a["convw"].rearrange("(c p) n -> p c n", p=128)), L_w[2])
                t_w = dma(lambda e: e.dma_start(W[:, :, :], a["wqkvg"].rearrange("(c p) n -> p c n", p=128)), L_w[3])
                t_wo = dma(lambda e: e.dma_start(WO[:, :, :], a["wo"].rearrange("(c p) n -> p c n", p=128)), L_w[4])
                t_wo = dve(lambda e: e.tensor_scalar(WO[:, :, :], WO[:, :, :], SM[:, 12:13], None, ALU.mult), [t_wo, t_sm])

                _, t_xt = layer_norm([t_x[i // 4] for i in range(NT)], lambda i: xnt2[:, i % 2, :])

                za = s1("za", [128, NT, H])
                zb = s1("zb", [128, NT, H])
                g = s1("g", [128, NT, H])
                beta = s1("beta", [128, NT, H])
                tmp = s1("tmp", [128, NT, H])
                sp = s1("sp", [128, NT, H])
                ea = s1("ea", [128, H])
                G = s1("G", [128, NT, H])
                eG = s1("eG", [128, NT, H])
                dG = s1("dG", [128, NT, H])
                eC = s1("eC", [128, NT, 3])
                nb = s1("nb", [128, NT, H])
                for i in range(NT):
                    for k in range(4):
                        t = mm(PS[:, 2, i * 12:i * 12 + 12], XNT[:, k, i * 128:(i + 1) * 128], WAB[:, k, :],
                               k == 0, k == 3, [t_xt[i], t_wab], sig=(i == NT - 1 and k == 3))
                ab = PS[:, 2, 0:NT * 12].rearrange("p (i n) -> p i n", n=12)
                t1 = dve(lambda e: e.tensor_tensor(za[:, :, :], ab[:, :, 0:H], SM[:, 0:H].unsqueeze(1).to_broadcast([128, NT, H]), ALU.add), [t, t_sm])
                t2 = dve(lambda e: e.tensor_copy(zb[:, :, :], ab[:, :, H:12]))
                free[2] = t2
                t3 = act(lambda e: e.activation(tmp[:, :, :], za[:, :, :], ACT.Abs), [t1])
                t3 = act(lambda e: e.activation(tmp[:, :, :], tmp[:, :, :], ACT.Exp, scale=-1.0), [t3])
                t4 = act(lambda e: e.activation(beta[:, :, :], zb[:, :, :], ACT.Exp, scale=-1.0), [t2])
                t5 = act(lambda e: e.activation(ea[:, :], SM[:, H:2 * H], ACT.Exp), [t_sm])
                t6 = act(lambda e: e.activation(sp[:, :, :], tmp[:, :, :], ACT.Ln, bias=1.0), [t3])
                t7 = dve(lambda e: e.scalar_tensor_tensor(sp[:, :, :], za[:, :, :], 0.0, sp[:, :, :], ALU.max, ALU.add), [t6])
                t_g = dve(lambda e: e.scalar_tensor_tensor(g[:, :, :], sp[:, :, :], -1.0, ea[:, :].unsqueeze(1).to_broadcast([128, NT, H]), ALU.mult, ALU.mult), [t7, t5])
                t8 = dve(lambda e: e.tensor_scalar(beta[:, :, :], beta[:, :, :], 1.0, None, ALU.add), [t4])
                t_beta = dve(lambda e: e.reciprocal(beta[:, :, :], beta[:, :, :]), [t8])
                t_nb = dve(lambda e: e.tensor_scalar(nb[:, :, :], beta[:, :, :], -1.0, None, ALU.mult), [t_beta])
                gf = g[:, :, :].rearrange("p i h -> p (i h)")
                mm(PS[:, 2, 0:96], triu, gf, True, True, [t_g, free[2]])
                t = mm(PS[:, 3, 0:96], ones[:, :], gf, True, True, [t_ones], sig=True)
                Gp = PS[:, 2, 0:96].rearrange("p (i h) -> p i h", h=H)
                Cp = PS[:, 3, 0:96].rearrange("p (i h) -> p i h", h=H)
                t_G = dve(lambda e: e.tensor_copy(G[:, :, :], Gp), [t])
                t_eG = act(lambda e: e.activation(eG[:, :, :], Gp, ACT.Exp), [t_G])
                t1 = dve(lambda e: e.tensor_tensor(dG[:, :, :], Cp, G[:, :, :], ALU.subtract), [t_G])
                act(lambda e: e.activation(eC[0:64, :, :], Cp[0:64, :, 0:H:2], ACT.Exp), [t1])
                t_eC = act(lambda e: e.activation(eC[64:128, :, :], Cp[64:128, :, 1:H:2], ACT.Exp))
                t_dG = act(lambda e: e.activation(dG[:, :, :], dG[:, :, :], ACT.Exp))
                free[2] = free[3] = [t_eC, t_eG, t_dG]

                raw = s1("raw", [128, 12, 3 + TB])
                cacc = s1("cacc", [128, 2, TB])
                th = s1("th", [128, 2, TB])
                qkv = s1("qkv", [128, 12, TB])
                sq = s1("sq", [128, 6, TB])
                rn = s1("rn", [128, 12])
                kh = s1("kh", [128, H, DK])
                kg = s1("kg", [128, H, DK])
                kd = s1("kd", [128, H, DK])
                khT = s1("khT", [128, 3, 128])
                V = s1("V", [128, H, 128])
                Dm = s1("Dm", [128, H, 128])
                NTm = s1("NTm", [128, H, 128])
                P = s1("P", [128, H, 128])
                R = s1("R", [128, H, 128])
                Tm = s1("Tm", [128, H, 128])
                Z = s1("Z", [128, H, 128])
                WT = s1("WT", [128, 3, 128])
                S = s1("S", [128, 3, 128])
                Dl = s1("Dl", [128, H, 128])
                o = s1("o", [128, H, 128])
                gs = s1("gs", [128, H, 128])
                ms = s1("ms", [128, H])
                ogT = s1("ogT", [128, H, 128])
                scr = s1("scr", [128, H, 128])

                t_halo = pool(lambda e: e.memset(raw[:, :, 0:3], 0.0))
                t_S = pool(lambda e: e.memset(S[:, :, :], 0.0))
                t_qkv_free = None
                t_sq_free = None

                def two(b, n=384):
                    return PS[:, b:b + 2, 0:n].rearrange("p b (h n) -> p b h n", n=128)

                def six(x):
                    return x[:, :, :].rearrange("p (h b) n -> p b h n", b=2)

                t_x_out = []
                t_prev = {}
                for nbk in range(NB):
                    tok0 = nbk * TB
                    t_conv, t_qkv = [], []
                    t_cacc_free = [None, None]
                    for ct in range(12):
                        b = 6 + ct % 2
                        u = ct % 2
                        for k in range(4):
                            t = mm(PS[:, b, 0:TB], W[:, k, ct * 128:(ct + 1) * 128], XNT[:, k, tok0:tok0 + TB],
                                   k == 0, k == 3, [t_w, free[b], t_xt], sig=(k == 3))
                        t1 = act(lambda e, ct=ct, b=b: e.activation(raw[:, ct, 3:3 + TB], PS[:, b, 0:TB], ACT.Copy), [t, t_halo])
                        t2 = act(lambda e, ct=ct, b=b, u=u: e.activation(cacc[:, u, :], PS[:, b, 0:TB], ACT.Copy, scale=CW[:, ct, 3:4]), [t, t_cw, t_cacc_free[u]])
                        free[b] = t2
                        t3 = [t1, t2]
                        for j in range(3):
                            t3 = dve(lambda e, ct=ct, j=j, u=u: e.scalar_tensor_tensor(
                                cacc[:, u, :], raw[:, ct, j:j + TB], CW[:, ct, j:j + 1], cacc[:, u, :], ALU.mult, ALU.add), [t3])
                        t_conv.append(t3)
                        t4 = act(lambda e, u=u: e.activation(th[:, u, :], cacc[:, u, :], ACT.Tanh, scale=0.5), [t3, t_cacc_free[u]])
                        t5 = dve(lambda e, ct=ct, u=u: e.scalar_tensor_tensor(
                            qkv[:, ct, :], th[:, u, :], 1.0, cacc[:, u, :], ALU.add, ALU.mult), [t4, t_qkv_free])
                        t_cacc_free[u] = t5
                        t_qkv.append(t5)
                        if ct < 6:
                            t_sq = act(lambda e, ct=ct: e.activation(sq[:, ct, :], qkv[:, ct, :], ACT.Square), [t5, t_sq_free])
                    t_halo = pool(lambda e: e.tensor_copy(raw[:, :, 0:3], raw[:, :, TB:TB + 3]), [t_conv])
                    t_qkv = t_qkv[11]
                    for cl in range(TB // 128):
                        ch = nbk * (TB // 128) + cl
                        cs = slice(cl * 128, cl * 128 + 128)
                        for n in range(2):
                            for k in range(4):
                                t_gate = mm(PS[:, 6 + n, 0:384], XNT[:, k, ch * 128:ch * 128 + 128],
                                            W[:, k, 1536 + 384 * n:1920 + 384 * n], k == 0, k == 3,
                                            [free[6 + n]], sig=(k == 3))
                        t1 = act(lambda e: e.activation(scr[:, :, :].rearrange("p (b h) n -> p b h n", b=2), two(6), ACT.Tanh, scale=0.5), [t_gate, t_prev.get("scr")])
                        t_gs = dve(lambda e: e.scalar_tensor_tensor(
                            gs[:, :, :].rearrange("p (b h) n -> p b (h n)", b=2),
                            scr[:, :, :].rearrange("p (b h) n -> p b (h n)", b=2), 1.0,
                            PS[:, 6:8, 0:384], ALU.add, ALU.mult), [t1, t_prev.get("gs")])
                        free[6] = free[7] = t_gs
                        for ct in range(6):
                            t = mm(PS[:, 0, 2 * ct:2 * ct + 2], sq[:, ct, cs], CON[:, C_BONE:C_BONE + 2], True, True,
                                   [t_sq, t_con, free[0]], sig=(ct == 5))
                        t_sq_free = t
                        t1 = dve(lambda e: e.tensor_scalar(rn[:, :], PS[:, 0, 0:12], 4e-6, None, ALU.add), [t, t_prev.get("rn")])
                        free[0] = t1
                        t_rn = pool(lambda e: e.tensor_tensor(rn[:, :], rn[:, :], pw[:, 0:12], ALU.pow), [t1, t_pw])
                        for j in range(3):
                            t = tr(PS[:, 1, j * 128:(j + 1) * 128], qkv[:, 3 + j, cs], [t_qkv, free[1]], sig=(j == 2))
                        for j in range(6):
                            tv = tr(PS[:, 2 + j % 2, (j // 2) * 128:(j // 2 + 1) * 128], qkv[:, 6 + j, cs],
                                    [free[2], free[3]], sig=(j == 5))
                        t_kh = dve(lambda e: e.tensor_tensor(
                            kh[:, :, :], PS[:, 1, 0:384].rearrange("p (h d) -> p h d", d=DK),
                            rn[:, 6:12].unsqueeze(2).to_broadcast([128, H, DK]), ALU.mult), [t, t_rn, t_prev.get("kh")])
                        free[1] = t_kh
                        t_V = act(lambda e: e.activation(six(V), two(2), ACT.Copy, scale=0.5), [tv, t_prev.get("V")])
                        free[2] = free[3] = t_V
                        t_kg = pool(lambda e, ch=ch: e.tensor_tensor(
                            kg[:, :, :], kh[:, :, :], eG[:, ch, :].unsqueeze(2).to_broadcast([128, H, DK]), ALU.mult),
                            [t_kh, t_eG, t_prev.get("kg")])
                        t_kd = pool(lambda e, ch=ch: e.tensor_tensor(
                            kd[:, :, :], kh[:, :, :], dG[:, ch, :].unsqueeze(2).to_broadcast([128, H, DK]), ALU.mult),
                            [t_kh, t_dG, t_prev.get("kd")])
                        for j in range(3):
                            t = tr(PS[:, 1, j * 128:(j + 1) * 128], kh[:, 2 * j:2 * j + 2, :].rearrange("p h d -> p (h d)"),
                                   [t_kh, free[1]], sig=(j == 2))
                        t_kh_read = t
                        t_khT = act(lambda e: e.activation(
                            khT[:, :, :], PS[:, 1, 0:384].rearrange("p (j n) -> p j n", n=128), ACT.Copy),
                            [t, t_prev.get("khT")])
                        free[1] = t_khT
                        for h in range(H):
                            t = mm(PS[:, 4 + h % 2, (h // 2) * 128:(h // 2 + 1) * 128],
                                   g[:, ch, h:h + 1].to_broadcast([128, 128]), triu, True, True,
                                   [free[4], free[5], t_g], sig=(h == 5))
                        for h in range(H):
                            t1 = dve(lambda e, h=h, ch=ch: e.tensor_scalar(
                                Dm[:, h, :], PS[:, 4 + h % 2, (h // 2) * 128:(h // 2 + 1) * 128], G[:, ch, h:h + 1], 0.0,
                                ALU.subtract, ALU.min), [t, t_prev.get("Dm")])
                        free[4] = free[5] = t1
                        t1 = act(lambda e: e.activation(Dm[:, :, :], Dm[:, :, :], ACT.Exp), [t1])
                        t_D = pool(lambda e: e.affine_select(
                            out=Dm[:, :, :], in_=Dm[:, :, :], compare_op=ALU.is_ge, fill=0.0, base=0,
                            pattern=[[0, H], [1, 128]], channel_multiplier=-1), [t1])
                        for h in range(H):
                            p0 = 64 * (h % 2)
                            mm(PS[:, 2 + h % 2, (h // 2) * 128:(h // 2 + 1) * 128], khT[p0:p0 + 64, h // 2, :],
                               khT[p0:p0 + 64, h // 2, :], True, True, [free[2], free[3], t_khT])
                            t = mm(PS[:, 4 + h % 2, (h // 2) * 128:(h // 2 + 1) * 128], khT[p0:p0 + 64, h // 2, :],
                                   qkv[p0:p0 + 64, h // 2, cs], True, True, [free[4], free[5]], sig=(h == 5))
                        for h in range(H):
                            t1 = dve(lambda e, h=h, ch=ch: e.scalar_tensor_tensor(
                                NTm[:, h, :], PS[:, 2 + h % 2, (h // 2) * 128:(h // 2 + 1) * 128], nb[:, ch, h:h + 1],
                                Dm[:, h, :], ALU.mult, ALU.mult), [t, t_D, t_nb, t_prev.get("NTm")])
                        t_P = dve(lambda e: e.tensor_tensor(six(P), two(4), six(Dm), ALU.mult), [t, t_prev.get("P")])
                        free[2] = free[3] = free[4] = free[5] = t_P
                        t_prev["Dm"] = t_P
                        t_prev["khT"] = t
                        t_N = pool(lambda e: e.affine_select(
                            out=NTm[:, :, :], in_=NTm[:, :, :], compare_op=ALU.not_equal, fill=1.0, base=0,
                            pattern=[[0, H], [-1, 128]], channel_multiplier=1), [t1])
                        t_R = dve(lambda e: e.tensor_tensor(
                            R[:, :, :], NTm[:, :, :], CON[:, C_M1T:C_M1T + 128].unsqueeze(1).to_broadcast([128, H, 128]),
                            ALU.mult), [t_N, t_prev.get("R")])
                        for h in range(H):
                            t = tr(PS[:, 2 + h % 2, (h // 2) * 128:(h // 2 + 1) * 128], R[:, h, :], [t_R, free[2], free[3]], sig=(h == 5))
                        t_T = act(lambda e: e.activation(six(Tm), two(2), ACT.Copy), [t])
                        free[2] = free[3] = t_T
                        t_Zr = None
                        for li in range(6):
                            last = li == 5
                            for h in range(H):
                                t = mm(PS[:, h % 2, (h // 2) * 128:(h // 2 + 1) * 128], NTm[:, h, :], Tm[:, h, :], True, True,
                                       [t_N, t_T, free[0], free[1]], sig=(h == 5))
                            m = CON[:, C_MASK + 128 * li:C_MASK + 128 * li + 128]
                            t_Z = dve(lambda e, m=m: e.tensor_tensor(
                                six(Z), two(0),
                                m.unsqueeze(1).unsqueeze(1).to_broadcast([128, 2, 3, 128]), ALU.mult), [t, t_Zr])
                            free[0] = free[1] = t_Z
                            if last:
                                t_N_read = t
                            for h in range(H):
                                if not last:
                                    mm(PS[:, 2 + h % 2, (h // 2) * 128:(h // 2 + 1) * 128], R[:, h, :], Z[:, h, :], True, True,
                                       [t_Z, free[2], free[3]])
                                t = mm(PS[:, 4 + h % 2, (h // 2) * 128:(h // 2 + 1) * 128], Z[:, h, :], R[:, h, :], True, True,
                                       [t_Z, free[4], free[5]], sig=(h == 5))
                            t_Zr = t
                            if not last:
                                t_T = act(lambda e: e.activation(six(Tm), two(2), ACT.Copy), [t])
                                free[2] = free[3] = t_T
                            t_R = act(lambda e: e.activation(six(R), two(4), ACT.Copy), [t])
                            free[4] = free[5] = t_R
                            t_T = [t_T, t_R]
                        t_prev["NTm"] = t_N_read
                        for h in range(H):
                            p0 = 64 * (h % 2)
                            t = mm(PS[p0:p0 + 64, 0, (h // 2) * 128:(h // 2 + 1) * 128], kg[:, h, :], R[:, h, :], True, True,
                                   [t_kg, t_R, free[0]], sig=(h == 5))
                        t_prev["kg"] = t
                        t_WT = act(lambda e: e.activation(
                            WT[:, :, :], PS[:, 0, 0:384].rearrange("p (j n) -> p j n", n=128), ACT.Copy, scale=-1.0),
                            [t, t_prev.get("WT")])
                        free[0] = t_WT
                        for h in range(H):
                            p0 = 64 * (h % 2)
                            ob = PS[:, 2 + h % 2, (h // 2) * 128:(h // 2 + 1) * 128]
                            mm(ob, R[:, h, :], V[:, h, :], True, False, [t_V, free[2], free[3]], skip=True)
                            t = mm(ob, WT[p0:p0 + 64, h // 2, :], S[p0:p0 + 64, h // 2, :], False, True, [t_WT, t_S],
                                   sig=(h == 5), skip=True)
                        t_prev["V"] = t_prev["R"] = t_prev["WT"] = t
                        t_Dl = dve(lambda e, ch=ch: e.tensor_tensor(
                            six(Dl), two(2),
                            beta[:, ch, :].rearrange("p (h b) -> p b h", b=2).unsqueeze(3).to_broadcast([128, 2, 3, 128]),
                            ALU.mult), [t, t_beta, t_prev.get("Dl")])
                        free[2] = free[3] = t_Dl
                        for h in range(H):
                            p0 = 64 * (h % 2)
                            t = mm(PS[:, 4 + h % 2, (h // 2) * 128:(h // 2 + 1) * 128], qkv[p0:p0 + 64, h // 2, cs],
                                   S[p0:p0 + 64, h // 2, :], True, True, [free[4], free[5], t_S], sig=(h == 5))
                        t_S_read = t
                        t_o1 = dve(lambda e, ch=ch: e.tensor_tensor(
                            six(o), two(4),
                            eG[:, ch, :].rearrange("p (h b) -> p b h", b=2).unsqueeze(3).to_broadcast([128, 2, 3, 128]),
                            ALU.mult), [t, t_prev.get("o")])
                        free[4] = free[5] = t_o1
                        for h in range(H):
                            t = mm(PS[:, 2 + h % 2, (h // 2) * 128:(h // 2 + 1) * 128], P[:, h, :], Dl[:, h, :], True, True,
                                   [t_P, t_Dl, free[2], free[3]], sig=(h == 5))
                        t_prev["P"] = t
                        for h in range(H):
                            p0 = 64 * (h % 2)
                            t_kS = mm(PS[p0:p0 + 64, 1, (h // 2) * 128:(h // 2 + 1) * 128], kd[:, h, :], Dl[:, h, :], True, True,
                                      [t_kd, free[1]], sig=(h == 5))
                        t_prev["kd"] = t_prev["Dl"] = t_kS
                        for j in range(3):
                            t_S = dve(lambda e, j=j, ch=ch: e.scalar_tensor_tensor(
                                S[:, j, :], S[:, j, :], eC[:, ch, j:j + 1], PS[:, 1, j * 128:(j + 1) * 128], ALU.mult, ALU.add),
                                [t_kS, t_S_read, t_eC])
                        free[1] = t_S
                        t1 = dve(lambda e: e.tensor_tensor(six(o), two(2), six(o), ALU.add), [t, t_o1])
                        free[2] = free[3] = t1
                        t1 = dve(lambda e: e.tensor_tensor(
                            o[:, :, :], o[:, :, :], rn[:, 0:6].unsqueeze(2).to_broadcast([128, H, 128]), ALU.mult), [t1])
                        t_prev["rn"] = t1
                        t1 = dve(lambda e: e.scalar_tensor_tensor(
                            o[:, :, :], o[:, :, :], 0.125, gs[:, :, :], ALU.mult, ALU.mult), [t1])
                        t_prev["gs"] = t1
                        t2 = act(lambda e: e.activation(scr[:, :, :], o[:, :, :], ACT.Square), [t1])
                        t2 = dve(lambda e: e.tensor_reduce(ms[:, :], scr[:, :, :], AX.X, ALU.add), [t2])
                        t_prev["scr"] = t2
                        t2 = dve(lambda e: e.tensor_scalar(ms[:, :], ms[:, :], 1.0 / 128, 4e-5, ALU.mult, ALU.add), [t2])
                        t2 = pool(lambda e: e.tensor_tensor(ms[:, :], ms[:, :], pw[:, 0:6], ALU.pow), [t2])
                        t1 = dve(lambda e: e.tensor_tensor(
                            o[:, :, :], o[:, :, :], ms[:, :].unsqueeze(2).to_broadcast([128, H, 128]), ALU.mult), [t1, t2])
                        for h in range(H):
                            t = tr(PS[:, 4 + h % 2, (h // 2) * 128:(h // 2 + 1) * 128], o[:, h, :], [t1, free[4], free[5]], sig=(h == 5))
                        t_prev["o"] = t
                        t1 = act(lambda e: e.activation(six(ogT), two(4), ACT.Copy), [t, t_prev.get("ogT")])
                        free[4] = free[5] = t1
                        for h in range(H):
                            t = mm(PS[:, 0, :], ogT[:, h, :], WO[:, h, :], h == 0, h == 5, [t1, t_wo, free[0]], sig=(h == 5))
                        t_prev["ogT"] = t
                        t1 = dve(lambda e, ch=ch: e.tensor_tensor(X[:, ch, :], X[:, ch, :], PS[:, 0, :], ALU.add), [t])
                        free[0] = t1
                        t_prev["kh"] = [t_kh_read, t_kg, t_kd]
                        t_qkv_free = t_S_read
                        t_x_out.append(t1)
                barrier()
            return t_x_out

        def moe(m, t_xi):
            with ExitStack() as c:
                def s1(name, shape, dt=F32):
                    return sb(f"{name}_{m}", shape, dt, c)
                XN = s1("XN", [128, NT, D])
                GW = s1("GW", [128, 4, E])
                GB = s1("GB", [128, E])
                SW = s1("SW", [128, 3, 4, D])
                NW = 2
                W13 = s1("W13", [128, NW, 4, 512])
                W2 = s1("W2", [128, NW, 2, 512])
                NBF = 2
                Bf = s1("Bf", [128, NBF, D])
                BT = s1("BT", [128, 4, 128])
                eth = s1("eth", [128, 256])
                eh = s1("eh", [128, 256])
                ehT = s1("ehT", [128, 2, 128])
                OB = s1("OB", [128, 2, D])
                L1 = [line(f"d{m}_{n}", 16) for n in ("gw", "gb", "sw")]
                Lw = [line(f"d{m}_w{i}", 16) for i in range(NW)]
                Lb = [line(f"d{m}_b{i}", 16) for i in range(NBF)]
                Lo = [line(f"d{m}_o{i}", 16) for i in range(2)]
                Ls = line(f"d{m}_s", 16)
                t_gw = dma(lambda e: e.dma_start(GW[:, :, :], a["gw"].rearrange("(c p) n -> p c n", p=128)), L1[0])
                t_gb = dma(lambda e: e.dma_start(GB[:, :], a["gb"]), L1[1])
                for j, n in enumerate(("sg", "su", "sd")):
                    t_sw = dma(lambda e, j=j, n=n: e.dma_start(SW[:, j, :, :], a[n].rearrange("(c p) n -> p c n", p=128)), L1[2])
                w13v = a["w13"].rearrange("e (c p) n -> e p c n", p=128)
                w2v = a["w2"].rearrange("e (c p) n -> e p c n", p=128)
                t_ew = {}

                def load_w(x, free_w):
                    s = x % NW
                    dma(lambda e, x=x, s=s: e.dma_start(W13[:, s, :, :], w13v[x]), Lw[s], free_w)
                    t_ew[x] = dma(lambda e, x=x, s=s: e.dma_start(W2[:, s, :, :], w2v[x]), Lw[s])

                for x in range(NW):
                    load_w(x, None)

                t_xn, t_xt = layer_norm(t_xi, lambda i: XN[:, i, :], keep=True)
                sg = s1
                for i in range(NT):
                    for k in range(4):
                        t = mm(PS[:, 2, i * E:(i + 1) * E], XNT[:, k, i * 128:(i + 1) * 128], GW[:, k, :], k == 0, k == 3,
                               [t_xt[i], t_gw, free[2]], sig=(i == NT - 1 and k == 3))
                lg = PS[:, 2, :].rearrange("p (i n) -> p i n", n=E)
                sc = sg("sc", [128, NT, E])
                sb_ = sg("sbias", [128, NT, E])
                oh = sg("oh", [128, 4, NT, E])
                m8 = sg("m8", [128, NT, 4, 8])
                gsum = sg("gsum", [128, NT, 4])
                cmp = sg("cmp", [128, NT, 4, 4])
                cm2 = sg("cm2", [128, NT, 4, 4])
                cnt = sg("cnt", [128, NT, 4])
                v8 = sg("v8", [128, NT, 8])
                i8 = sg("i8", [128, NT, 8], U32)
                i8f = sg("i8f", [128, NT, 8])
                wk = s1("wk", [128, NT, 4])
                ws = sg("ws", [128, NT])
                msk = sg("msk", [128, NT, E])
                cum = sg("cum", [128, NT, E])
                tmp = sg("gtmp", [128, 4, NT, E])
                pk = sg("pk", [128, 4, NT])
                kp = sg("kp", [128, 4, NT])
                offs = s1("offs", [128, 4, NT], U32)
                t1 = act(lambda e: e.activation(sc[:, :, :], lg, ACT.Exp, scale=-1.0), [t])
                free[2] = t1
                t1 = dve(lambda e: e.tensor_scalar(sc[:, :, :], sc[:, :, :], 1.0, None, ALU.add), [t1])
                t_sc = dve(lambda e: e.reciprocal(sc[:, :, :], sc[:, :, :]), [t1])
                t1 = dve(lambda e: e.tensor_tensor(sb_[:, :, :], sc[:, :, :], GB[:, :].unsqueeze(1).to_broadcast([128, NT, E]), ALU.add), [t_sc, t_gb])
                for i in range(NT):
                    for gi in range(4):
                        t2 = dve(lambda e, i=i, gi=gi: e.max(m8[:, i, gi, :], sb_[:, i, gi * 8:(gi + 1) * 8]), [t1])
                t2 = dve(lambda e: e.tensor_tensor(gsum[:, :, :], m8[:, :, :, 0], m8[:, :, :, 1], ALU.add), [t2])
                gi_ = gsum[:, :, :].unsqueeze(3).to_broadcast([128, NT, 4, 4])
                gj_ = gsum[:, :, :].unsqueeze(2).to_broadcast([128, NT, 4, 4])
                cu = CON[:, C_U:C_U + 16].rearrange("p (i j) -> p i j", j=4).unsqueeze(1).to_broadcast([128, NT, 4, 4])
                cl_ = CON[:, C_L:C_L + 16].rearrange("p (i j) -> p i j", j=4).unsqueeze(1).to_broadcast([128, NT, 4, 4])
                t3 = dve(lambda e: e.tensor_tensor(cmp[:, :, :, :], gi_, gj_, ALU.is_ge), [t2])
                t4 = dve(lambda e: e.tensor_tensor(cm2[:, :, :, :], gi_, gj_, ALU.is_gt), [t2])
                t3 = dve(lambda e: e.tensor_tensor(cmp[:, :, :, :], cmp[:, :, :, :], cu, ALU.mult), [t3])
                t4 = dve(lambda e: e.tensor_tensor(cm2[:, :, :, :], cm2[:, :, :, :], cl_, ALU.mult), [t4])
                t3 = dve(lambda e: e.tensor_tensor(cmp[:, :, :, :], cmp[:, :, :, :], cm2[:, :, :, :], ALU.add), [t3, t4])
                t3 = dve(lambda e: e.tensor_reduce(cnt[:, :, :], cmp[:, :, :, :], AX.X, ALU.add), [t3])
                t3 = dve(lambda e: e.tensor_scalar(cnt[:, :, :], cnt[:, :, :], 2.0, None, ALU.is_ge), [t3])
                t3 = dve(lambda e: e.tensor_tensor(
                    sb_[:, :, :].rearrange("p i (g n) -> p i g n", g=4), sb_[:, :, :].rearrange("p i (g n) -> p i g n", g=4),
                    cnt[:, :, :].unsqueeze(3).to_broadcast([128, NT, 4, 8]), ALU.mult), [t3])
                for i in range(NT):
                    t4 = dve(lambda e, i=i: e.max(v8[:, i, :], sb_[:, i, :]), [t3])
                for i in range(NT):
                    t4 = dve(lambda e, i=i: e.max_index(i8[:, i, :], v8[:, i, :], sb_[:, i, :]), [t4])
                t4 = dve(lambda e: e.tensor_copy(i8f[:, :, :], i8[:, :, :]), [t4])
                io = CON[:, C_IOTA:C_IOTA + 32].unsqueeze(1).to_broadcast([128, NT, E])
                t5 = []
                for k in range(4):
                    t5.append(dve(lambda e, k=k: e.tensor_tensor(
                        oh[:, k, :, :], io, i8f[:, :, k:k + 1].to_broadcast([128, NT, E]), ALU.is_equal), [t4]))
                t6 = dve(lambda e: e.tensor_tensor(msk[:, :, :], oh[:, 0, :, :], oh[:, 1, :, :], ALU.add), [t5])
                t6 = dve(lambda e: e.tensor_tensor(msk[:, :, :], msk[:, :, :], oh[:, 2, :, :], ALU.add), [t6])
                t_mk = dve(lambda e: e.tensor_tensor(msk[:, :, :], msk[:, :, :], oh[:, 3, :, :], ALU.add), [t6])
                t6 = dve(lambda e: e.memset(cum[:, 0, :], 0.0))
                for i in range(1, NT):
                    t6 = dve(lambda e, i=i: e.tensor_tensor(cum[:, i, :], cum[:, i - 1, :], msk[:, i - 1, :], ALU.add), [t6, t_mk])
                mm(PS[:, 3, :], stri, msk[:, :, :].rearrange("p i n -> p (i n)"), True, False, [t_mk, free[3]])
                t_ps = mm(PS[:, 3, :], ones[:, :], cum[:, :, :].rearrange("p i n -> p (i n)"), False, True, [t6], sig=True)
                for k in range(4):
                    t7 = dve(lambda e, k=k: e.tensor_tensor(tmp[:, k, :, :], oh[:, k, :, :], sc[:, :, :], ALU.mult))
                t7 = dve(lambda e: e.tensor_reduce(wk[:, :, :].rearrange("p i k -> p k i"), tmp[:, :, :, :], AX.X, ALU.add), [t7])
                t8 = dve(lambda e: e.tensor_reduce(ws[:, :], wk[:, :, :], AX.X, ALU.add), [t7])
                t8 = dve(lambda e: e.tensor_scalar(ws[:, :], ws[:, :], 1e-20, None, ALU.add), [t8])
                t8 = dve(lambda e: e.reciprocal(ws[:, :], ws[:, :]), [t8])
                t_wk = dve(lambda e: e.tensor_tensor(wk[:, :, :], wk[:, :, :], ws[:, :].unsqueeze(2).to_broadcast([128, NT, 4]), ALU.mult), [t8])
                pos = PS[:, 3, :].rearrange("p (i n) -> p i n", n=E)
                for k in range(4):
                    t9 = dve(lambda e, k=k: e.tensor_tensor(tmp[:, k, :, :], oh[:, k, :, :], pos, ALU.mult), [t_ps, t7])
                free[3] = t9
                t9 = dve(lambda e: e.tensor_reduce(pk[:, :, :], tmp[:, :, :, :], AX.X, ALU.add), [t9])
                t10 = dve(lambda e: e.tensor_scalar(kp[:, :, :], pk[:, :, :], float(CAP), None, ALU.is_lt), [t9])
                t9 = dve(lambda e: e.scalar_tensor_tensor(
                    pk[:, :, :], i8f[:, :, 0:4].rearrange("p i k -> p k i"), float(CAP), pk[:, :, :], ALU.mult, ALU.add), [t10])
                t9 = dve(lambda e: e.scalar_tensor_tensor(pk[:, :, :], pk[:, :, :], float(-E * CAP), kp[:, :, :], ALU.add, ALU.mult), [t9])
                t_of = dve(lambda e: e.tensor_scalar(offs[:, :, :], pk[:, :, :], float(E * CAP), None, ALU.add), [t9])
                t_sc = None
                for i in range(NT):
                    for k in range(4):
                        t_sc = dma(lambda e, i=i, k=k: e.indirect_dma_start(
                            out=buf, out_offset=bass.IndirectOffsetOnAxis(ap=offs[:, k, i:i + 1], axis=0),
                            in_=XN[:, i, :], in_offset=None, bounds_check=E * CAP - 1, oob_is_err=False),
                            Ls, [t_of, t_xn[i], (L_z, L_z.n)], "gpsimd")

                shT = s1("shT", [128, 4, 512])
                sth = s1("sth", [128, 2, 512])
                t_sh_free = None
                t_xs = [None] * NT
                t_sth = [None, None]
                for nb4 in range(4):
                    for f in range(4):
                        u = f % 2
                        for j in range(2):
                            for k in range(4):
                                t = mm(PS[:, 4 + 2 * u + j, :], SW[:, j, k, f * 128:(f + 1) * 128], XNT[:, k, nb4 * 512:(nb4 + 1) * 512],
                                       k == 0, k == 3, [t_sw, free[4 + 2 * u + j], t_xt], sig=(k == 3))
                        t1 = act(lambda e, u=u: e.activation(sth[:, u, :], PS[:, 4 + 2 * u, :], ACT.Tanh, scale=0.5), [t, t_sth[u]])
                        t1 = dve(lambda e, u=u: e.scalar_tensor_tensor(sth[:, u, :], sth[:, u, :], 1.0, PS[:, 4 + 2 * u, :], ALU.add, ALU.mult), [t1])
                        t_h = dve(lambda e, u=u, f=f: e.tensor_tensor(shT[:, f, :], sth[:, u, :], PS[:, 5 + 2 * u, :], ALU.mult), [t1, t_sh_free])
                        t_sth[u] = t_h
                        free[4 + 2 * u] = free[5 + 2 * u] = t_h
                    for tl in range(4):
                        i = nb4 * 4 + tl
                        b = tl % 2
                        for f in range(4):
                            t = mm(PS[:, b, :], shT[:, f, tl * 128:(tl + 1) * 128], SW[:, 2, f, :], f == 0, f == 3, [t_h, free[b]], sig=(f == 3))
                        t_xs[i] = dve(lambda e, i=i, b=b: e.scalar_tensor_tensor(X[:, i, :], PS[:, b, :], 0.5, X[:, i, :], ALU.mult, ALU.add), [t, t_xi[i], t_xn[i]])
                        free[b] = t_xs[i]
                    t_sh_free = t

                t_bf_free, t_ob_free, t_bt, t_eh, t_ehT, t_w_free = [None] * NBF, [None] * 2, None, None, None, {}
                for x in range(E):
                    s, w = x % NBF, x % NW
                    t_b = dma(lambda e, x=x, s=s: e.dma_start(Bf[:, s, :], buf[x * CAP:(x + 1) * CAP, :]), Lb[s], [t_sc, t_bf_free[s]])
                    if x >= NW - 1 and x + 1 < E:
                        pass
                    for k in range(4):
                        t = tr(PS[:, 0, k * 128:(k + 1) * 128], Bf[:, s, k * 128:(k + 1) * 128], [t_b, free[0]], sig=(k == 3))
                    t_bf_free[s] = t
                    t1 = act(lambda e: e.activation(BT[:, :, :], PS[:, 0, :].rearrange("p (k n) -> p k n", k=4), ACT.Copy), [t, t_bt])
                    free[0] = t1
                    for k in range(4):
                        t = mm(PS[:, 2, :], BT[:, k, :], W13[:, w, k, :], k == 0, k == 3, [t1, t_ew[x], free[2]], sig=(k == 3))
                    t_bt = t
                    t1 = act(lambda e: e.activation(eth[:, :], PS[:, 2, 0:256], ACT.Tanh, scale=0.5), [t, t_eh])
                    t1 = dve(lambda e: e.scalar_tensor_tensor(eth[:, :], eth[:, :], 1.0, PS[:, 2, 0:256], ALU.add, ALU.mult), [t1])
                    t_eh = dve(lambda e: e.tensor_tensor(eh[:, :], eth[:, :], PS[:, 2, 256:512], ALU.mult), [t1, t_ehT])
                    free[2] = t_eh
                    for k in range(2):
                        t = tr(PS[:, 1, k * 128:(k + 1) * 128], eh[:, k * 128:(k + 1) * 128], [t_eh, free[1]], sig=(k == 1))
                    t_ehT = t
                    t1 = act(lambda e: e.activation(ehT[:, :, :], PS[:, 1, 0:256].rearrange("p (k n) -> p k n", k=2), ACT.Copy), [t])
                    free[1] = t1
                    for k in range(2):
                        t = mm(PS[:, 3, :], ehT[:, k, :], W2[:, w, k, :], k == 0, k == 1, [t1, free[3]], sig=(k == 1))
                    if x + NW < E:
                        load_w(x + NW, t)
                    so = x % 2
                    t1 = act(lambda e, so=so: e.activation(OB[:, so, :], PS[:, 3, :], ACT.Copy), [t, t_ob_free[so]])
                    free[3] = t1
                    t_ob_free[so] = dma(lambda e, x=x, so=so: e.dma_start(obd[x * CAP:(x + 1) * CAP, :], OB[:, so, :]), Lo[so], [t1])
                NGB = 8
                Lg = [line(f"d{m}_g{i}", 16) for i in range(NGB)]
                t_gf = [None] * NGB
                t_xo = []
                for i in range(NT):
                    tt = t_xs[i]
                    for k in range(4):
                        s = (i * 4 + k) % NGB
                        gt = XN[:, s, :]
                        t = dma(lambda e, i=i, k=k, gt=gt: e.indirect_dma_start(
                            out=gt, out_offset=None, in_=obd,
                            in_offset=bass.IndirectOffsetOnAxis(ap=offs[:, k, i:i + 1], axis=0)),
                            Lg[s], [t_ob_free, t_gf[s], t_sc, (L_z, L_z.n)], "gpsimd")
                        tt = dve(lambda e, i=i, k=k, gt=gt: e.scalar_tensor_tensor(
                            X[:, i, :], gt, wk[:, i, k:k + 1], X[:, i, :], ALU.mult, ALU.add), [t, tt, t_wk])
                        t_gf[s] = tt
                    t_xo.append(tt)
                barrier()
            return t_xo

        def lru(t_xi):
            with ExitStack() as c:
                def s1(name, shape, dt=F32):
                    return sb(f"{name}_l", shape, dt, c)
                XN = s1("XN", [128, NT, D])
                BW = s1("BW", [128, 2, 4, 128])
                CWt = s1("CW", [128, 2, 512])
                LS = s1("LS", [128, 8])
                DB = s1("DB", [128, D])
                LL = [line(f"d_l{i}", 16) for i in range(4)]
                t_bw = [dma(lambda e, j=j: e.dma_start(BW[:, j, :, :], a[("bt", "btsw")[j]].rearrange("(c p) n -> p c n", p=128)), LL[0]) for j in range(2)][1]
                t_cw = [dma(lambda e, j=j: e.dma_start(CWt[:, j, :], a[("ct", "ctsw")[j]]), LL[1]) for j in range(2)][1]
                t_ls = dma(lambda e: e.dma_start(LS[:, 0:2], a["lsm"]), LL[2])
                t_db = dma(lambda e: e.dma_start(DB[:, :], a["dvec"]), LL[3])
                t_cw = dve(lambda e: e.tensor_scalar(CWt[:, 0, :], CWt[:, 0, :], CON[:, C_SGN:C_SGN + 1], None, ALU.mult), [t_cw])
                t_cw = dve(lambda e: e.tensor_scalar(CWt[:, 1, :], CWt[:, 1, :], -1.0, None, ALU.mult), [t_cw])
                c2 = s1("c2", [128, 4])
                col = lambda j: LS[:, j:j + 1]
                t = act(lambda e: e.activation(c2[:, 0:1], col(0), ACT.Abs), [t_ls])
                t = act(lambda e: e.activation(c2[:, 0:1], c2[:, 0:1], ACT.Exp, scale=-1.0), [t])
                t = act(lambda e: e.activation(c2[:, 1:2], c2[:, 0:1], ACT.Ln, bias=1.0), [t])
                t = dve(lambda e: e.scalar_tensor_tensor(c2[:, 1:2], col(0), 0.0, c2[:, 1:2], ALU.max, ALU.add), [t])
                t = act(lambda e: e.activation(c2[:, 1:2], c2[:, 1:2], ACT.Exp), [t])
                t = act(lambda e: e.activation(col(2), c2[:, 1:2], ACT.Exp, scale=-1.0), [t])
                t_th = act(lambda e: e.activation(c2[:, 2:3], col(1), ACT.Exp))
                t = dve(lambda e: e.tensor_tensor(col(3), col(2), col(2), ALU.mult), [t])
                t = dve(lambda e: e.tensor_scalar(col(3), col(3), -1.0, 1.0, ALU.mult, ALU.add), [t])
                t = dve(lambda e: e.tensor_scalar(col(3), col(3), 0.0, None, ALU.max), [t])
                t = act(lambda e: e.activation(col(3), col(3), ACT.Sqrt), [t])
                t_gam = dve(lambda e: e.tensor_tensor(col(4), col(3), CON[:, C_SGN:C_SGN + 1], ALU.mult), [t])
                t = dve(lambda e: e.tensor_scalar(c2[:, 2:3], c2[:, 2:3], 0.15915494309189535, None, ALU.mult), [t_th])
                t = dve(lambda e: e.tensor_scalar(c2[:, 3:4], c2[:, 2:3], MAGIC, -MAGIC, ALU.add, ALU.add), [t])
                t = dve(lambda e: e.tensor_tensor(c2[:, 2:3], c2[:, 2:3], c2[:, 3:4], ALU.subtract), [t])
                t = dve(lambda e: e.tensor_scalar(c2[:, 3:4], c2[:, 2:3], 4096.0, None, ALU.mult), [t])
                t = dve(lambda e: e.tensor_scalar(c2[:, 3:4], c2[:, 3:4], MAGIC, -MAGIC, ALU.add, ALU.add), [t])
                t = dve(lambda e: e.tensor_scalar(col(5), c2[:, 3:4], 1.0 / 4096, None, ALU.mult), [t])
                t_u = dve(lambda e: e.tensor_tensor(col(6), c2[:, 2:3], col(5), ALU.subtract), [t])
                ti = s1("ti", [128, T], I32)
                tf = s1("tf", [128, T])
                A1 = s1("A1", [128, T])
                A2 = s1("A2", [128, T])
                Ct = s1("Ct", [128, T])
                St = s1("St", [128, T])
                t = pool(lambda e: e.iota(ti[:, :], pattern=[[1, T]], base=0, channel_multiplier=0))
                t = dve(lambda e: e.tensor_copy(tf[:, :], ti[:, :]), [t])

                def wrap(src, dst, t):
                    t = dve(lambda e: e.tensor_scalar(A2[:, :], src[:, :], MAGIC, -MAGIC, ALU.add, ALU.add), [t])
                    return dve(lambda e: e.tensor_tensor(dst[:, :], src[:, :], A2[:, :], ALU.subtract), [t])
                t = dve(lambda e: e.tensor_scalar(A1[:, :], tf[:, :], col(5), None, ALU.mult), [t, t_u])
                t = wrap(A1, A1, t)
                t = dve(lambda e: e.scalar_tensor_tensor(A1[:, :], tf[:, :], col(6), A1[:, :], ALU.mult, ALU.add), [t])
                t = wrap(A1, A1, t)
                t_st = act(lambda e: e.activation(St[:, :], A1[:, :], ACT.Sin, scale=TWO_PI), [t])
                t = dve(lambda e: e.tensor_scalar(A1[:, :], A1[:, :], 0.25, None, ALU.add), [t_st])
                t = wrap(A1, A1, t)
                t_ct = act(lambda e: e.activation(Ct[:, :], A1[:, :], ACT.Sin, scale=TWO_PI), [t])
                t_xn, t_xt = layer_norm(t_xi, lambda i: XN[:, i, :], keep=True)
                bu = s1("bu", [128, 2, 512])
                r = A1
                g = A2
                t_bu = [None, None]
                t_g = None
                for n in range(4):
                    ns = slice(n * 512, n * 512 + 512)
                    t_r = []
                    for j in range(2):
                        b = 4 + j
                        for k in range(4):
                            t = mm(PS[:, b, :], BW[:, j, k, :], XNT[:, k, ns], k == 0, k == 3, [t_bw, t_xt, free[b]], sig=(k == 3))
                        t = act(lambda e, j=j, b=b: e.activation(bu[:, j, :], PS[:, b, :], ACT.Copy, scale=col(3 + j)), [t, t_gam, t_bu[j]])
                        free[b] = t
                        tab = (Ct, St)[j]
                        t_r.append(dve(lambda e, j=j, tab=tab, ns=ns: e.tensor_tensor(bu[:, j, :], bu[:, j, :], tab[:, ns], ALU.mult), [t, t_ct, t_st]))
                    t = dve(lambda e, ns=ns: e.tensor_tensor(r[:, ns], bu[:, 0, :], bu[:, 1, :], ALU.add), [t_r])
                    t_bu = [t, t]
                    init = 0.0 if n == 0 else g[:, n * 512 - 1:n * 512]
                    t_g = dve(lambda e, ns=ns, init=init: e.tensor_tensor_scan(
                        g[:, ns], col(2).to_broadcast([128, 512]), r[:, ns], init, ALU.mult, ALU.add), [t, t_g])
                    t1 = dve(lambda e, ns=ns: e.tensor_tensor(Ct[:, ns], g[:, ns], Ct[:, ns], ALU.mult), [t_g])
                    t_p = dve(lambda e, ns=ns: e.tensor_tensor(St[:, ns], g[:, ns], St[:, ns], ALU.mult), [t_g])
                    for tl in range(4):
                        i = n * 4 + tl
                        b = tl % 2
                        mm(PS[:, b, :], Ct[:, i * 128:(i + 1) * 128], CWt[:, 0, :], True, False, [t1, t_p, t_cw, free[b]])
                        t = mm(PS[:, b, :], St[:, i * 128:(i + 1) * 128], CWt[:, 1, :], False, True, sig=True)
                        t2 = dve(lambda e, i=i: e.tensor_tensor(XN[:, i, :], XN[:, i, :], DB[:, :], ALU.mult), [t_xn[i], t_xt[i], t_db])
                        t3 = dve(lambda e, i=i: e.tensor_tensor(X[:, i, :], X[:, i, :], XN[:, i, :], ALU.add), [t2, t_xi[i]])
                        t4 = dve(lambda e, i=i, b=b: e.tensor_tensor(X[:, i, :], X[:, i, :], PS[:, b, :], ALU.add), [t, t3])
                        free[b] = t4
                barrier()

        t_o = [t_x[i // 4] for i in range(NT)]
        if stage >= 1:
            delta_net()
            t_o = [None] * NT
        if stage >= 2:
            moe(0, t_o)
        if stage >= 3:
            lru(t_o)
        if stage >= 4:
            moe(1, t_o)
        barrier()
        L_out = line("d_out", 16)
        ov = out.rearrange("b (i p) n -> p (b i) n", p=128)
        dma(lambda e: e.dma_start(ov, X[:, :, :]), L_out)
        q["sync"].append(([(L_out, L_out.n)], None, None))

        block = ctx.enter_context(nc.Block())

        def run(eng, name):
            seen = {}
            for waits, fn, on in q[name]:
                need = {}
                for ln, v in waits:
                    if v > seen.get(ln, 0):
                        need[ln] = max(v, need.get(ln, 0))
                for ln, v in need.items():
                    eng.wait_ge(ln.sem, v)
                    seen[ln] = v
                if fn is not None:
                    ins = fn(eng)
                    if on is not None:
                        ins.then_inc(on.sem, on.by)

        @block.sync
        def _(eng):
            run(eng, "sync")

        @block.scalar
        def _(eng):
            run(eng, "scalar")

        @block.vector
        def _(eng):
            run(eng, "vector")

        @block.tensor
        def _(eng):
            run(eng, "tensor")

        @block.gpsimd
        def _(eng):
            run(eng, "gpsimd")


def layout(i):
    import numpy as _np
    f = lambda n: _np.asarray(i["L0_" + n])
    cat = _np.concatenate
    rows = lambda v: _np.broadcast_to(v, (128,) + v.shape)
    small = _np.zeros((128, 16), _np.float32)
    small[:, 0:6] = f("attn_a_dt_bias")
    small[:, 6:12] = f("attn_a_A_log")
    small[:, 12] = f("attn_a_norm_w")
    br, bi, cr, ci = (f("attn_b_" + n).T for n in ("B_re", "B_im", "C_re", "C_im"))
    lsm = _np.stack([cat([f("attn_b_nu_log")] * 2), cat([f("attn_b_theta_log")] * 2)], 1)
    d = {
        "x": f("attn_a_x"), "consts": shape_constants(), "small": small, "lsm": lsm,
        "wqkvg": cat([f("attn_a_" + n) for n in ("Wq", "Wk", "Wv", "Wg")]).T,
        "wab": cat([f("attn_a_Wa"), f("attn_a_Wb")]).T, "wo": f("attn_a_Wo").T,
        "convw": cat([f("attn_a_conv_q_w"), f("attn_a_conv_k_w"), f("attn_a_conv_v_w")])[:, 0, :],
        "bt": cat([br, bi], 1), "btsw": cat([bi, br], 1), "ct": cat([cr, ci]), "ctsw": cat([ci, cr]),
        "dvec": rows(f("attn_b_D")), "gw": f("ffn_gate_w").T, "gb": rows(f("ffn_gate_bias")),
        "w13": cat([f("ffn_w1"), f("ffn_w3")], 2), "w2": f("ffn_w2"),
        "sg": f("ffn_shared_gate"), "su": f("ffn_shared_up"), "sd": f("ffn_shared_down"),
    }
    return {k: _np.ascontiguousarray(v) for k, v in d.items()}


def kernel(**inputs):
    import numpy as _np
    import concourse.bacc as _bacc
    from concourse import mybir as _mybir
    from concourse.bass_utils import run_bass_kernel_spmd as _run

    nc = _bacc.Bacc("TRN2", target_bir_lowering=False, num_devices=1)
    arrays, args = {}, {}
    for name, v in layout(inputs).items():
        arrays[f"in_{name}_dram"] = v
        args[name] = nc.dram_tensor(f"in_{name}_dram", v.shape, _mybir.dt.from_np(v.dtype), kind="ExternalInput").ap()
    out = nc.dram_tensor("out_0_dram", (1, 2048, 512), _mybir.dt.float32, kind="ExternalOutput").ap()
    program(nc, args, out)
    r = _run(nc, [arrays], core_ids=[0])
    return r.results[0]["out_0_dram"]
```

```python
from contextlib import ExitStack

import numpy as np
import concourse.bass as bass
from concourse import mybir

F32 = mybir.dt.float32
F32R = mybir.dt.float32r
U32 = mybir.dt.uint32
I32 = mybir.dt.int32
ALU = mybir.AluOpType
ACT = mybir.ActivationFunctionType
AX = mybir.AxisListType

T = 2048
D = 512
NT = 16
H = 6
DK = 64
E = 32
CAP = 128
TB = 256
NB = T // TB
MAGIC = 12582912.0
TWO_PI = 6.283185
LEVELS = (1, 2, 4, 8, 16, 32, 64)
C_ID, C_TRI, C_STRI, C_M1T = 0, 128, 256, 384
C_MASK = 512
C_BONE = C_MASK + 6 * 128
C_IOTA = C_BONE + 2
C_SGN = C_IOTA + 32
C_U = C_SGN + 2
C_L = C_U + 16
C_N = C_L + 16


def shape_constants():
    c = np.zeros((128, C_N), np.float32)
    r = np.arange(128)
    s, t = r[:, None], r[None, :]
    c[:, C_ID:C_ID + 128] = s == t
    c[:, C_TRI:C_TRI + 128] = s <= t
    c[:, C_STRI:C_STRI + 128] = s < t

    def level(n, row, col):
        return (row == col) | ((row // (2 * n) == col // (2 * n)) & (row // n % 2 == 1) & (col // n % 2 == 0))

    c[:, C_M1T:C_M1T + 128] = level(1, t, s)
    for i, n in enumerate(LEVELS[1:7]):
        c[:, C_MASK + 128 * i:C_MASK + 128 * i + 128] = level(n, s, t)
    c[:64, C_BONE] = 1
    c[64:, C_BONE + 1] = 1
    c[:, C_IOTA:C_IOTA + 32] = np.arange(32)
    c[:64, C_SGN] = 1
    c[64:, C_SGN] = -1
    c[:, C_SGN + 1] = -1
    i, j = np.arange(16) // 4, np.arange(16) % 4
    c[:, C_U:C_U + 16] = j > i
    c[:, C_L:C_L + 16] = j < i
    return c


class Line:

    def __init__(self, sem, by=1):
        self.sem, self.by, self.n = sem, by, 0

    def up(self):
        self.n += self.by
        return (self, self.n)


def program(nc, a, out, stage=9):
    ctx = ExitStack()
    q = {"sync": [], "scalar": [], "vector": [], "tensor": [], "gpsimd": []}
    lines = []

    def line(name, by=1):
        x = Line(ctx.enter_context(nc.semaphore(name)), by)
        lines.append(x)
        return x

    def flat(w):
        if w is None:
            return []
        if isinstance(w, tuple) and w and isinstance(w[0], Line):
            return [w]
        return [y for x in w for y in flat(x)]

    def op(engine, fn, waits=(), on=None):
        q[engine].append((flat(waits), fn, on))
        return on.up() if on is not None else None

    def fence(waits):
        for engine in q:
            q[engine].append((flat(waits), None, None))

    def merge(threads):
        at = [[0, n, gen] for gen, n in threads if gen is not None]
        while at:
            x = min(at, key=lambda x: x[0] / x[1])
            x[0] += 1
            if next(x[2], 0) == 0:
                at.remove(x)

    def barrier():
        now = [(x, x.n) for x in lines if x.n]
        for engine in q:
            q[engine].append((now, None, None))

    with ctx:
        L_pe, L_dve, L_act, L_pool = line("pe"), line("dve"), line("act"), line("pool")

        def pe(fn, waits=(), sig=True):
            return op("tensor", fn, waits, L_pe if sig else None)

        def dve(fn, waits=()):
            return op("vector", fn, waits, L_dve)

        def act(fn, waits=()):
            return op("scalar", fn, waits, L_act)

        def pool(fn, waits=()):
            return op("gpsimd", fn, waits, L_pool)

        def dma(fn, on, waits=(), engine="sync"):
            return op(engine, fn, waits, on)

        def mm(o, lhsT, rhs, start=True, stop=True, waits=(), sig=False, skip=False):
            return pe(lambda e: e.matmul(o, lhsT, rhs, start=start, stop=stop, skip_group_check=skip), waits, sig)

        def tr(o, i, waits=(), sig=False):
            n = i.shape[0]
            return pe(lambda e: e.transpose(o, i, ident[0:n, 0:n]), waits, sig)

        def sb(name, shape, dt=F32, c=ctx):
            return c.enter_context(nc.sbuf_tensor(name, shape, dt))

        PS = ctx.enter_context(nc.psum_tensor("PS", [128, 8, 512], F32))
        free = [None] * 8

        X = sb("X", [128, NT, D])
        CON = sb("CON", [128, C_N])
        ones = sb("ones", [128, 128])
        ident = CON[:, C_ID:C_ID + 128]
        triu = CON[:, C_TRI:C_TRI + 128]
        stri = CON[:, C_STRI:C_STRI + 128]
        bst = sb("bst", [128, NT, 6])
        bmv = sb("bmv", [128, NT, 2])
        rstd = sb("rstd", [128, NT])
        pw = sb("pw", [128, 64])

        L_x = [line(f"d_x{i}", 16) for i in range(4)]
        L_con, L_ls = line("d_con", 16), line("d_ls", 16)
        L_tb = [line("d_tb0", 16), line("d_tb1", 16)]
        L_ti = [line(f"d_ti{i}", 16) for i in range(4)]
        L_w = [line(f"d_w{i}", 16) for i in range(8)]
        t_con = dma(lambda e: e.dma_start(CON[:, :], a["consts"]), L_con)
        xv = a["x"].rearrange("b (i p) n -> p (b i) n", p=128)
        t_x = [dma(lambda e, i=i: e.dma_start(X[:, 4 * i:4 * i + 4, :], xv[:, 4 * i:4 * i + 4, :]), L_x[i])
               for i in range(4)]
        t_ones = pool(lambda e: e.memset(ones[:, :], 1.0))
        t_pw = pool(lambda e: e.memset(pw[:, :], -0.5))

        LS = sb("LS", [128, 8])
        c2 = sb("c2", [128, 4])
        tabs = nc.dram_tensor("rot", [2, 128, T], F32, kind="Internal").ap()
        buf = nc.dram_tensor("moe_buf", [E * CAP, D], F32, kind="Internal").ap()
        obd = nc.dram_tensor("moe_out", [E * CAP + 128, D], F32, kind="Internal").ap()
        zero = sb("zero", [128, 128])
        t_z = pool(lambda e: e.memset(zero[:, :], 0.0))
        L_z = line("d_z", 16)
        for j in range(E):
            dma(lambda e, j=j: e.dma_start(buf[j * 128:(j + 1) * 128, :].rearrange("p (a n) -> p a n", n=128), zero[:, :].unsqueeze(1).to_broadcast([128, 4, 128])), L_z, [t_z], "gpsimd")
        dma(lambda e: e.dma_start(obd[E * CAP:E * CAP + 128, :].rearrange("p (a n) -> p a n", n=128), zero[:, :].unsqueeze(1).to_broadcast([128, 4, 128])), L_z, [t_z], "gpsimd")

        def moments(i, t):
            t = dve(lambda e: e.bn_stats(bst[:, i, :], X[:, i, :]), [t])
            return dve(lambda e: e.bn_aggr(bmv[:, i, :], bst[:, i, :]), [t])

        def inverse_std(ii, t):
            t = dve(lambda e: e.tensor_scalar(rstd[:, ii], bmv[:, ii, 1], 1e-5, None, ALU.add), [t])
            return pool(lambda e: e.tensor_tensor(rstd[:, ii], rstd[:, ii], pw[:, ii], ALU.pow), [t, t_pw])

        def normalise(i, xn, t):
            return dve(lambda e: e.tensor_scalar(xn, X[:, i, :], bmv[:, i, 0:1], rstd[:, i:i + 1], ALU.subtract, ALU.mult), [t])

        def transpose_tile(xn, dst, b, t, t_dst):
            for k in range(4):
                t1 = tr(PS[:, b, k * 128:(k + 1) * 128], xn[:, k * 128:(k + 1) * 128], [t, free[b], t_con], sig=(k == 3))
            free[b] = act(lambda e: e.activation(dst, PS[:, b, :].rearrange("p (k n) -> p k n", k=4), ACT.Copy), [t1, t_dst])
            return t1, free[b]

        def delta_net():
            with ExitStack() as c:
                def s1(name, shape, dt=F32):
                    return sb(name, shape, dt, c)
                W = s1("W", [128, 4, 2304])
                WO = s1("WO", [128, H, D])
                WAB = s1("WAB", [128, 4, 12])
                CW = s1("CW", [128, 12, 4])
                SM = s1("SM", [128, 16])
                trr = s1("trr", [128, 128], F32R)
                t_sm = dma(lambda e: e.dma_start(SM[:, :], a["small"]), L_w[1])
                t_wab = dma(lambda e: e.dma_start(WAB[:, :, :], a["wab"].rearrange("(c p) n -> p c n", p=128)), L_w[0])
                t_cw = dma(lambda e: e.dma_start(CW[:, :, :], a["convw"].rearrange("(c p) n -> p c n", p=128)), L_w[2])
                wv = a["wqkvg"].rearrange("(c p) n -> p c n", p=128)
                t_w = []
                for j in range(3):
                    t_w.append(dma(lambda e, j=j: e.dma_start(W[:, :, 768 * j:768 * j + 768], wv[:, :, 768 * j:768 * j + 768]), L_w[3 + j]))
                t_wo = dma(lambda e: e.dma_start(WO[:, :, :], a["wo"].rearrange("(c p) n -> p c n", p=128)), L_w[6])
                t_trr = dve(lambda e: e.tensor_copy(trr[:, :], triu), [t_con])
                t_wo = act(lambda e: e.activation(WO[:, :, :], WO[:, :, :], ACT.Copy, scale=SM[:, 12:13]), [t_wo, t_sm])

                xnt2 = s1("xnt2", [128, 2, D])
                XB = s1("XB", [128, 3, 4, TB])
                kv = s1("kv", [128, 2, 9, TB])
                qb = s1("qb", [128, 3, 3, TB])
                raw = s1("raw", [128, 12, 3 + TB])
                cacc = s1("cacc", [128, 2, TB])
                th = s1("th", [128, 2, TB])
                sq = s1("sq", [128, 2, TB])
                rn = s1("rn", [128, NT, 12])
                za = s1("za", [128, NT, H])
                sp = s1("sp", [128, NT, H])
                g = s1("g", [128, NT, H])
                gh = s1("gh", [128, 2, NT, H], F32R)
                beta = s1("beta", [128, NT, H])
                ea = s1("ea", [128, H])
                G = s1("G", [128, NT, H])
                eG = s1("eG", [128, NT, H])
                neG = s1("neG", [128, NT, H])
                dG = s1("dG", [128, NT, H])
                eC = s1("eC", [128, NT, 3])
                nb = s1("nb", [128, NT, H])

                kh = s1("kh", [128, 3, 2, DK])
                kd = s1("kd", [128, 2, 3, 2, DK])
                khT = s1("khT", [128, 2, 3, 128])
                V = s1("V", [128, 2, H, 128])
                Dm = s1("Dm", [128, H, 128])
                NTm = s1("NTm", [128, H, 128])
                NTr = s1("NTr", [128, H, 128], F32R)
                P = s1("P", [128, 2, H, 128])
                R = s1("R", [128, H, 128], F32R)
                Rf = s1("Rf", [128, 2, H, 128])
                Tm = s1("Tm", [128, H, 128], F32R)
                Z = s1("Z", [128, H, 128], F32R)
                S = s1("S", [128, 2, 3, 128])
                o = s1("o", [128, H, 128])
                gs = s1("gs", [128, H, 128])
                ms = s1("ms", [128, H])

                t_halo = [pool(lambda e: e.memset(raw[:, :, 0:3], 0.0))]
                t_S = [pool(lambda e: e.memset(S[:, 0, :, :], 0.0))]
                t_ea = act(lambda e: e.activation(ea[:, :], SM[:, H:2 * H], ACT.Exp), [t_sm])

                def cols(x, h):
                    return x[:, h * 128:h * 128 + 128]

                def grp(x, gr):
                    return x[:, 3 * gr:3 * gr + 3, :].rearrange("p h n -> p (h n)")

                rel = {}
                done = {}

                def tables():
                    def col(j):
                        return LS[:, j:j + 1]
                    t_ls = dma(lambda e: e.dma_start(LS[:, 0:2], a["lsm"]), L_ls)
                    t_th = act(lambda e: e.activation(c2[:, 2:3], col(1), ACT.Exp), [t_ls])
                    t = act(lambda e: e.activation(c2[:, 0:1], col(0), ACT.Abs))
                    t = act(lambda e: e.activation(c2[:, 0:1], c2[:, 0:1], ACT.Exp, scale=-1.0), [t])
                    t = act(lambda e: e.activation(c2[:, 1:2], c2[:, 0:1], ACT.Ln, bias=1.0), [t])
                    t = dve(lambda e: e.scalar_tensor_tensor(c2[:, 1:2], col(0), 0.0, c2[:, 1:2], ALU.max, ALU.add), [t])
                    t = act(lambda e: e.activation(c2[:, 1:2], c2[:, 1:2], ACT.Exp), [t])
                    t = act(lambda e: e.activation(col(2), c2[:, 1:2], ACT.Exp, scale=-1.0), [t])
                    t = dve(lambda e: e.tensor_tensor(col(3), col(2), col(2), ALU.mult), [t])
                    t = dve(lambda e: e.tensor_scalar(col(3), col(3), -1.0, 1.0, ALU.mult, ALU.add), [t])
                    t = dve(lambda e: e.tensor_scalar(col(3), col(3), 0.0, None, ALU.max), [t])
                    t = act(lambda e: e.activation(col(3), col(3), ACT.Sqrt), [t])
                    dve(lambda e: e.tensor_tensor(col(4), col(3), CON[:, C_SGN:C_SGN + 1], ALU.mult), [t, t_con])
                    t = dve(lambda e: e.tensor_scalar(c2[:, 2:3], c2[:, 2:3], 0.15915494309189535, None, ALU.mult), [t_th])
                    t = dve(lambda e: e.tensor_scalar(c2[:, 3:4], c2[:, 2:3], MAGIC, -MAGIC, ALU.add, ALU.add), [t])
                    t = dve(lambda e: e.tensor_tensor(c2[:, 2:3], c2[:, 2:3], c2[:, 3:4], ALU.subtract), [t])
                    t = dve(lambda e: e.tensor_scalar(c2[:, 3:4], c2[:, 2:3], 4096.0, None, ALU.mult), [t])
                    t = dve(lambda e: e.tensor_scalar(c2[:, 3:4], c2[:, 3:4], MAGIC, -MAGIC, ALU.add, ALU.add), [t])
                    t = dve(lambda e: e.tensor_scalar(col(5), c2[:, 3:4], 1.0 / 4096, None, ALU.mult), [t])
                    t_u = dve(lambda e: e.tensor_tensor(col(6), c2[:, 2:3], col(5), ALU.subtract), [t])
                    yield
                    rf = Rf[:, :, :, :].rearrange("p s h n -> p (s h n)")
                    pf = P[:, :, :, :].rearrange("p s h n -> p (s h n)")
                    tf, A1, A2 = rf[:, 0:512], rf[:, 512:1024], rf[:, 1024:1536]

                    def wrap(t):
                        t = dve(lambda e: e.tensor_scalar(A2, A1, MAGIC, -MAGIC, ALU.add, ALU.add), [t])
                        return dve(lambda e: e.tensor_tensor(A1, A1, A2, ALU.subtract), [t])
                    t_s, t_o = None, [None, None]
                    for n in range(4):
                        t_i = dma(lambda e, n=n: e.dma_start(tf, a["tidx"][:, 512 * n:512 * n + 512]), L_ti[n], [t_s])
                        t = dve(lambda e: e.tensor_scalar(A1, tf, col(5), None, ALU.mult), [t_i, t_u, t_s])
                        t = wrap(t)
                        t = dve(lambda e: e.scalar_tensor_tensor(A1, tf, col(6), A1, ALU.mult, ALU.add), [t])
                        t = wrap(t)
                        yield
                        for j in (1, 0):
                            dst = pf[:, 512 * j:512 * j + 512]
                            if j == 0:
                                t = dve(lambda e: e.tensor_scalar(A1, A1, 0.25, None, ALU.add), [t])
                                t = wrap(t)
                            t = act(lambda e, dst=dst: e.activation(dst, A1, ACT.Sin, scale=TWO_PI), [t, t_o[j]])
                            t_o[j] = dma(lambda e, n=n, j=j, dst=dst: e.dma_start(tabs[j, :, 512 * n:512 * n + 512], dst), L_tb[j], [t])
                            yield
                        t_s = t
                    rel[("P", 0)] = rel[("P", 1)] = t_o
                    rel[("Rf", 0)] = rel[("Rf", 1)] = t_s

                def proj(B):
                    x3, k2, q3 = B % 3, B % 2, B % 3
                    tt = slice(2 * B, 2 * B + 2)
                    t_r = inverse_std(tt, [moments(i, t_x[i // 4]) for i in (2 * B, 2 * B + 1)])
                    t_xb = []
                    for u, i in enumerate((2 * B, 2 * B + 1)):
                        t = normalise(i, xnt2[:, u, :], [t_r, rel.get(("xn", u))])
                        rel[("xn", u)], t2 = transpose_tile(
                            xnt2[:, u, :], XB[:, x3, :, u * 128:(u + 1) * 128], 6 + u, t, rel.get(("XB", x3)))
                        t_xb.append(t2)
                        yield
                    for u in range(2):
                        for k in range(4):
                            t = mm(PS[:, 6, u * 12:u * 12 + 12], XB[:, x3, k, u * 128:(u + 1) * 128], WAB[:, k, :],
                                   k == 0, k == 3, [t_xb, t_wab, free[6]], sig=(k == 3))
                    yield
                    ab = PS[:, 6, 0:24].rearrange("p (i n) -> p i n", n=12)
                    z2 = za[:, tt, :]
                    t1 = dve(lambda e: e.tensor_tensor(z2, ab[:, :, 0:H], SM[:, 0:H].unsqueeze(1).to_broadcast([128, 2, H]), ALU.add), [t, t_sm])
                    t4 = act(lambda e: e.activation(beta[:, tt, :], ab[:, :, H:12], ACT.Exp, scale=-1.0), [t1])
                    free[6] = t4
                    t3 = act(lambda e: e.activation(sp[:, tt, :], z2, ACT.Abs), [t1])
                    t3 = act(lambda e: e.activation(sp[:, tt, :], sp[:, tt, :], ACT.Exp, scale=-1.0), [t3])
                    t3 = act(lambda e: e.activation(sp[:, tt, :], sp[:, tt, :], ACT.Ln, bias=1.0), [t3])
                    t8 = dve(lambda e: e.tensor_scalar(beta[:, tt, :], beta[:, tt, :], 1.0, None, ALU.add), [t4])
                    t8 = dve(lambda e: e.reciprocal(beta[:, tt, :], beta[:, tt, :]), [t8])
                    t_nb = dve(lambda e: e.tensor_scalar(nb[:, tt, :], beta[:, tt, :], -1.0, None, ALU.mult), [t8])
                    t7 = dve(lambda e: e.scalar_tensor_tensor(sp[:, tt, :], z2, 0.0, sp[:, tt, :], ALU.max, ALU.add), [t3])
                    t_g = dve(lambda e: e.scalar_tensor_tensor(
                        g[:, tt, :], sp[:, tt, :], -1.0, ea[:, :].unsqueeze(1).to_broadcast([128, 2, H]), ALU.mult, ALU.mult), [t7, t_ea])
                    t1 = dve(lambda e: e.tensor_copy(gh[:, 0, tt, :], g[:, tt, :]), [t_g])
                    t_gh = dve(lambda e: e.tensor_tensor(gh[:, 1, tt, :], g[:, tt, :], gh[:, 0, tt, :].bitcast(F32), ALU.subtract), [t1])
                    gf = g[:, tt, :].rearrange("p i h -> p (i h)")
                    mm(PS[:, 6, 0:12], triu, gf, True, True, [t_g, free[6]])
                    t = mm(PS[:, 6, 16:28], ones[:, :], gf, True, True, [t_ones], sig=True)
                    yield
                    Gp = PS[:, 6, 0:12].rearrange("p (i h) -> p i h", h=H)
                    Cp = PS[:, 6, 16:28].rearrange("p (i h) -> p i h", h=H)
                    t_G = dve(lambda e: e.tensor_copy(G[:, tt, :], Gp), [t])
                    t1 = dve(lambda e: e.tensor_tensor(dG[:, tt, :], Cp, G[:, tt, :], ALU.subtract), [t_G])
                    act(lambda e: e.activation(eC[0:64, tt, :], Cp[0:64, :, 0:3], ACT.Exp), [t1])
                    t_eC = act(lambda e: e.activation(eC[64:128, tt, :], Cp[64:128, :, 3:6], ACT.Exp))
                    free[6] = t_eC
                    t_eG = act(lambda e: e.activation(eG[:, tt, :], G[:, tt, :], ACT.Exp), [t_G])
                    t2 = act(lambda e: e.activation(dG[:, tt, :], dG[:, tt, :], ACT.Exp), [t1])
                    t_neG = dve(lambda e: e.tensor_scalar(neG[:, tt, :], eG[:, tt, :], -1.0, None, ALU.mult), [t_eG])
                    t_dG = dve(lambda e: e.tensor_tensor(dG[:, tt, :], dG[:, tt, :], beta[:, tt, :], ALU.mult), [t2])
                    t_conv, t_last = [], {}
                    for ct in range(12):
                        b = 6 + ct % 2
                        u = ct % 2
                        dst = qb[:, q3, ct, :] if ct < 3 else kv[:, k2, ct - 3, :]
                        t_dst = rel.get(("qb", q3)) if ct < 3 else rel.get(("kv", k2))
                        for k in range(4):
                            t = mm(PS[:, b, 0:TB], W[:, k, ct * 128:(ct + 1) * 128], XB[:, x3, k, :],
                                   k == 0, k == 3, [t_w[ct // 6], free[b], t_xb], sig=(k == 3))
                        t1 = act(lambda e, ct=ct, b=b: e.activation(raw[:, ct, 3:3 + TB], PS[:, b, 0:TB], ACT.Copy), [t, t_halo])
                        t2 = act(lambda e, ct=ct, b=b, u=u: e.activation(cacc[:, u, :], PS[:, b, 0:TB], ACT.Copy, scale=CW[:, ct, 3:4]), [t, t_cw, rel.get(("cacc", u))])
                        free[b] = t2
                        t3 = [t1, t2]
                        for j in range(3):
                            t3 = dve(lambda e, ct=ct, j=j, u=u: e.scalar_tensor_tensor(
                                cacc[:, u, :], raw[:, ct, j:j + TB], CW[:, ct, j:j + 1], cacc[:, u, :], ALU.mult, ALU.add), [t3])
                        t_conv.append(t3)
                        t4 = act(lambda e, u=u: e.activation(th[:, u, :], cacc[:, u, :], ACT.Tanh, scale=0.5), [t3, rel.get(("cacc", u))])
                        t5 = dve(lambda e, dst=dst, u=u: e.scalar_tensor_tensor(
                            dst, th[:, u, :], 1.0, cacc[:, u, :], ALU.add, ALU.mult), [t4, t_dst])
                        rel[("cacc", u)] = t5
                        if ct < 6:
                            t_qk = t5
                        yield
                        if ct == 7:
                            for j in range(6):
                                src = qb[:, q3, j, :] if j < 3 else kv[:, k2, j - 3, :]
                                t_sq = act(lambda e, j=j, src=src: e.activation(sq[:, j % 2, :], src, ACT.Square), [t_qk, rel.get(("sq", j % 2))])
                                for cl in range(2):
                                    o0 = cl * 12 + (j // 3) * 6 + j % 3
                                    t = mm(PS[:, 6, o0:o0 + 4:3], sq[:, j % 2, cl * 128:cl * 128 + 128], CON[:, C_BONE:C_BONE + 2], True, True,
                                           [t_sq, t_con, free[6]], sig=(cl == 1))
                                rel[("sq", j % 2)] = t
                            t1 = dve(lambda e: e.tensor_scalar(rn[:, tt, :], PS[:, 6, 0:24].rearrange("p (i n) -> p i n", n=12), 4e-6, None, ALU.add), [t])
                            free[6] = t1
                            t_rn = pool(lambda e: e.tensor_tensor(rn[:, tt, :], rn[:, tt, :], pw[:, 0:24].rearrange("p (i n) -> p i n", n=12), ALU.pow), [t1, t_pw])
                            yield
                    t_halo[0] = pool(lambda e: e.tensor_copy(raw[:, :, 0:3], raw[:, :, TB:TB + 3]), [t_conv])
                    done[B] = dict(qkv=t5, rn=t_rn, gh=t_gh, G=t_G, eG=t_eG, neG=t_neG, dG=t_dG, nb=t_nb, eC=t_eC)

                def solve(ch):
                    B, cl, s2 = ch // 2, ch % 2, ch % 2
                    k2, q3 = B % 2, B % 3
                    cs = slice(cl * 128, cl * 128 + 128)
                    ok = done[B]
                    for j in range(3):
                        t = tr(PS[:, 0, j * 128:(j + 1) * 128], kv[:, k2, j, cs], [ok["qkv"], free[0]], sig=(j == 2))
                    for gr in range(2):
                        for j in range(3):
                            tv = tr(PS[:, 1 + 2 * gr, j * 128:(j + 1) * 128], kv[:, k2, 3 + 3 * gr + j, cs],
                                    [free[1], free[3]], sig=(gr == 1 and j == 2))
                    rel[("kv", k2)] = tv
                    t_kh = dve(lambda e: e.tensor_tensor(
                        kh[:, :, :, :], PS[:, 0, 0:384].rearrange("p (j g d) -> p j g d", d=DK, g=2),
                        rn[:, ch, 6:12].rearrange("p (g j) -> p j g", g=2).unsqueeze(3).to_broadcast([128, 3, 2, DK]), ALU.mult),
                        [t, ok["rn"], rel.get("kh")])
                    free[0] = t_kh
                    t_V = [act(lambda e, gr=gr: e.activation(
                        grp(V[:, s2, :, :], gr), PS[:, 1 + 2 * gr, 0:384], ACT.Copy, scale=0.5),
                        [tv, rel.get(("V", s2))]) for gr in range(2)]
                    free[1] = free[3] = t_V
                    for gr in range(2):
                        for j in range(3):
                            h = 3 * gr + j
                            for p in range(2):
                                t = mm(cols(PS[:, 2 + gr, :], j), gh[:, p, ch, h:h + 1].to_broadcast([128, 128]), trr[:, :],
                                       p == 0, p == 1, [free[2 + gr], ok["gh"], t_trr], sig=(j == 2 and p == 1))
                        for j in range(3):
                            h = 3 * gr + j
                            t1 = dve(lambda e, h=h, j=j, gr=gr: e.tensor_scalar(
                                Dm[:, h, :], cols(PS[:, 2 + gr, :], j), G[:, ch, h:h + 1], 0.0, ALU.subtract, ALU.min),
                                [t, rel.get("Dm")])
                        free[2 + gr] = t1
                    t_kd = pool(lambda e: e.tensor_tensor(
                        kd[:, s2, :, :, :], kh[:, :, :, :],
                        dG[:, ch, :].rearrange("p (g j) -> p j g", g=2).unsqueeze(3).to_broadcast([128, 3, 2, DK]), ALU.mult),
                        [t_kh, ok["dG"], rel.get(("kd", s2))])
                    for j in range(3):
                        t = tr(PS[:, 0, j * 128:(j + 1) * 128], kh[:, j, :, :].rearrange("p g d -> p (g d)"), [t_kh, free[0]], sig=(j == 2))
                    rel["kh"] = [t, t_kd]
                    t_khT = act(lambda e: e.activation(
                        khT[:, s2, :, :], PS[:, 0, 0:384].rearrange("p (j n) -> p j n", n=128), ACT.Copy),
                        [t, rel.get(("khT", s2))])
                    free[0] = t_khT
                    yield
                    t1 = act(lambda e: e.activation(Dm[:, :, :], Dm[:, :, :], ACT.Exp), [t1])
                    t1 = pool(lambda e: e.affine_select(
                        out=Dm[:, :, :], in_=Dm[:, :, :], compare_op=ALU.is_ge, fill=0.0, base=0,
                        pattern=[[0, H], [1, 128]], channel_multiplier=-1), [t1])
                    t_D = pool(lambda e: e.tensor_tensor(
                        Dm[:, :, :], Dm[:, :, :], nb[:, ch, :].unsqueeze(2).to_broadcast([128, H, 128]), ALU.mult), [t1, ok["nb"]])
                    for j in range(3):
                        for gr in range(2):
                            p0 = 64 * gr
                            tk = mm(cols(PS[:, 2 * gr, :], j), khT[p0:p0 + 64, s2, j, :], khT[p0:p0 + 64, s2, j, :], True, True,
                                    [free[2 * gr], t_khT], sig=(j == 2))
                    yield
                    for j in range(3):
                        for gr in range(2):
                            p0 = 64 * gr
                            t = mm(cols(PS[:, 2 * gr + 1, :], j), khT[p0:p0 + 64, s2, j, :], qb[p0:p0 + 64, q3, j, cs], True, True,
                                   [free[2 * gr + 1]], sig=(j == 2))
                    yield
                    t_N, t_R, t_Nr = [None] * 2, [None] * 2, [None] * 2
                    for gr in range(2):
                        t1 = dve(lambda e, gr=gr: e.tensor_tensor(grp(NTm, gr), PS[:, 2 * gr, 0:384], grp(Dm, gr), ALU.mult), [tk, t_D, rel.get("NTm")])
                        free[2 * gr] = t1
                        t_Nr[gr] = pool(lambda e, gr=gr: e.affine_select(
                            out=NTr[:, 3 * gr:3 * gr + 3, :], in_=NTm[:, 3 * gr:3 * gr + 3, :], compare_op=ALU.not_equal, fill=1.0, base=0,
                            pattern=[[0, 3], [-1, 128]], channel_multiplier=1), [t1, rel.get(("NTr", gr))])
                    for gr in range(2):
                        t_N[gr] = pool(lambda e, gr=gr: e.affine_select(
                            out=NTm[:, 3 * gr:3 * gr + 3, :], in_=NTm[:, 3 * gr:3 * gr + 3, :], compare_op=ALU.not_equal, fill=-1.0, base=0,
                            pattern=[[0, 3], [-1, 128]], channel_multiplier=1), [t_Nr[gr]])
                    t_P = []
                    for gr in range(2):
                        t1 = dve(lambda e, gr=gr: e.tensor_tensor(grp(P[:, s2, :, :], gr), PS[:, 2 * gr + 1, 0:384], grp(Dm, gr), ALU.mult),
                                 [t, t_D, rel.get(("P", s2))])
                        free[2 * gr + 1] = t1
                        t_P.append(t1)
                    rel["Dm"] = t_P
                    for gr in range(2):
                        t_R[gr] = dve(lambda e, gr=gr: e.tensor_tensor(
                            R[:, 3 * gr:3 * gr + 3, :], NTr[:, 3 * gr:3 * gr + 3, :].bitcast(F32),
                            CON[:, C_M1T:C_M1T + 128].unsqueeze(1).to_broadcast([128, 3, 128]), ALU.mult), [t_Nr[gr], rel.get(("R", gr))])
                    t_T = [None] * 2
                    for gr in range(2):
                        for j in range(3):
                            t = tr(cols(PS[:, 2 * gr + 1, :], j), R[:, 3 * gr + j, :].bitcast(F32), [t_R[gr], free[2 * gr + 1]], sig=(j == 2))
                        t_T[gr] = act(lambda e, gr=gr: e.activation(grp(Tm, gr), PS[:, 2 * gr + 1, 0:384], ACT.Copy), [t, rel.get(("Tm", gr))])
                        free[2 * gr + 1] = t_T[gr]
                    yield
                    t_Z, t_Zr = [None] * 2, [rel.get(("Z", 0)), rel.get(("Z", 1))]
                    for li in range(6):
                        m = CON[:, C_MASK + 128 * li:C_MASK + 128 * li + 128]
                        for gr in range(2):
                            for j in range(3):
                                h = 3 * gr + j
                                t = mm(cols(PS[:, 2 * gr, :], j), NTr[:, h, :], Tm[:, h, :], True, True,
                                       [t_Nr[gr], t_T[gr], free[2 * gr]], sig=(j == 2))
                            if li == 5:
                                rel[("NTr", gr)] = t
                            t_Z[gr] = dve(lambda e, gr=gr, m=m: e.tensor_tensor(
                                Z[:, 3 * gr:3 * gr + 3, :], PS[:, 2 * gr, 0:384].rearrange("p (h n) -> p h n", n=128),
                                m.unsqueeze(1).to_broadcast([128, 3, 128]), ALU.mult), [t, t_Zr[gr]])
                            free[2 * gr] = t_Z[gr]
                        yield
                        for gr in range(2):
                            for j in range(3):
                                h = 3 * gr + j
                                t = mm(cols(PS[:, 2 * gr + 1, :], j), R[:, h, :], Z[:, h, :], True, True,
                                       [t_Z[gr], t_R[gr], free[2 * gr + 1]], sig=(j == 2))
                            for j in range(3):
                                h = 3 * gr + j
                                t2 = mm(cols(PS[:, 2 * gr, :], j), Z[:, h, :], R[:, h, :], True, True, [free[2 * gr]], sig=(j == 2))
                            t_Zr[gr] = t2
                            t_T[gr] = act(lambda e, gr=gr: e.activation(grp(Tm, gr), PS[:, 2 * gr + 1, 0:384], ACT.Copy), [t])
                            free[2 * gr + 1] = t_T[gr]
                            t_R[gr] = act(lambda e, gr=gr: e.activation(grp(R, gr), PS[:, 2 * gr, 0:384], ACT.Copy), [t2])
                            free[2 * gr] = t_R[gr]
                        yield
                    t_Rf = []
                    for gr in range(2):
                        for j in range(3):
                            h = 3 * gr + j
                            t = mm(cols(PS[:, 2 * gr + 1, :], j), NTm[:, h, :], Tm[:, h, :].bitcast(F32), True, True,
                                   [t_T[gr], t_N[gr], free[2 * gr + 1]], sig=(j == 2))
                        rel[("Tm", gr)] = rel["NTm"] = t
                        t_Z[gr] = dve(lambda e, gr=gr: e.tensor_tensor(
                            Z[:, 3 * gr:3 * gr + 3, :], ident.unsqueeze(1).to_broadcast([128, 3, 128]),
                            PS[:, 2 * gr + 1, 0:384].rearrange("p (h n) -> p h n", n=128), ALU.add), [t, t_Zr[gr]])
                        free[2 * gr + 1] = t_Z[gr]
                    yield
                    for gr in range(2):
                        for j in range(3):
                            h = 3 * gr + j
                            t = mm(cols(PS[:, 2 * gr, :], j), Z[:, h, :], R[:, h, :], True, True, [t_Z[gr], t_R[gr], free[2 * gr]], sig=(j == 2))
                        rel[("Z", gr)] = t
                        t1 = dve(lambda e, gr=gr: e.tensor_tensor(
                            grp(Rf[:, s2, :, :], gr), PS[:, 2 * gr, 0:384], grp(R, gr).bitcast(F32), ALU.add), [t, rel.get(("Rf", s2))])
                        free[2 * gr] = t1
                        rel[("R", gr)] = t1
                        t_Rf.append(t1)
                    done[("s", ch)] = dict(Rf=t_Rf, P=t_P, kd=t_kd, khT=t_khT, V=t_V)
                    yield

                def output(ch):
                    B, cl, s2 = ch // 2, ch % 2, ch % 2
                    x3, q3 = B % 3, B % 3
                    cs = slice(cl * 128, cl * 128 + 128)
                    ok = done[B]
                    iv = done[("s", ch)]
                    Xv = Y = V[:, s2, :, :]
                    So, Sn = S[:, ch % 2, :, :], S[:, (ch + 1) % 2, :, :]
                    two = PS[:, 4:6, 0:384]
                    t_So = t_S[0]
                    for j in range(3):
                        for gr in range(2):
                            p0 = 64 * gr
                            t = mm(cols(PS[:, 4 + gr, :], j), khT[p0:p0 + 64, s2, j, :], So[p0:p0 + 64, j, :], True, True,
                                   [free[4 + gr], iv["khT"], t_So], sig=(j == 2))
                    rel[("khT", s2)] = t
                    for h in range(H):
                        t1 = dve(lambda e, h=h: e.scalar_tensor_tensor(
                            Xv[:, h, :], cols(PS[:, 4 + h // 3, :], h % 3), neG[:, ch, h:h + 1], V[:, s2, h, :], ALU.mult, ALU.add),
                            [t, ok["neG"], iv["V"]])
                        if h == 2:
                            free[4] = t1
                    free[5] = t1
                    yield
                    t_Y = []
                    for gr in range(2):
                        for j in range(3):
                            h = 3 * gr + j
                            t = mm(cols(PS[:, 4 + gr, :], j), Rf[:, s2, h, :], Xv[:, h, :], True, True,
                                   [free[4 + gr], t1, iv["Rf"]], sig=(j == 2))
                        t_Y.append(act(lambda e, gr=gr: e.activation(grp(Y, gr), PS[:, 4 + gr, 0:384], ACT.Copy), [t]))
                        free[4 + gr] = t_Y[gr]
                    rel[("Rf", s2)] = t
                    yield
                    for gr in range(2):
                        p0 = 64 * gr
                        for j in range(3):
                            t = mm(PS[p0:p0 + 64, 4, j * 128:(j + 1) * 128], kd[:, s2, j, gr, :], Y[:, 3 * gr + j, :], True, True,
                                   [t_Y[gr], iv["kd"], free[4]], sig=(gr == 1 and j == 2))
                    rel[("kd", s2)] = t
                    for j in range(3):
                        t1 = dve(lambda e, j=j: e.scalar_tensor_tensor(
                            Sn[:, j, :], So[:, j, :], eC[:, ch, j:j + 1], PS[:, 4, j * 128:(j + 1) * 128], ALU.mult, ALU.add),
                            [t, ok["eC"], rel.get(("S", (ch + 1) % 2))])
                    t_S[0] = t1
                    free[4] = t1
                    yield
                    for j in range(3):
                        for gr in range(2):
                            p0 = 64 * gr
                            t = mm(cols(PS[:, 4 + gr, :], j), qb[p0:p0 + 64, q3, j, cs], So[p0:p0 + 64, j, :], True, True,
                                   [free[4 + gr]], sig=(j == 2))
                    rel[("S", ch % 2)] = [t, t1]
                    rel[("qb", q3)] = t
                    t_o = []
                    for gr in range(2):
                        t1 = dve(lambda e, gr=gr: e.tensor_tensor(
                            o[:, 3 * gr:3 * gr + 3, :], PS[:, 4 + gr, 0:384].rearrange("p (h n) -> p h n", n=128),
                            eG[:, ch, 3 * gr:3 * gr + 3].unsqueeze(2).to_broadcast([128, 3, 128]), ALU.mult), [t, ok["eG"], rel.get("o")])
                        t_o.append(t1)
                        free[4 + gr] = t1
                    yield
                    for gr in range(2):
                        for j in range(3):
                            h = 3 * gr + j
                            t = mm(cols(PS[:, 4 + gr, :], j), P[:, s2, h, :], Y[:, h, :], True, True, [free[4 + gr], iv["P"]], sig=(j == 2))
                        t_o[gr] = dve(lambda e, gr=gr: e.tensor_tensor(grp(o, gr), grp(o, gr), PS[:, 4 + gr, 0:384], ALU.subtract), [t, t_o[gr]])
                        free[4 + gr] = t_o[gr]
                    rel[("P", s2)] = rel[("V", s2)] = t
                    yield
                    t_g = []
                    for gr in range(2):
                        for k in range(4):
                            t = mm(PS[:, 4 + gr, 0:384], XB[:, x3, k, cs], W[:, k, 1536 + 384 * gr:1920 + 384 * gr], k == 0, k == 3,
                                   [free[4 + gr], t_w[2]], sig=(k == 3))
                        t1 = act(lambda e, gr=gr: e.activation(grp(gs, gr), PS[:, 4 + gr, 0:384], ACT.Tanh, scale=0.5), [t, rel.get("gs")])
                        t1 = dve(lambda e, gr=gr: e.scalar_tensor_tensor(grp(gs, gr), grp(gs, gr), 1.0, PS[:, 4 + gr, 0:384], ALU.add, ALU.mult), [t1])
                        t_g.append(t1)
                        free[4 + gr] = t1
                        yield
                    rel[("XB", x3)] = t
                    t1 = dve(lambda e: e.tensor_tensor(
                        o[:, :, :], o[:, :, :], rn[:, ch, 0:6].unsqueeze(2).to_broadcast([128, H, 128]), ALU.mult), [t_o])
                    t1 = dve(lambda e: e.scalar_tensor_tensor(
                        o[:, :, :], o[:, :, :], 0.125, gs[:, :, :], ALU.mult, ALU.mult), [t1, t_g])
                    t2 = act(lambda e: e.activation(gs[:, :, :], o[:, :, :], ACT.Square), [t1])
                    t2 = dve(lambda e: e.tensor_reduce(ms[:, :], gs[:, :, :], AX.X, ALU.add), [t2])
                    t2 = dve(lambda e: e.tensor_scalar(ms[:, :], ms[:, :], 1.0 / 128, 4e-5, ALU.mult, ALU.add), [t2])
                    t2 = pool(lambda e: e.tensor_tensor(ms[:, :], ms[:, :], pw[:, 0:6], ALU.pow), [t2])
                    t1 = dve(lambda e: e.tensor_tensor(
                        o[:, :, :], o[:, :, :], ms[:, :].unsqueeze(2).to_broadcast([128, H, 128]), ALU.mult), [t1, t2])
                    yield
                    t3 = []
                    for gr in range(2):
                        for j in range(3):
                            t = tr(cols(PS[:, 4 + gr, :], j), o[:, 3 * gr + j, :], [t1, free[4 + gr]], sig=(j == 2))
                        t3.append(act(lambda e, gr=gr: e.activation(grp(gs, gr), PS[:, 4 + gr, 0:384], ACT.Copy), [t]))
                        free[4 + gr] = t3[gr]
                    rel["o"] = t
                    yield
                    for h in range(H):
                        t = mm(PS[:, 4, :], gs[:, h, :], WO[:, h, :], h == 0, h == 5, [t3[h // 3], t_wo, free[4]], sig=(h == 5))
                        if h == 2:
                            yield
                    rel["gs"] = t
                    t1 = dve(lambda e: e.tensor_tensor(X[:, ch, :], X[:, ch, :], PS[:, 4, :], ALU.add), [t])
                    free[4] = t1
                    t_x_out[ch] = moments(ch, t1)
                    yield

                t_x_out = [None] * NT

                def half(gen, n):
                    for _ in range(n):
                        if next(gen, 0) == 0:
                            return
                        yield

                NP = 17
                merge([(proj(0), 17), (tables(), 13)])
                pj = {}
                for ch in range(-1, NT):
                    B = (ch + 3) // 2
                    th_ = []
                    if B not in pj and B < NB:
                        pj[B] = proj(B)
                    if B < NB:
                        first = ch % 2 == 1
                        th_.append((half(pj[B], 8) if first else pj[B], 8 if first else NP - 8))
                    if ch + 1 < NT:
                        th_.append((solve(ch + 1), 18))
                    if ch >= 0:
                        th_.append((output(ch), 13))
                    merge(th_)
                barrier()
            return t_x_out

        def mixtures(t_in):
            c = ctx.enter_context(ExitStack())

            def s1(name, shape, dt=F32, c=c):
                return sb(name, shape, dt, c)
            NW, NBF, NOB, NGB = 3, 4, 3, 8
            XN = s1("XN", [128, NT, D])
            XNT = s1("XNT", [128, 4, T])
            GW = s1("GW", [128, 4, E])
            GB = s1("GB", [128, E])
            SW = s1("SW", [128, 3, 4, D])
            W13 = s1("W13", [128, NW, 4, 512])
            W2 = s1("W2", [128, NW, 2, 512])
            shT = s1("shT", [128, 4, 512])
            sth = s1("sth", [128, 2, 512])
            wk = s1("wk", [128, NT, 4])
            offs = s1("offs", [128, 4, NT], U32)
            Lm = [line(f"d_m{n}", 16) for n in range(5)]
            Lw = [line(f"d_ew{i}", 16) for i in range(NW)]
            Lb = [line(f"d_eb{i}", 16) for i in range(NBF)]
            Lo = [line(f"d_eo{i}", 16) for i in range(NOB)]
            Lg = [line(f"d_eg{i}", 16) for i in range(NGB)]
            Ls = line("d_es", 16)
            w13v = a["w13"].rearrange("e (c p) n -> e p c n", p=128)
            w2v = a["w2"].rearrange("e (c p) n -> e p c n", p=128)
            t_ew = {}

            def load_w(y, t_free):
                s, x = y % NW, y % E
                dma(lambda e: e.dma_start(W13[:, s, :, :], w13v[x]), Lw[s], t_free)
                t_ew[y] = dma(lambda e: e.dma_start(W2[:, s, :, :], w2v[x]), Lw[s])

            t_gw = dma(lambda e: e.dma_start(GW[:, :, :], a["gw"].rearrange("(c p) n -> p c n", p=128)), Lm[0])
            t_gb = dma(lambda e: e.dma_start(GB[:, :], a["gb"]), Lm[1])
            t_sw = []
            for j, n in enumerate(("sg", "su", "sd")):
                t_sw.append(dma(lambda e, j=j, n=n: e.dma_start(SW[:, j, :, :], a[n].rearrange("(c p) n -> p c n", p=128)), Lm[2 + j]))
            for y in range(NW):
                load_w(y, None)

            t_buf, t_gath = [None], [[None] * NGB]
            t_sth, t_shT = [None, None], [None]
            t_used = {"xn": [None] * NT, "xnt": None}
            total = (1 if stage < 4 else 2) * E

            def moe(m, t_x0, tail):
                t_xn, t_xt, t_xs = [None] * NT, [None] * NT, [None] * NT

                def shared(nb4, pairs, downs):
                    while t_xt[4 * nb4 + 3] is None:
                        yield
                    for f in range(4):
                        u = f % len(pairs)
                        b0, b1 = pairs[u]
                        for j, b in ((0, b0), (1, b1)):
                            for k in range(4):
                                t = mm(PS[:, b, :], SW[:, j, k, f * 128:(f + 1) * 128], XNT[:, k, nb4 * 512:(nb4 + 1) * 512],
                                       k == 0, k == 3, [t_sw[j], free[b], t_xt[4 * nb4:4 * nb4 + 4]], sig=(k == 3))
                                if k == 1:
                                    yield
                            yield
                        if f == 3 and nb4 == 3:
                            t_used["xnt"] = t
                        t1 = act(lambda e, u=u, b0=b0: e.activation(sth[:, u, :], PS[:, b0, :], ACT.Tanh, scale=0.5), [t, t_sth[u]])
                        t1 = dve(lambda e, u=u, b0=b0: e.scalar_tensor_tensor(sth[:, u, :], sth[:, u, :], 1.0, PS[:, b0, :], ALU.add, ALU.mult), [t1])
                        t_h = dve(lambda e, u=u, f=f, b1=b1: e.tensor_tensor(shT[:, f, :], sth[:, u, :], PS[:, b1, :], ALU.mult), [t1, t_shT[0]])
                        t_sth[u] = t_h
                        free[b0] = free[b1] = t_h
                        yield
                    for tl in range(4):
                        i = nb4 * 4 + tl
                        b = downs[tl % len(downs)]
                        for f in range(4):
                            t = mm(PS[:, b, :], shT[:, f, tl * 128:(tl + 1) * 128], SW[:, 2, f, :], f == 0, f == 3, [t_h, t_sw[2], free[b]], sig=(f == 3))
                            if f == 1:
                                yield
                        t_xs[i] = dve(lambda e, i=i, b=b: e.scalar_tensor_tensor(X[:, i, :], PS[:, b, :], 0.5, X[:, i, :], ALU.mult, ALU.add), [t, t_xn[i]])
                        free[b] = t_xs[i]
                        yield
                    t_shT[0] = t

                def norm_tiles(nb4):
                    ii = slice(4 * nb4, 4 * nb4 + 4)
                    t_r = inverse_std(ii, t_x0[ii])
                    for i in range(4 * nb4, 4 * nb4 + 4):
                        t_xn[i] = normalise(i, XN[:, i, :], [t_r, t_used["xn"][i]])
                        t_xt[i] = transpose_tile(XN[:, i, :], XNT[:, :, i * 128:(i + 1) * 128], i % 2, t_xn[i], t_used["xnt"])[1]
                        for k in range(4):
                            t = mm(PS[:, 2, i * E:(i + 1) * E], XNT[:, k, i * 128:(i + 1) * 128], GW[:, k, :], k == 0, k == 3,
                                   [t_xt[i], t_gw, free[2]], sig=(k == 3))
                        t_lg[i] = t
                        yield
                t_lg = [None] * NT
                route = {}

                def gate(c):
                    def sg(name, shape, dt=F32):
                        return s1(f"{name}_{m}", shape, dt, c)
                    sc = sg("sc", [128, NT, E])
                    sb_ = sg("sbias", [128, NT, E])
                    oh = sg("oh", [128, 4, NT, E])
                    m8 = sg("m8", [128, NT, 4, 8])
                    gsum = sg("gsum", [128, NT, 4])
                    cmp = sg("cmp", [128, NT, 4, 4])
                    cm2 = sg("cm2", [128, NT, 4, 4])
                    cnt = sg("cnt", [128, NT, 4])
                    v8 = sg("v8", [128, NT, 8])
                    i8 = sg("i8", [128, NT, 8], U32)
                    i8f = sg("i8f", [128, NT, 8])
                    ws = sg("ws", [128, NT])
                    msk = sg("msk", [128, NT, E])
                    cum = sg("cum", [128, NT, E])
                    tmp = sg("gtmp", [128, 2, NT, E])
                    pk = sg("pk", [128, 4, NT])
                    kp = sg("kp", [128, 4, NT])
                    for nb4 in range(1, 4):
                        yield from norm_tiles(nb4)
                    lg = PS[:, 2, :].rearrange("p (i n) -> p i n", n=E)
                    t1 = act(lambda e: e.activation(sc[:, :, :], lg, ACT.Exp, scale=-1.0), [t_lg[NT - 1]])
                    free[2] = t1
                    t1 = dve(lambda e: e.tensor_scalar(sc[:, :, :], sc[:, :, :], 1.0, None, ALU.add), [t1])
                    t_sc = dve(lambda e: e.reciprocal(sc[:, :, :], sc[:, :, :]), [t1])
                    t1 = dve(lambda e: e.tensor_tensor(sb_[:, :, :], sc[:, :, :], GB[:, :].unsqueeze(1).to_broadcast([128, NT, E]), ALU.add), [t_sc, t_gb])
                    yield
                    for i in range(NT):
                        for gi in range(4):
                            t2 = dve(lambda e, i=i, gi=gi: e.max(m8[:, i, gi, :], sb_[:, i, gi * 8:(gi + 1) * 8]), [t1])
                        if i % 4 == 3:
                            yield
                    t2 = dve(lambda e: e.tensor_tensor(gsum[:, :, :], m8[:, :, :, 0], m8[:, :, :, 1], ALU.add), [t2])
                    gi_ = gsum[:, :, :].unsqueeze(3).to_broadcast([128, NT, 4, 4])
                    gj_ = gsum[:, :, :].unsqueeze(2).to_broadcast([128, NT, 4, 4])
                    cu = CON[:, C_U:C_U + 16].rearrange("p (i j) -> p i j", j=4).unsqueeze(1).to_broadcast([128, NT, 4, 4])
                    cl_ = CON[:, C_L:C_L + 16].rearrange("p (i j) -> p i j", j=4).unsqueeze(1).to_broadcast([128, NT, 4, 4])
                    t3 = dve(lambda e: e.tensor_tensor(cmp[:, :, :, :], gi_, gj_, ALU.is_ge), [t2])
                    t4 = dve(lambda e: e.tensor_tensor(cm2[:, :, :, :], gi_, gj_, ALU.is_gt), [t2])
                    t3 = dve(lambda e: e.tensor_tensor(cmp[:, :, :, :], cmp[:, :, :, :], cu, ALU.mult), [t3])
                    t4 = dve(lambda e: e.tensor_tensor(cm2[:, :, :, :], cm2[:, :, :, :], cl_, ALU.mult), [t4])
                    t3 = dve(lambda e: e.tensor_tensor(cmp[:, :, :, :], cmp[:, :, :, :], cm2[:, :, :, :], ALU.add), [t3, t4])
                    t3 = dve(lambda e: e.tensor_reduce(cnt[:, :, :], cmp[:, :, :, :], AX.X, ALU.add), [t3])
                    t3 = dve(lambda e: e.tensor_scalar(cnt[:, :, :], cnt[:, :, :], 2.0, None, ALU.is_ge), [t3])
                    t3 = dve(lambda e: e.tensor_tensor(
                        sb_[:, :, :].rearrange("p i (g n) -> p i g n", g=4), sb_[:, :, :].rearrange("p i (g n) -> p i g n", g=4),
                        cnt[:, :, :].unsqueeze(3).to_broadcast([128, NT, 4, 8]), ALU.mult), [t3])
                    yield
                    for i in range(NT):
                        t4 = dve(lambda e, i=i: e.max(v8[:, i, :], sb_[:, i, :]), [t3])
                    yield
                    for i in range(NT):
                        t4 = dve(lambda e, i=i: e.max_index(i8[:, i, :], v8[:, i, :], sb_[:, i, :]), [t4])
                    yield
                    t4 = dve(lambda e: e.tensor_copy(i8f[:, :, :], i8[:, :, :]), [t4])
                    io = CON[:, C_IOTA:C_IOTA + 32].unsqueeze(1).to_broadcast([128, NT, E])
                    t5 = []
                    for k in range(4):
                        t5.append(dve(lambda e, k=k: e.tensor_tensor(
                            oh[:, k, :, :], io, i8f[:, :, k:k + 1].to_broadcast([128, NT, E]), ALU.is_equal), [t4]))
                    yield
                    t6 = dve(lambda e: e.tensor_tensor(msk[:, :, :], oh[:, 0, :, :], oh[:, 1, :, :], ALU.add), [t5])
                    t6 = dve(lambda e: e.tensor_tensor(msk[:, :, :], msk[:, :, :], oh[:, 2, :, :], ALU.add), [t6])
                    t_mk = dve(lambda e: e.tensor_tensor(msk[:, :, :], msk[:, :, :], oh[:, 3, :, :], ALU.add), [t6])
                    t6 = dve(lambda e: e.memset(cum[:, 0, :], 0.0))
                    for i in range(1, NT):
                        t6 = dve(lambda e, i=i: e.tensor_tensor(cum[:, i, :], cum[:, i - 1, :], msk[:, i - 1, :], ALU.add), [t6, t_mk])
                    mm(PS[:, 3, :], stri, msk[:, :, :].rearrange("p i n -> p (i n)"), True, False, [t_mk, free[3]])
                    t_ps = mm(PS[:, 3, :], ones[:, :], cum[:, :, :].rearrange("p i n -> p (i n)"), False, True, [t6], sig=True)
                    yield
                    pos = PS[:, 3, :].rearrange("p (i n) -> p i n", n=E)
                    t9 = [None, None]
                    for k in range(4):
                        t = dve(lambda e, k=k: e.tensor_tensor(tmp[:, k % 2, :, :], oh[:, k, :, :], pos, ALU.mult), [t_ps, t9[k % 2]])
                        t9[k % 2] = dve(lambda e, k=k: e.tensor_reduce(pk[:, k, :], tmp[:, k % 2, :, :], AX.X, ALU.add), [t])
                    free[3] = t
                    t10 = dve(lambda e: e.tensor_scalar(kp[:, :, :], pk[:, :, :], float(CAP), None, ALU.is_lt), [t9])
                    t = dve(lambda e: e.scalar_tensor_tensor(
                        pk[:, :, :], i8f[:, :, 0:4].rearrange("p i k -> p k i"), float(CAP), pk[:, :, :], ALU.mult, ALU.add), [t10])
                    t = dve(lambda e: e.scalar_tensor_tensor(pk[:, :, :], pk[:, :, :], float(-E * CAP), kp[:, :, :], ALU.add, ALU.mult), [t])
                    t_of = dve(lambda e: e.tensor_scalar(offs[:, :, :], pk[:, :, :], float(E * CAP), None, ALU.add), [t, t_gath[0]])
                    yield
                    for i in range(NT):
                        for k in range(4):
                            route["sc"] = dma(lambda e, i=i, k=k: e.indirect_dma_start(
                                out=buf, out_offset=bass.IndirectOffsetOnAxis(ap=offs[:, k, i:i + 1], axis=0),
                                in_=XN[:, i, :], in_offset=None, bounds_check=E * CAP - 1, oob_is_err=False),
                                Ls, [t_of, t_xn[i], (L_z, L_z.n), t_buf[0]], "gpsimd")
                    t8 = [t9[0], t9[1]]
                    for k in range(4):
                        t = dve(lambda e, k=k: e.tensor_tensor(tmp[:, k % 2, :, :], oh[:, k, :, :], sc[:, :, :], ALU.mult), [t8[k % 2]])
                        t8[k % 2] = dve(lambda e, k=k: e.tensor_reduce(wk[:, :, k], tmp[:, k % 2, :, :], AX.X, ALU.add), [t])
                    t = dve(lambda e: e.tensor_reduce(ws[:, :], wk[:, :, :], AX.X, ALU.add), [t8])
                    t = dve(lambda e: e.tensor_scalar(ws[:, :], ws[:, :], 1e-20, None, ALU.add), [t])
                    t = dve(lambda e: e.reciprocal(ws[:, :], ws[:, :]), [t])
                    route["wk"] = dve(lambda e: e.tensor_tensor(wk[:, :, :], wk[:, :, :], ws[:, :].unsqueeze(2).to_broadcast([128, NT, 4]), ALU.mult), [t])
                    yield

                def experts(c):
                    Bf = s1(f"Bf_{m}", [128, NBF, D], F32, c)
                    BT = s1(f"BT_{m}", [128, 2, 4, 128], F32, c)
                    eth = s1(f"eth_{m}", [128, 2, 256], F32, c)
                    hT = s1(f"hT_{m}", [128, 2, 2, 128], F32, c)
                    OB = s1(f"OB_{m}", [128, NOB, D], F32, c)
                    t_b, t_tr, t_bt, t_w13, t_h, t_w2, t_st = {}, {}, {}, {}, {}, {}, {}

                    def load(x):
                        s = x % NBF
                        t_b[x] = dma(lambda e: e.dma_start(Bf[:, s, :], buf[x * CAP:(x + 1) * CAP, :]), Lb[s], [route["sc"], t_tr.get(x - NBF)])

                    def turn(x):
                        s, b, u = x % NBF, x % 2, x % 2
                        t_tr[x], t_bt[x] = transpose_tile(Bf[:, s, :], BT[:, u, :, :], b, t_b[x], t_w13.get(x - 2))

                    def hidden(x):
                        u, b, w = x % 2, 2 + x % 2, (m * E + x) % NW
                        for f in range(4):
                            for k in range(4):
                                t = mm(PS[:, b, f * 128:(f + 1) * 128], W13[:, w, k, f * 128:(f + 1) * 128], BT[:, u, k, :], k == 0, k == 3,
                                       [t_bt[x], t_ew[m * E + x], free[b]], sig=(f == 3 and k == 3))
                        t_w13[x] = t
                        t1 = act(lambda e: e.activation(eth[:, u, :], PS[:, b, 0:256], ACT.Tanh, scale=0.5), [t, t_h.get(x - 2)])
                        t1 = dve(lambda e: e.scalar_tensor_tensor(eth[:, u, :], eth[:, u, :], 1.0, PS[:, b, 0:256], ALU.add, ALU.mult), [t1])
                        t_h[x] = dve(lambda e: e.tensor_tensor(
                            hT[:, u, :, :].rearrange("p k n -> p (k n)"), eth[:, u, :], PS[:, b, 256:512], ALU.mult), [t1, t_w2.get(x - 2)])
                        free[b] = t_h[x]

                    def down(x):
                        u, b, w, s = x % 2, 4 + x % 2, (m * E + x) % NW, x % NOB
                        for k in range(2):
                            t = mm(PS[:, b, :], hT[:, u, k, :], W2[:, w, k, :], k == 0, k == 1, [t_h[x], free[b]], sig=(k == 1))
                        t_w2[x] = t
                        if m * E + x + NW < total:
                            load_w(m * E + x + NW, t)
                        t1 = act(lambda e: e.activation(OB[:, s, :], PS[:, b, :], ACT.Copy), [t, t_st.get(x - NOB)])
                        free[b] = t1
                        t_st[x] = dma(lambda e: e.dma_start(obd[x * CAP:(x + 1) * CAP, :], OB[:, s, :]), Lo[s], [t1, t_gath[0]], "scalar")

                    for x in range(NBF):
                        load(x)
                    for x in range(-2, E):
                        if x + 2 < E:
                            turn(x + 2)
                            if x + 2 + NBF < E:
                                load(x + 2 + NBF)
                        if 0 <= x + 1 < E:
                            hidden(x + 1)
                        yield
                        if x >= 0:
                            down(x)
                            yield
                    route["ob"] = [t_st[E - 1 - j] for j in range(NOB)]
                    t_buf[0] = [t_b[E - 1 - j] for j in range(NBF)]

                t_xo = [None] * NT

                def gather():
                    t_gf = [None] * NGB
                    for i in range(NT):
                        tt = t_xs[i]
                        for k in range(4):
                            s = (i * 4 + k) % NGB
                            gt = XN[:, s, :]
                            t = dma(lambda e, i=i, k=k, gt=gt: e.indirect_dma_start(
                                out=gt, out_offset=None, in_=obd,
                                in_offset=bass.IndirectOffsetOnAxis(ap=offs[:, k, i:i + 1], axis=0)),
                                Lg[s], [route["ob"], t_gf[s], (L_z, L_z.n)], "gpsimd")
                            tt = dve(lambda e, i=i, k=k, gt=gt: e.scalar_tensor_tensor(
                                X[:, i, :], gt, wk[:, i, k:k + 1], X[:, i, :], ALU.mult, ALU.add), [t, tt, route["wk"]])
                            t_gf[s] = tt
                        t_xo[i] = tt
                        yield
                    for s in range(NGB):
                        t_used["xn"][s] = t_gf[s]
                    t_gath[0] = t_gf

                for _ in norm_tiles(0):
                    pass
                with ExitStack() as c1:
                    pairs, downs = ((4, 5), (6, 7)), (0, 1)

                    def chain():
                        for nb4 in range(3):
                            yield from shared(nb4, pairs, downs)
                    merge([(gate(c1), 27), (chain(), 160)])
                fence([route["wk"], free[2]])
                with ExitStack() as c1:
                    merge([(experts(c1), 66), (shared(3, ((6, 7),), (6, 7)), 32)])
                fence([route["ob"], free])
                tail(gather(), t_xo)

            def lru(c, t_xi, t_o):
                xr = XNT[:, 0:2, :].rearrange("p s (k n) -> p s k n", k=4)
                Ct, St = XNT[:, 2, :], XNT[:, 3, :]
                BW = s1("BW", [128, 2, 4, 128], F32, c)
                CWt = s1("CWt", [128, 2, 512], F32, c)
                DB = s1("DB", [128, D], F32, c)
                bu = s1("bu", [128, 2, 512], F32, c)
                r = s1("r", [128, 512], F32, c)
                g = s1("gst", [128, 2, 512], F32, c)
                pr = s1("pr", [128, 2, 512], F32, c)
                LL = [line(f"d_l{i}", 16) for i in range(4)]

                def col(j):
                    return LS[:, j:j + 1]
                t_bw = [dma(lambda e, j=j: e.dma_start(BW[:, j, :, :], a[("bt", "btsw")[j]].rearrange("(c p) n -> p c n", p=128)), LL[0]) for j in range(2)][1]
                t_cw = [dma(lambda e, j=j: e.dma_start(CWt[:, j, :], a[("ct", "ctsw")[j]]), LL[1]) for j in range(2)][1]
                t_db = dma(lambda e: e.dma_start(DB[:, :], a["dvec"]), LL[2])
                t_tb = [(ln, ln.n) for ln in L_tb]
                t_rot = [dma(lambda e, j=j: e.dma_start(XNT[:, 2 + j, :], tabs[j]), LL[3], [t_tb, t_used["xnt"]]) for j in range(2)][1]
                t_cw = dve(lambda e: e.tensor_scalar(CWt[:, 0, :], CWt[:, 0, :], CON[:, C_SGN:C_SGN + 1], None, ALU.mult), [t_cw])
                t_cw = dve(lambda e: e.tensor_scalar(CWt[:, 1, :], CWt[:, 1, :], -1.0, None, ALU.mult), [t_cw])
                yield
                t_bu, t_g, t_pr, t_xr = [None, None], None, None, [None, None]
                t_sl = [None] * 8
                for n in range(4):
                    ns = slice(n * 512, n * 512 + 512)
                    u = n % 2
                    t_xn, t_xt = {}, {}
                    for i in range(4 * n, 4 * n + 4):
                        while t_xi[i] is None:
                            yield
                        s = 8 + i % 8
                        t = inverse_std(slice(i, i + 1), moments(i, t_xi[i]))
                        t_xn[i] = normalise(i, XN[:, s, :], [t, t_sl[i % 8]])
                        t_xt[i] = transpose_tile(XN[:, s, :], xr[:, u, :, (i % 4) * 128:(i % 4) * 128 + 128], i % 2, t_xn[i], [t_used["xnt"], t_xr[u]])
                        t_xn[i] = dve(lambda e, s=s: e.tensor_tensor(XN[:, s, :], XN[:, s, :], DB[:, :], ALU.mult), [t_xt[i][0], t_db])
                        t_xn[i] = dve(lambda e, i=i, s=s: e.tensor_tensor(X[:, i, :], X[:, i, :], XN[:, s, :], ALU.add), [t_xn[i]])
                        t_sl[i % 8] = t_xn[i]
                        yield
                    t_r = []
                    for j in range(2):
                        b = 4 + j
                        for k in range(4):
                            t = mm(PS[:, b, :], BW[:, j, k, :], xr[:, u, k, :], k == 0, k == 3,
                                   [t_bw, [x[1] for x in t_xt.values()], free[b]], sig=(k == 3))
                        t_xr[u] = t
                        t = act(lambda e, j=j, b=b: e.activation(bu[:, j, :], PS[:, b, :], ACT.Copy, scale=col(3 + j)), [t, t_bu[j]])
                        free[b] = t
                        tab = (Ct, St)[j]
                        t_r.append(dve(lambda e, j=j, tab=tab, ns=ns: e.tensor_tensor(bu[:, j, :], bu[:, j, :], tab[:, ns], ALU.mult), [t, t_rot]))
                        yield
                    t = dve(lambda e: e.tensor_tensor(r[:, :], bu[:, 0, :], bu[:, 1, :], ALU.add), [t_r, t_g])
                    t_bu = [t, t]
                    init = 0.0 if n == 0 else g[:, 1 - u, 511:512]
                    t_g = dve(lambda e, u=u, init=init: e.tensor_tensor_scan(
                        g[:, u, :], col(2).to_broadcast([128, 512]), r[:, :], init, ALU.mult, ALU.add), [t, t_g])
                    for j, tab in ((0, Ct), (1, St)):
                        t1 = dve(lambda e, j=j, tab=tab, ns=ns, u=u: e.tensor_tensor(pr[:, j, :], g[:, u, :], tab[:, ns], ALU.mult), [t_g, t_pr])
                    yield
                    for i in range(4 * n, 4 * n + 4):
                        b = 6 + i % 2
                        lt = slice((i % 4) * 128, (i % 4) * 128 + 128)
                        mm(PS[:, b, :], pr[:, 0, lt], CWt[:, 0, :], True, False, [t1, t_cw, free[b]])
                        t = mm(PS[:, b, :], pr[:, 1, lt], CWt[:, 1, :], False, True, sig=True)
                        t4 = dve(lambda e, i=i, b=b: e.tensor_tensor(X[:, i, :], X[:, i, :], PS[:, b, :], ALU.add), [t, t_xn[i]])
                        free[b] = t4
                        t_o[i] = moments(i, t4)
                        yield
                    t_pr = t
                t_used["xnt"] = [t_xr, t1]
                for s in range(8):
                    t_used["xn"][8 + s] = t_sl[s]

            def tail1(gen, t_xo):
                if stage < 3:
                    return merge([(gen, 1)])
                with ExitStack() as c2_:
                    merge([(gen, NT), (lru(c2_, t_xo, t_mid), 45)])
                fence([t_mid, t_used["xnt"]])

            def tail2(gen, t_xo):
                for i, _ in enumerate(gen):
                    if i % 4 == 3:
                        dma(lambda e, i=i: e.dma_start(ov[:, i - 3:i + 1, :], X[:, i - 3:i + 1, :]), L_out[i // 4], [t_xo[i]])

            t_mid = [None] * NT
            moe(0, t_in, tail1)
            if stage >= 4:
                moe(1, t_mid, tail2)

        L_out = [line(f"d_out{i}", 16) for i in range(4)]
        ov = out.rearrange("b (i p) n -> p (b i) n", p=128)
        t_o = delta_net()
        if stage >= 2:
            mixtures(t_o)
        if stage < 4:
            barrier()
            dma(lambda e: e.dma_start(ov, X[:, :, :]), L_out[0])
        q["sync"].append(([(ln, ln.n) for ln in lines], None, None))

        block = ctx.enter_context(nc.Block())

        def run(eng, name):
            seen = {}
            for waits, fn, on in q[name]:
                need = {}
                for ln, v in waits:
                    if v > seen.get(ln, 0):
                        need[ln] = max(v, need.get(ln, 0))
                for ln, v in need.items():
                    eng.wait_ge(ln.sem, v)
                    seen[ln] = v
                if fn is not None:
                    ins = fn(eng)
                    if on is not None:
                        ins.then_inc(on.sem, on.by)

        @block.sync
        def _(eng):
            run(eng, "sync")

        @block.scalar
        def _(eng):
            run(eng, "scalar")

        @block.vector
        def _(eng):
            run(eng, "vector")

        @block.tensor
        def _(eng):
            run(eng, "tensor")

        @block.gpsimd
        def _(eng):
            run(eng, "gpsimd")


def layout(i):
    import numpy as _np
    f = lambda n: _np.asarray(i["L0_" + n])
    cat = _np.concatenate
    rows = lambda v: _np.broadcast_to(v, (128,) + v.shape)
    small = _np.zeros((128, 16), _np.float32)
    order = [0, 2, 4, 1, 3, 5]
    heads = lambda v: v.reshape((H, -1) + v.shape[1:])[order].reshape(v.shape)
    small[:, 0:6] = heads(f("attn_a_dt_bias"))
    small[:, 6:12] = heads(f("attn_a_A_log"))
    small[:, 12] = f("attn_a_norm_w")
    br, bi, cr, ci = (f("attn_b_" + n).T for n in ("B_re", "B_im", "C_re", "C_im"))
    lsm = _np.stack([cat([f("attn_b_nu_log")] * 2), cat([f("attn_b_theta_log")] * 2)], 1)
    d = {
        "x": f("attn_a_x"), "consts": shape_constants(), "small": small, "lsm": lsm,
        "wqkvg": cat([f("attn_a_Wq"), f("attn_a_Wk"), heads(f("attn_a_Wv")), heads(f("attn_a_Wg"))]).T,
        "wab": cat([heads(f("attn_a_Wa")), heads(f("attn_a_Wb"))]).T, "wo": heads(f("attn_a_Wo").T),
        "convw": cat([f("attn_a_conv_q_w"), f("attn_a_conv_k_w"), heads(f("attn_a_conv_v_w"))])[:, 0, :],
        "bt": cat([br, bi], 1), "btsw": cat([bi, br], 1), "ct": cat([cr, ci]), "ctsw": cat([ci, cr]),
        "tidx": rows(_np.arange(T, dtype=_np.float32)), "dvec": rows(f("attn_b_D")), "gw": f("ffn_gate_w").T, "gb": rows(f("ffn_gate_bias")),
        "w13": cat([f("ffn_w1"), f("ffn_w3")], 2), "w2": f("ffn_w2"),
        "sg": f("ffn_shared_gate"), "su": f("ffn_shared_up"), "sd": f("ffn_shared_down"),
    }
    return {k: _np.ascontiguousarray(v) for k, v in d.items()}


def kernel(**inputs):
    import numpy as _np
    import concourse.bacc as _bacc
    from concourse import mybir as _mybir
    from concourse.bass_utils import run_bass_kernel_spmd as _run

    nc = _bacc.Bacc("TRN2", target_bir_lowering=False, num_devices=1)
    arrays, args = {}, {}
    for name, v in layout(inputs).items():
        arrays[f"in_{name}_dram"] = v
        args[name] = nc.dram_tensor(f"in_{name}_dram", v.shape, _mybir.dt.from_np(v.dtype), kind="ExternalInput").ap()
    out = nc.dram_tensor("out_0_dram", (1, 2048, 512), _mybir.dt.float32, kind="ExternalOutput").ap()
    program(nc, args, out)
    r = _run(nc, [arrays], core_ids=[0])
    return r.results[0]["out_0_dram"]
```

```python
from contextlib import ExitStack

import numpy as np
import concourse.bass as bass
from concourse import mybir

F32 = mybir.dt.float32
F32R = mybir.dt.float32r
U32 = mybir.dt.uint32
I32 = mybir.dt.int32
ALU = mybir.AluOpType
ACT = mybir.ActivationFunctionType
AX = mybir.AxisListType

T = 2048
D = 512
NT = 16
H = 6
DK = 64
E = 32
CAP = 128
TB = 256
NB = T // TB
MAGIC = 12582912.0
TWO_PI = 6.283185
LEVELS = (1, 2, 4, 8, 16, 32, 64)
C_ID, C_TRI, C_STRI, C_M1T = 0, 128, 256, 384
C_MASK = 512
C_BONE = C_MASK + 6 * 128
C_IOTA = C_BONE + 2
C_SGN = C_IOTA + 128
C_U = C_SGN + 2
C_L = C_U + 16
C_TOK = C_L + 16
C_N = C_TOK + 16


def shape_constants():
    c = np.zeros((128, C_N), np.float32)
    r = np.arange(128)
    s, t = r[:, None], r[None, :]
    c[:, C_ID:C_ID + 128] = s == t
    c[:, C_TRI:C_TRI + 128] = s <= t
    c[:, C_STRI:C_STRI + 128] = s < t

    def level(n, row, col):
        return (row == col) | ((row // (2 * n) == col // (2 * n)) & (row // n % 2 == 1) & (col // n % 2 == 0))

    c[:, C_M1T:C_M1T + 128] = level(1, t, s)
    for i, n in enumerate(LEVELS[1:7]):
        c[:, C_MASK + 128 * i:C_MASK + 128 * i + 128] = level(n, s, t)
    c[:64, C_BONE] = 1
    c[64:, C_BONE + 1] = 1
    c[:, C_IOTA:C_IOTA + 128] = np.arange(128)
    c[:, C_TOK:C_TOK + 16] = s + 128 * np.arange(16) - 2 * T
    c[:64, C_SGN] = 1
    c[64:, C_SGN] = -1
    c[:, C_SGN + 1] = -1
    i, j = np.arange(16) // 4, np.arange(16) % 4
    c[:, C_U:C_U + 16] = j > i
    c[:, C_L:C_L + 16] = j < i
    return c


class Size:

    def elementwise(self, out, *args, **kw):
        n = 1
        for x in out.shape[1:]:
            n *= x
        return n

    activation = tensor_tensor = tensor_scalar = scalar_tensor_tensor = tensor_copy = bn_aggr = elementwise
    reciprocal = memset = max = elementwise

    def source(self, out, in_, *args, **kw):
        return self.elementwise(in_)

    tensor_reduce = bn_stats = max_index = tensor_tensor_scan = source

    def affine_select(self, out, **kw):
        return self.elementwise(out)


class Line:

    def __init__(self, sem, by=1):
        self.sem, self.by, self.n = sem, by, 0

    def up(self):
        self.n += self.by
        return (self, self.n)


def program(nc, a, out, stage=9):
    ctx = ExitStack()
    q = {"sync": [], "scalar": [], "vector": [], "tensor": [], "gpsimd": []}
    lines = []

    def line(name, by=1):
        x = Line(ctx.enter_context(nc.semaphore(name)), by)
        lines.append(x)
        return x

    def flat(w):
        if w is None:
            return []
        if isinstance(w, tuple) and w and isinstance(w[0], Line):
            return [w]
        return [y for x in w for y in flat(x)]

    clock = {engine: 0.0 for engine in q}
    ends = {}
    last = [0.0]

    def op(engine, fn, waits=(), on=None, cost=0.1, lag=0.3):
        waits = flat(waits)
        q[engine].append((waits, fn, on))
        clock[engine] = cost + max([clock[engine]] + [ends.get(w, 0.0) for w in waits])
        if on is None:
            return None
        t = on.up()
        ends[t] = clock[engine] + lag
        last[0] = max(last[0], ends[t])
        return t

    def fence(waits):
        for engine in q:
            q[engine].append((flat(waits), None, None))

    def weave(chains, until=None):
        ready = {x: 0.0 for x in chains}
        blocked = set()
        while any(x in ready for x in until or chains):
            able = [x for x in chains if x in ready and x not in blocked]
            due = [x for x in able if ready[x] <= clock["tensor"]]
            x = due[0] if due else min(able, key=lambda x: ready[x])
            last[0] = 0.0
            r = next(x, 0)
            if r is True:
                blocked.add(x)
                continue
            blocked.clear()
            if r == 0:
                ready.pop(x)
            else:
                ready[x] = ends[r] if isinstance(r, tuple) else 0.0 if r == 3 else last[0]

    def merge(threads):
        at = [[0, n, gen] for gen, n in threads if gen is not None]
        while at:
            x = min(at, key=lambda x: x[0] / x[1])
            x[0] += 1
            if next(x[2], 0) == 0:
                at.remove(x)

    def barrier():
        now = [(x, x.n) for x in lines if x.n]
        for engine in q:
            q[engine].append((now, None, None))

    with ctx:
        L_pe, L_dve, L_act, L_pool = line("pe"), line("dve"), line("act"), line("pool")

        size = Size()

        def pe(fn, waits=(), sig=True, cost=0.1):
            return op("tensor", fn, waits, L_pe if sig else None, cost)

        def dve(fn, waits=()):
            return op("vector", fn, waits, L_dve, 0.07 + 0.00104 * fn(size))

        def act(fn, waits=()):
            return op("scalar", fn, waits, L_act, 0.1 + 0.00075 * fn(size))

        def pool(fn, waits=()):
            return op("gpsimd", fn, waits, L_pool, 0.1 + 0.0013 * fn(size))

        def dma(fn, on, waits=(), engine="sync"):
            return op(engine, fn, waits, on, 0.1, 4.0)

        def mm(o, lhsT, rhs, start=True, stop=True, waits=(), sig=False, skip=False):
            n = max(64, rhs.shape[-1]) / 2400 * (2 if rhs.dtype == F32R else 4)
            return pe(lambda e: e.matmul(o, lhsT, rhs, start=start, stop=stop, skip_group_check=skip), waits, sig, n)

        def tr(o, i, waits=(), sig=False):
            n = i.shape[0]
            return pe(lambda e: e.transpose(o, i, ident[0:n, 0:n]), waits, sig, 0.11)

        def sb(name, shape, dt=F32, c=ctx):
            return c.enter_context(nc.sbuf_tensor(name, shape, dt))

        PS = ctx.enter_context(nc.psum_tensor("PS", [128, 8, 512], F32))
        free = [None] * 8

        X = sb("X", [128, NT, D])
        CON = sb("CON", [128, C_N])
        ones = sb("ones", [128, 128])
        ident = CON[:, C_ID:C_ID + 128]
        triu = CON[:, C_TRI:C_TRI + 128]
        stri = CON[:, C_STRI:C_STRI + 128]
        bst = sb("bst", [128, NT, 6])
        bmv = sb("bmv", [128, NT, 2])
        rstd = sb("rstd", [128, NT])
        pw = sb("pw", [128, 64])

        L_x = [line(f"d_x{i}", 16) for i in range(4)]
        L_con, L_ls = line("d_con", 16), line("d_ls", 16)
        L_tb = [line("d_tb0", 16), line("d_tb1", 16)]
        L_ti = [line(f"d_ti{i}", 16) for i in range(4)]
        L_w = [line(f"d_w{i}", 16) for i in range(8)]
        t_con = dma(lambda e: e.dma_start(CON[:, :], a["consts"]), L_con)
        xv = a["x"].rearrange("b (i p) n -> p (b i) n", p=128)
        t_x = [None] * 4

        def load_x(i):
            t_x[i] = dma(lambda e: e.dma_start(X[:, 4 * i:4 * i + 4, :], xv[:, 4 * i:4 * i + 4, :]), L_x[i])
        load_x(0)
        t_ones = pool(lambda e: e.memset(ones[:, :], 1.0))
        t_pw = pool(lambda e: e.memset(pw[:, :], -0.5))
        eps = sb("eps", [128, 1])
        t_eps = pool(lambda e: e.memset(eps[:, :], 1e-5))

        LS = sb("LS", [128, 8])
        c2 = sb("c2", [128, 4])
        tabs = nc.dram_tensor("rot", [2, 128, T], F32, kind="Internal").ap()
        xnd = nc.dram_tensor("moe_in", [T, D], F32, kind="Internal").ap()
        yd = nc.dram_tensor("moe_out", [T, D], F32, kind="Internal").ap()

        def moments(i, t):
            t = dve(lambda e: e.bn_stats(bst[:, i, :], X[:, i, :]), [t])
            return dve(lambda e: e.bn_aggr(bmv[:, i, :], bst[:, i, :]), [t])

        def inverse_std(ii, t):
            t = dve(lambda e: e.tensor_scalar(rstd[:, ii], bmv[:, ii, 1], 1e-5, None, ALU.add), [t])
            return pool(lambda e: e.tensor_tensor(rstd[:, ii], rstd[:, ii], pw[:, ii], ALU.pow), [t, t_pw])

        def normalise(i, xn, t):
            return dve(lambda e: e.tensor_scalar(xn, X[:, i, :], bmv[:, i, 0:1], rstd[:, i:i + 1], ALU.subtract, ALU.mult), [t])

        def transpose_tile(xn, dst, b, t, t_dst):
            for k in range(4):
                t1 = tr(PS[:, b, k * 128:(k + 1) * 128], xn[:, k * 128:(k + 1) * 128], [t, free[b], t_con], sig=(k == 3))
            free[b] = act(lambda e: e.activation(dst, PS[:, b, :].rearrange("p (k n) -> p k n", k=4), ACT.Copy), [t1, t_dst])
            return t1, free[b]

        def delta_net():
            with ExitStack() as c:
                def s1(name, shape, dt=F32):
                    return sb(name, shape, dt, c)
                W = s1("W", [128, 4, 2304])
                WO = s1("WO", [128, H, D])
                WAB = s1("WAB", [128, 4, 12])
                CW = s1("CW", [128, 12, 4])
                SM = s1("SM", [128, 16])
                trr = s1("trr", [128, 128], F32R)
                t_sm = dma(lambda e: e.dma_start(SM[:, :], a["small"]), L_w[1])
                t_wab = dma(lambda e: e.dma_start(WAB[:, :, :], a["wab"].rearrange("(c p) n -> p c n", p=128)), L_w[0])
                t_cw = dma(lambda e: e.dma_start(CW[:, :, :], a["convw"].rearrange("(c p) n -> p c n", p=128)), L_w[2])
                wv = a["wqkvg"].rearrange("(c p) n -> p c n", p=128)
                t_w = [t_x[0]]
                for j in range(3):
                    t_w.append(dma(lambda e, j=j: e.dma_start(W[:, :, 768 * j:768 * j + 768], wv[:, :, 768 * j:768 * j + 768]), L_w[3 + j], [t_w[-1]]))
                t_w = t_w[1:]
                t_wo = dma(lambda e: e.dma_start(WO[:, :, :], a["wo"].rearrange("(c p) n -> p c n", p=128)), L_w[6], [t_w[2]])
                for i in range(1, 4):
                    load_x(i)
                t_trr = dve(lambda e: e.tensor_copy(trr[:, :], triu), [t_con])

                xnt2 = s1("xnt2", [128, D])
                XB = s1("XB", [128, 3, 4, TB])
                kv = s1("kv", [128, 2, 9, TB])
                qb = s1("qb", [128, 3, 3, TB])
                raw = s1("raw", [128, 2, 3 + TB])
                halo = s1("halo", [128, 12, 3])
                cacc = s1("cacc", [128, 2, 2, TB])
                th = s1("th", [128, 2, TB])
                sq = xnt2[:, :].rearrange("p (j n) -> p j n", j=2)
                rn = s1("rn", [128, NT, 12])
                za = s1("za", [128, NT, H])
                sp = s1("sp", [128, NT, H])
                g = s1("g", [128, NT, H])
                gh = s1("gh", [128, 2, NT, H], F32R)
                beta = s1("beta", [128, NT, H])
                ea = s1("ea", [128, H])
                G = s1("G", [128, NT, H])
                eG = s1("eG", [128, NT, H])
                neG = s1("neG", [128, NT, H])
                dG = s1("dG", [128, NT, H])
                eC = s1("eC", [128, NT, 3])
                nb = s1("nb", [128, NT, H])

                kh = s1("kh", [128, 3, 2, DK])
                kd = s1("kd", [128, 3, 3, 2, DK])
                khT = s1("khT", [128, 3, 3, 128])
                V = s1("V", [128, 3, H, 128])
                Dm = s1("Dm", [128, H, 128])
                NTm = s1("NTm", [128, 2, H, 128])
                NTr = s1("NTr", [128, H, 128], F32R)
                P = s1("P", [128, 3, H, 128])
                R = s1("R", [128, H, 128], F32R)
                Rf = s1("Rf", [128, 2, H, 128])
                Tm = s1("Tm", [128, H, 128], F32R)
                Z = s1("Z", [128, H, 128], F32R)
                S = s1("S", [128, 2, 3, 128])
                o = s1("o", [128, H, 128])
                gs = s1("gs", [128, H, 128])
                ms = s1("ms", [128, H])
                qs = s1("qs", [128, H])

                t_halo = [pool(lambda e: e.memset(halo[:, :, :], 0.0))]
                t_S = [pool(lambda e: e.memset(S[:, 0, :, :], 0.0))]
                t_ea = act(lambda e: e.activation(ea[:, :], SM[:, H:2 * H], ACT.Exp), [t_sm])

                def cols(x, h):
                    return x[:, h * 128:h * 128 + 128]

                def grp(x, gr):
                    return x[:, 3 * gr:3 * gr + 3, :].rearrange("p h n -> p (h n)")

                rel = {}
                done = {}

                def tables():
                    def col(j):
                        return LS[:, j:j + 1]
                    t_ls = dma(lambda e: e.dma_start(LS[:, 0:2], a["lsm"]), L_ls, (), "scalar")
                    t_th = act(lambda e: e.activation(c2[:, 2:3], col(1), ACT.Exp), [t_ls])
                    t = act(lambda e: e.activation(c2[:, 0:1], col(0), ACT.Abs))
                    t = act(lambda e: e.activation(c2[:, 0:1], c2[:, 0:1], ACT.Exp, scale=-1.0), [t])
                    t = act(lambda e: e.activation(c2[:, 1:2], c2[:, 0:1], ACT.Ln, bias=1.0), [t])
                    yield
                    t = dve(lambda e: e.scalar_tensor_tensor(c2[:, 1:2], col(0), 0.0, c2[:, 1:2], ALU.max, ALU.add), [t])
                    yield
                    t = act(lambda e: e.activation(c2[:, 1:2], c2[:, 1:2], ACT.Exp), [t])
                    t = act(lambda e: e.activation(col(2), c2[:, 1:2], ACT.Exp, scale=-1.0), [t])
                    yield
                    t = dve(lambda e: e.tensor_tensor(col(3), col(2), col(2), ALU.mult), [t])
                    t = dve(lambda e: e.tensor_scalar(col(3), col(3), -1.0, 1.0, ALU.mult, ALU.add), [t])
                    t = dve(lambda e: e.tensor_scalar(col(3), col(3), 0.0, None, ALU.max), [t])
                    yield
                    t = act(lambda e: e.activation(col(3), col(3), ACT.Sqrt), [t])
                    yield
                    dve(lambda e: e.tensor_tensor(col(4), col(3), CON[:, C_SGN:C_SGN + 1], ALU.mult), [t, t_con])
                    t = dve(lambda e: e.tensor_scalar(c2[:, 2:3], c2[:, 2:3], 0.15915494309189535, None, ALU.mult), [t_th])
                    t = dve(lambda e: e.tensor_scalar(c2[:, 3:4], c2[:, 2:3], MAGIC, -MAGIC, ALU.add, ALU.add), [t])
                    t = dve(lambda e: e.tensor_tensor(c2[:, 2:3], c2[:, 2:3], c2[:, 3:4], ALU.subtract), [t])
                    t = dve(lambda e: e.tensor_scalar(c2[:, 3:4], c2[:, 2:3], 4096.0, None, ALU.mult), [t])
                    t = dve(lambda e: e.tensor_scalar(c2[:, 3:4], c2[:, 3:4], MAGIC, -MAGIC, ALU.add, ALU.add), [t])
                    t = dve(lambda e: e.tensor_scalar(col(5), c2[:, 3:4], 1.0 / 4096, None, ALU.mult), [t])
                    t_u = dve(lambda e: e.tensor_tensor(col(6), c2[:, 2:3], col(5), ALU.subtract), [t])
                    yield
                    xb, qv = XB[:, 2, :, :].rearrange("p k n -> p (k n)"), qb[:, 2, :, :].rearrange("p j n -> p (j n)")
                    tf, A1, A2 = xb[:, 0:512], xb[:, 512:1024], qv[:, 0:512]

                    def wrap(t):
                        t = dve(lambda e: e.tensor_scalar(A2, A1, MAGIC, -MAGIC, ALU.add, ALU.add), [t])
                        return dve(lambda e: e.tensor_tensor(A1, A1, A2, ALU.subtract), [t])
                    t_s, t_o = None, [None, None]
                    for n in range(4):
                        t_i = dma(lambda e, n=n: e.dma_start(tf, a["tidx"][:, 512 * n:512 * n + 512]), L_ti[n], [t_s], "scalar")
                        t = dve(lambda e: e.tensor_scalar(A1, tf, col(5), None, ALU.mult), [t_i, t_u, t_s])
                        t = wrap(t)
                        t = dve(lambda e: e.scalar_tensor_tensor(A1, tf, col(6), A1, ALU.mult, ALU.add), [t])
                        t = wrap(t)
                        yield
                        for j in (1, 0):
                            dst = (gs, o)[j][:, 0:4, :].rearrange("p h n -> p (h n)")
                            if j == 0:
                                t = dve(lambda e: e.tensor_scalar(A1, A1, 0.25, None, ALU.add), [t])
                                t = wrap(t)
                            yield
                            t = act(lambda e, dst=dst: e.activation(dst, A1, ACT.Sin, scale=TWO_PI), [t, t_o[j]])
                            t_o[j] = dma(lambda e, n=n, j=j, dst=dst: e.dma_start(tabs[j, :, 512 * n:512 * n + 512], dst), L_tb[j], [t], "scalar")
                            yield
                        t_s = t
                    rel[("XB", 2)] = rel[("qb", 2)] = t_s
                    rel["gs"] = rel["o"] = t_o
                    done["tab"] = True
                    yield

                def proj(B):
                    x3, k2, q3 = B % 3, B % 2, B % 3
                    tt = slice(2 * B, 2 * B + 2)
                    t_r = inverse_std(tt, [moments(i, t_x[i // 4]) for i in (2 * B, 2 * B + 1)])
                    yield 2
                    t_xb = []
                    for u, i in enumerate((2 * B, 2 * B + 1)):
                        t = normalise(i, xnt2[:, :], [t_r, rel.get("xn")])
                        yield 2
                        rel["xn"], t2 = transpose_tile(
                            xnt2[:, :], XB[:, x3, :, u * 128:(u + 1) * 128], 7, t, rel.get(("XB", x3)))
                        t_xb.append(t2)
                        yield 2
                    for u in range(2):
                        for k in range(4):
                            t = mm(PS[:, 7, u * 12:u * 12 + 12], XB[:, x3, k, u * 128:(u + 1) * 128], WAB[:, k, :],
                                   k == 0, k == 3, [t_xb, t_wab, free[7]], sig=(k == 3))
                    ab = PS[:, 7, 0:24].rearrange("p (i n) -> p i n", n=12)
                    z2 = za[:, tt, :]
                    t1 = dve(lambda e: e.tensor_tensor(z2, ab[:, :, 0:H], SM[:, 0:H].unsqueeze(1).to_broadcast([128, 2, H]), ALU.add), [t, t_sm])
                    t4 = act(lambda e: e.activation(beta[:, tt, :], ab[:, :, H:12], ACT.Exp, scale=-1.0), [t1])
                    free[7] = t4
                    t3 = act(lambda e: e.activation(sp[:, tt, :], z2, ACT.Abs), [t1])
                    t3 = act(lambda e: e.activation(sp[:, tt, :], sp[:, tt, :], ACT.Exp, scale=-1.0), [t3])
                    t3 = act(lambda e: e.activation(sp[:, tt, :], sp[:, tt, :], ACT.Ln, bias=1.0), [t3])
                    yield 2
                    t8 = dve(lambda e: e.tensor_scalar(beta[:, tt, :], beta[:, tt, :], 1.0, None, ALU.add), [t4])
                    t8 = dve(lambda e: e.reciprocal(beta[:, tt, :], beta[:, tt, :]), [t8])
                    t_nb = dve(lambda e: e.tensor_scalar(nb[:, tt, :], beta[:, tt, :], -1.0, None, ALU.mult), [t8])
                    t7 = dve(lambda e: e.scalar_tensor_tensor(sp[:, tt, :], z2, 0.0, sp[:, tt, :], ALU.max, ALU.add), [t3])
                    t_g = dve(lambda e: e.scalar_tensor_tensor(
                        g[:, tt, :], sp[:, tt, :], -1.0, ea[:, :].unsqueeze(1).to_broadcast([128, 2, H]), ALU.mult, ALU.mult), [t7, t_ea])
                    t1 = dve(lambda e: e.tensor_copy(gh[:, 0, tt, :], g[:, tt, :]), [t_g])
                    t_gh = dve(lambda e: e.tensor_tensor(gh[:, 1, tt, :], g[:, tt, :], gh[:, 0, tt, :].bitcast(F32), ALU.subtract), [t1])
                    yield
                    t_raw, t_cv, t_th, t_act = {}, {}, {}, {}

                    def conv(c2, v):
                        if c2 >= 0:
                            t = t_raw[c2]
                            for j in range(3):
                                t = dve(lambda e, j=j: e.scalar_tensor_tensor(
                                    cacc[:, c2 % 2, v, :], raw[:, v, j:j + TB], CW[:, 2 * c2 + v, j:j + 1], cacc[:, c2 % 2, v, :], ALU.mult, ALU.add), [t])
                            t_cv[c2] = t
                            rel["raw"] = [t, t_raw[c2]]

                    def tanh(c2):
                        if c2 >= 0:
                            t_th[c2] = act(lambda e: e.activation(th[:, :, :], cacc[:, c2 % 2, :, :], ACT.Tanh, scale=0.5), [t_cv[c2], rel.get("th")])

                    def silu(c2):
                        if c2 >= 0:
                            for v in range(2):
                                ct = 2 * c2 + v
                                dst = qb[:, q3, ct, :] if ct < 3 else kv[:, k2, ct - 3, :]
                                t_act[ct] = dve(lambda e, dst=dst, v=v: e.scalar_tensor_tensor(
                                    dst, th[:, v, :], 1.0, cacc[:, c2 % 2, v, :], ALU.add, ALU.mult),
                                    [t_th[c2], rel.get(("qb", q3)) if ct < 3 else rel.get(("kv", k2))])
                            rel["th"] = rel[("cacc", c2 % 2)] = t_act[ct]

                    for c2 in range(6):
                        while (c2 == 0 and B >= 3 and ("o", 2 * B - 5) not in done) or (c2 == 3 and B >= 2 and ("a", 2 * B - 3) not in done):
                            yield True
                        if c2 == 1:
                            gf = g[:, tt, :].rearrange("p i h -> p (i h)")
                            mm(PS[:, 7, 0:12], triu, gf, True, True, [t_g, free[7]])
                            t = mm(PS[:, 7, 16:28], ones[:, :], gf, True, True, [t_ones], sig=True)
                            Gp = PS[:, 7, 0:12].rearrange("p (i h) -> p i h", h=H)
                            Cp = PS[:, 7, 16:28].rearrange("p (i h) -> p i h", h=H)
                            t_G = dve(lambda e: e.tensor_copy(G[:, tt, :], Gp), [t])
                            t1 = dve(lambda e: e.tensor_tensor(dG[:, tt, :], Cp, G[:, tt, :], ALU.subtract), [t_G])
                            yield 2
                            act(lambda e: e.activation(eC[0:64, tt, :], Cp[0:64, :, 0:3], ACT.Exp), [t1])
                            t_eC = act(lambda e: e.activation(eC[64:128, tt, :], Cp[64:128, :, 3:6], ACT.Exp))
                            free[7] = t_eC
                            t_eG = act(lambda e: e.activation(eG[:, tt, :], G[:, tt, :], ACT.Exp), [t_G])
                            t2 = act(lambda e: e.activation(dG[:, tt, :], dG[:, tt, :], ACT.Exp), [t1])
                            yield 2
                            t_neG = dve(lambda e: e.tensor_scalar(neG[:, tt, :], eG[:, tt, :], -1.0, None, ALU.mult), [t_eG])
                            t_dG = dve(lambda e: e.tensor_tensor(dG[:, tt, :], dG[:, tt, :], beta[:, tt, :], ALU.mult), [t2])
                            yield 3
                        pair = PS[:, 7, :].rearrange("p (c n) -> p c n", c=2)
                        for v in range(2):
                            ct = 2 * c2 + v
                            for k in range(4):
                                t = mm(pair[:, v, :], W[:, k, ct * 128:(ct + 1) * 128], XB[:, x3, k, :],
                                       k == 0, k == 3, [t_w[ct // 6], free[7], t_xb], sig=(k == 3))
                            conv(c2 - 1, v)
                            if v == 0:
                                silu(c2 - 2)
                            yield t
                        t0 = pool(lambda e, c2=c2: e.tensor_copy(raw[:, :, 0:3], halo[:, 2 * c2:2 * c2 + 2, :]), [t_halo[0], rel.get("raw")])
                        t1 = act(lambda e: e.activation(raw[:, :, 3:3 + TB], pair, ACT.Copy), [t, rel.get("raw")])
                        for v in range(2):
                            t2 = act(lambda e, c2=c2, v=v: e.activation(
                                cacc[:, c2 % 2, v, :], pair[:, v, :], ACT.Copy, scale=CW[:, 2 * c2 + v, 3:4]), [t, t_cw, rel.get(("cacc", c2 % 2))])
                        free[7] = t2
                        t_hl = pool(lambda e, c2=c2: e.tensor_copy(halo[:, 2 * c2:2 * c2 + 2, :], raw[:, :, TB:TB + 3]), [t1, t0])
                        t_raw[c2] = [t0, t1, t2, t_hl]
                        tanh(c2 - 1)
                        yield t2
                        if c2 == 4:
                            for j2 in range(0, 6, 2):
                                for j in (j2, j2 + 1):
                                    src = qb[:, q3, j, :] if j < 3 else kv[:, k2, j - 3, :]
                                    t_sq = act(lambda e, j=j, src=src: e.activation(sq[:, j % 2, :], src, ACT.Square), [t_act[j], rel["xn"]])
                                yield 2
                                for j in (j2, j2 + 1):
                                    for cl in range(2):
                                        o0 = cl * 12 + (j // 3) * 6 + j % 3
                                        t = mm(PS[:, 7, o0:o0 + 4:3], sq[:, j % 2, cl * 128:cl * 128 + 128], CON[:, C_BONE:C_BONE + 2], True, True,
                                               [t_sq, t_con, free[7]], sig=(cl == 1))
                                    rel["xn"] = t
                                for j in (j2, j2 + 1):
                                    o0 = (j // 3) * 6 + j % 3
                                    free[7] = t1 = dve(lambda e, o0=o0: e.tensor_scalar(
                                        rn[:, tt, o0:o0 + 4:3], PS[:, 7, 0:24].rearrange("p (i n) -> p i n", n=12)[:, :, o0:o0 + 4:3], 4e-6, None, ALU.add), [t])
                            t1 = act(lambda e: e.activation(rn[:, tt, :], rn[:, tt, :], ACT.Sqrt), [t1])
                            yield t1
                            t_rn = dve(lambda e: e.reciprocal(rn[:, tt, :], rn[:, tt, :]), [t1])
                            yield 3
                    conv(5, 0)
                    conv(5, 1)
                    silu(4)
                    yield 2
                    tanh(5)
                    yield 2
                    silu(5)
                    done[B] = dict(qkv=t_act[11], rn=t_rn, gh=t_gh, G=t_G, eG=t_eG, neG=t_neG, dG=t_dG, nb=t_nb, eC=t_eC)

                def prepare(ch):
                    B, cl, s2 = ch // 2, ch % 2, ch % 3
                    k2, q3, n2 = B % 2, B % 3, ch % 2
                    cs = slice(cl * 128, cl * 128 + 128)
                    ok = done[B]
                    for j in range(3):
                        t = tr(PS[:, 3, j * 128:(j + 1) * 128], kv[:, k2, j, cs], [ok["qkv"], free[3]], sig=(j == 2))
                    t_kh = dve(lambda e: e.tensor_tensor(
                        kh[:, :, :, :], PS[:, 3, 0:384].rearrange("p (j g d) -> p j g d", d=DK, g=2),
                        rn[:, ch, 6:12].rearrange("p (g j) -> p j g", g=2).unsqueeze(3).to_broadcast([128, 3, 2, DK]), ALU.mult),
                        [t, ok["rn"], rel.get("kh")])
                    free[3] = t_kh
                    yield
                    for gr in range(2):
                        for j in range(3):
                            tv = tr(PS[:, 3 + gr, j * 128:(j + 1) * 128], kv[:, k2, 3 + 3 * gr + j, cs],
                                    [free[3], free[4]], sig=(gr == 1 and j == 2))
                    rel[("kv", k2)] = tv
                    t_V = [act(lambda e, gr=gr: e.activation(
                        grp(V[:, s2, :, :], gr), PS[:, 3 + gr, 0:384], ACT.Copy, scale=0.5),
                        [tv, rel.get(("V", s2))]) for gr in range(2)]
                    free[3] = free[4] = t_V
                    yield
                    for gr in range(2):
                        for j in range(3):
                            h = 3 * gr + j
                            for p in range(2):
                                t = mm(cols(PS[:, 3 + gr, :], j), gh[:, p, ch, h:h + 1].to_broadcast([128, 128]), trr[:, :],
                                       p == 0, p == 1, [free[3 + gr], ok["gh"], t_trr], sig=(j == 2 and p == 1))
                        for j in range(3):
                            h = 3 * gr + j
                            t1 = dve(lambda e, h=h, j=j, gr=gr: e.tensor_scalar(
                                Dm[:, h, :], cols(PS[:, 3 + gr, :], j), G[:, ch, h:h + 1], 0.0, ALU.subtract, ALU.min),
                                [t, rel.get("Dm")])
                        free[3 + gr] = t1
                    t_kd = pool(lambda e: e.tensor_tensor(
                        kd[:, s2, :, :, :], kh[:, :, :, :],
                        dG[:, ch, :].rearrange("p (g j) -> p j g", g=2).unsqueeze(3).to_broadcast([128, 3, 2, DK]), ALU.mult),
                        [t_kh, ok["dG"], rel.get(("kd", s2))])
                    yield
                    for j in range(3):
                        t = tr(PS[:, 3, j * 128:(j + 1) * 128], kh[:, j, :, :].rearrange("p g d -> p (g d)"), [t_kh, free[3]], sig=(j == 2))
                    rel["kh"] = [t, t_kd]
                    t_khT = act(lambda e: e.activation(
                        khT[:, s2, :, :], PS[:, 3, 0:384].rearrange("p (j n) -> p j n", n=128), ACT.Copy),
                        [t, rel.get(("khT", s2))])
                    free[3] = t_khT
                    yield
                    t1 = act(lambda e: e.activation(Dm[:, :, :], Dm[:, :, :], ACT.Exp), [t1])
                    yield
                    for h in range(H):
                        t_D = dve(lambda e, h=h: e.scalar_tensor_tensor(
                            Dm[:, h, :], Dm[:, h, :], nb[:, ch, h:h + 1], triu, ALU.mult, ALU.mult), [t1, ok["nb"]])
                    for j in range(3):
                        for gr in range(2):
                            p0 = 64 * gr
                            tk = mm(cols(PS[:, 3 + gr, :], j), khT[p0:p0 + 64, s2, j, :], khT[p0:p0 + 64, s2, j, :], True, True,
                                    [free[3 + gr], t_khT], sig=(j == 2))
                    t_N, t_P = [], []
                    for gr in range(2):
                        t1 = dve(lambda e, gr=gr: e.tensor_tensor(grp(NTm[:, n2, :, :], gr), PS[:, 3 + gr, 0:384], grp(Dm, gr), ALU.mult), [tk, t_D, rel.get(("NTm", n2, gr))])
                        free[3 + gr] = t1
                        t_N.append(pool(lambda e, gr=gr: e.affine_select(
                            out=NTm[:, n2, 3 * gr:3 * gr + 3, :], in_=NTm[:, n2, 3 * gr:3 * gr + 3, :], compare_op=ALU.not_equal, fill=-1.0, base=0,
                            pattern=[[0, 3], [-1, 128]], channel_multiplier=1), [t1]))
                    yield
                    yield
                    for j in range(3):
                        for gr in range(2):
                            p0 = 64 * gr
                            t = mm(cols(PS[:, 3 + gr, :], j), khT[p0:p0 + 64, s2, j, :], qb[p0:p0 + 64, q3, j, cs], True, True,
                                   [free[3 + gr]], sig=(j == 2))
                    for gr in range(2):
                        t1 = dve(lambda e, gr=gr: e.tensor_tensor(grp(P[:, s2, :, :], gr), PS[:, 3 + gr, 0:384], grp(Dm, gr), ALU.mult),
                                 [t, t_D, rel.get(("P", s2))])
                        free[3 + gr] = t1
                        t_P.append(t1)
                    rel["Dm"] = t_P
                    done[("a", ch)] = dict(N=t_N, P=t_P, kd=t_kd, khT=t_khT, V=t_V)
                    yield

                def solve(ch, gr):
                    n2, s2, hs = ch % 2, ch % 2, slice(3 * gr, 3 * gr + 3)
                    ok = done[("a", ch)]
                    b0, b1 = ((0, 1), (2, 1))[gr]
                    pb, pr = PS[:, b0, 0:384], PS[:, b1, 0:384]
                    p3 = pb.rearrange("p (h n) -> p h n", n=128)
                    t_Nr = pool(lambda e: e.affine_select(
                        out=NTr[:, hs, :], in_=NTm[:, n2, hs, :], compare_op=ALU.not_equal, fill=1.0, base=0,
                        pattern=[[0, 3], [-1, 128]], channel_multiplier=1), [ok["N"][gr], rel.get(("NTr", gr))])
                    yield
                    t_R = dve(lambda e: e.tensor_tensor(
                        R[:, hs, :], NTr[:, hs, :].bitcast(F32),
                        CON[:, C_M1T:C_M1T + 128].unsqueeze(1).to_broadcast([128, 3, 128]), ALU.mult), [t_Nr, rel.get(("R", gr))])
                    yield
                    for j in range(3):
                        t = tr(cols(pb, j), R[:, 3 * gr + j, :].bitcast(F32), [t_R, free[b0]], sig=(j == 2))
                    free[b0] = t_T = act(lambda e: e.activation(grp(Tm, gr), pb, ACT.Copy), [t, rel.get(("Tm", gr))])
                    yield
                    t_Z, t_Zr = None, rel.get(("Z", gr))
                    for li in range(6):
                        m = CON[:, C_MASK + 128 * li:C_MASK + 128 * li + 128]
                        for h in range(3 * gr, 3 * gr + 3):
                            t = mm(cols(pb, h % 3), NTr[:, h, :], Tm[:, h, :], True, True, [t_Nr, t_T, free[b0]], sig=(h % 3 == 2))
                        if li == 5:
                            rel[("NTr", gr)] = t
                        free[b0] = t_Z = dve(lambda e, m=m: e.tensor_tensor(
                            Z[:, hs, :], p3, m.unsqueeze(1).to_broadcast([128, 3, 128]), ALU.mult), [t, t_Zr])
                        yield
                        for h in range(3 * gr, 3 * gr + 3):
                            t = mm(cols(pb, h % 3), R[:, h, :], Z[:, h, :], True, True, [t_Z, t_R, free[b0]], sig=(h % 3 == 2))
                        free[b0] = t_T = act(lambda e: e.activation(grp(Tm, gr), pb, ACT.Copy), [t])
                        yield free[b1] or 3
                        for h in range(3 * gr, 3 * gr + 3):
                            t_Zr = mm(cols(pr, h % 3), Z[:, h, :], R[:, h, :], True, True, [free[b1]], sig=(h % 3 == 2))
                        free[b1] = t_R = act(lambda e: e.activation(grp(R, gr), pr, ACT.Copy), [t_Zr])
                        yield t_T
                    for h in range(3 * gr, 3 * gr + 3):
                        t = mm(cols(pb, h % 3), NTm[:, n2, h, :], Tm[:, h, :].bitcast(F32), True, True, [t_T, ok["N"][gr], free[b0]], sig=(h % 3 == 2))
                    rel[("Tm", gr)] = t
                    rel[("NTm", n2, gr)] = t
                    free[b0] = t_Z = dve(lambda e: e.tensor_tensor(
                        Z[:, hs, :], ident.unsqueeze(1).to_broadcast([128, 3, 128]), p3, ALU.add), [t, t_Zr])
                    yield
                    for h in range(3 * gr, 3 * gr + 3):
                        t = mm(cols(pb, h % 3), Z[:, h, :], R[:, h, :], True, True, [t_Z, t_R, free[b0]], sig=(h % 3 == 2))
                    rel[("Z", gr)] = t
                    free[b0] = rel[("R", gr)] = done[("s", ch, gr)] = dve(lambda e: e.tensor_tensor(
                        grp(Rf[:, s2, :, :], gr), pb, grp(R, gr).bitcast(F32), ALU.add), [t, rel.get(("Rf", s2))])
                    yield

                def output(ch):
                    B, cl, s2, f2 = ch // 2, ch % 2, ch % 3, ch % 2
                    x3, q3 = B % 3, B % 3
                    cs = slice(cl * 128, cl * 128 + 128)
                    ok = done[B]
                    iv = {**done[("a", ch)], "Rf": [done[("s", ch, 0)], done[("s", ch, 1)]]}
                    Xv = Y = V[:, s2, :, :]
                    So, Sn = S[:, ch % 2, :, :], S[:, (ch + 1) % 2, :, :]
                    t_So = t_S[0]
                    for j in range(3):
                        for gr in range(2):
                            p0 = 64 * gr
                            t = mm(cols(PS[:, 5 + gr, :], j), khT[p0:p0 + 64, s2, j, :], So[p0:p0 + 64, j, :], True, True,
                                   [free[5 + gr], iv["khT"], t_So], sig=(j == 2))
                    rel[("khT", s2)] = t
                    for h in range(H):
                        t1 = dve(lambda e, h=h: e.scalar_tensor_tensor(
                            Xv[:, h, :], cols(PS[:, 5 + h // 3, :], h % 3), neG[:, ch, h:h + 1], V[:, s2, h, :], ALU.mult, ALU.add),
                            [t, ok["neG"], iv["V"]])
                        if h == 2:
                            free[5] = t1
                    free[6] = t1
                    yield
                    t_Y = []
                    for gr in range(2):
                        for j in range(3):
                            h = 3 * gr + j
                            t = mm(cols(PS[:, 5 + gr, :], j), Rf[:, f2, h, :], Xv[:, h, :], True, True,
                                   [free[5 + gr], t1, iv["Rf"]], sig=(j == 2))
                        t_Y.append(act(lambda e, gr=gr: e.activation(grp(Y, gr), PS[:, 5 + gr, 0:384], ACT.Copy), [t]))
                        free[5 + gr] = t_Y[gr]
                    rel[("Rf", f2)] = t
                    yield
                    for gr in range(2):
                        p0 = 64 * gr
                        for j in range(3):
                            t = mm(PS[p0:p0 + 64, 5, j * 128:(j + 1) * 128], kd[:, s2, j, gr, :], Y[:, 3 * gr + j, :], True, True,
                                   [t_Y[gr], iv["kd"], free[5]], sig=(gr == 1 and j == 2))
                    rel[("kd", s2)] = t
                    for j in range(3):
                        t1 = dve(lambda e, j=j: e.scalar_tensor_tensor(
                            Sn[:, j, :], So[:, j, :], eC[:, ch, j:j + 1], PS[:, 5, j * 128:(j + 1) * 128], ALU.mult, ALU.add),
                            [t, ok["eC"], rel.get(("S", (ch + 1) % 2))])
                    t_S[0] = t1
                    free[5] = t1
                    yield
                    for j in range(3):
                        for gr in range(2):
                            p0 = 64 * gr
                            t = mm(cols(PS[:, 5 + gr, :], j), qb[p0:p0 + 64, q3, j, cs], So[p0:p0 + 64, j, :], True, True,
                                   [free[5 + gr]], sig=(j == 2))
                    rel[("S", ch % 2)] = [t, t1]
                    rel[("qb", q3)] = t
                    t_o = []
                    for gr in range(2):
                        t1 = dve(lambda e, gr=gr: e.tensor_tensor(
                            o[:, 3 * gr:3 * gr + 3, :], PS[:, 5 + gr, 0:384].rearrange("p (h n) -> p h n", n=128),
                            eG[:, ch, 3 * gr:3 * gr + 3].unsqueeze(2).to_broadcast([128, 3, 128]), ALU.mult), [t, ok["eG"], rel.get("o")])
                        t_o.append(t1)
                        free[5 + gr] = t1
                    yield
                    for gr in range(2):
                        for j in range(3):
                            h = 3 * gr + j
                            t = mm(cols(PS[:, 5 + gr, :], j), P[:, s2, h, :], Y[:, h, :], True, True, [free[5 + gr], iv["P"]], sig=(j == 2))
                        t_o[gr] = dve(lambda e, gr=gr: e.tensor_tensor(grp(o, gr), grp(o, gr), PS[:, 5 + gr, 0:384], ALU.subtract), [t, t_o[gr]])
                        free[5 + gr] = t_o[gr]
                    rel[("P", s2)] = rel[("V", s2)] = t
                    yield
                    t_g = []
                    for gr in range(2):
                        for k in range(4):
                            t = mm(PS[:, 5 + gr, 0:384], XB[:, x3, k, cs], W[:, k, 1536 + 384 * gr:1920 + 384 * gr], k == 0, k == 3,
                                   [free[5 + gr], t_w[2]], sig=(k == 3))
                            if k == 1:
                                yield
                        yield
                        t1 = act(lambda e, gr=gr: e.activation(grp(gs, gr), PS[:, 5 + gr, 0:384], ACT.Tanh, scale=0.5), [t, rel.get("gs")])
                        yield
                        t1 = dve(lambda e, gr=gr: e.scalar_tensor_tensor(grp(gs, gr), grp(gs, gr), 1.0, PS[:, 5 + gr, 0:384], ALU.add, ALU.mult), [t1])
                        free[5 + gr] = t1
                        t_g.append(dve(lambda e, gr=gr: e.tensor_tensor(grp(o, gr), grp(o, gr), grp(gs, gr), ALU.mult), [t1, t_o[gr]]))
                    rel[("XB", x3)] = t
                    t_q = dve(lambda e: e.tensor_scalar(qs[:, :], rn[:, ch, 0:6], 0.125, None, ALU.mult), [rel.get("qs")])
                    yield
                    t2 = act(lambda e: e.activation(gs[:, :, :], o[:, :, :], ACT.Square), [t_g])
                    yield
                    t2 = dve(lambda e: e.tensor_reduce(ms[:, :], gs[:, :, :], AX.X, ALU.add), [t2])
                    t2 = dve(lambda e: e.scalar_tensor_tensor(ms[:, :], ms[:, :], 1.0 / 128, qs[:, :], ALU.mult, ALU.mult), [t2, t_q])
                    t2 = dve(lambda e: e.tensor_tensor(ms[:, :], ms[:, :], qs[:, :], ALU.mult), [t2])
                    t2 = dve(lambda e: e.tensor_scalar(ms[:, :], ms[:, :], 4e-5, None, ALU.add), [t2])
                    t2 = pool(lambda e: e.tensor_tensor(ms[:, :], ms[:, :], pw[:, 0:6], ALU.pow), [t2])
                    t2 = rel["qs"] = pool(lambda e: e.tensor_tensor(ms[:, :], ms[:, :], qs[:, :], ALU.mult), [t2, t_q])
                    yield
                    t1 = []
                    for gr in range(2):
                        t1.append(dve(lambda e, gr=gr: e.tensor_tensor(
                            o[:, 3 * gr:3 * gr + 3, :], o[:, 3 * gr:3 * gr + 3, :], ms[:, 3 * gr:3 * gr + 3].unsqueeze(2).to_broadcast([128, 3, 128]), ALU.mult), [t2]))
                    yield
                    t3 = []
                    for gr in range(2):
                        for j in range(3):
                            t = tr(cols(PS[:, 5 + gr, :], j), o[:, 3 * gr + j, :], [t1[gr], free[5 + gr]], sig=(j == 2))
                        t3.append(act(lambda e, gr=gr: e.activation(grp(gs, gr), PS[:, 5 + gr, 0:384], ACT.Copy), [t]))
                        free[5 + gr] = t3[gr]
                    rel["o"] = t
                    yield
                    for h in range(H):
                        t = mm(PS[:, 5, :], gs[:, h, :], WO[:, h, :], h == 0, h == 5, [t3[h // 3], t_wo, free[5]], sig=(h == 5))
                        if h % 2 == 1:
                            yield
                    rel["gs"] = t
                    t1 = dve(lambda e: e.tensor_tensor(X[:, ch, :], X[:, ch, :], PS[:, 5, :], ALU.add), [t])
                    free[5] = t1
                    t_x_out[ch] = moments(ch, t1)
                    yield

                t_x_out = [None] * NT

                def projections():
                    for B in range(NB):
                        while (B >= 2 and "tab" not in done) or (B >= 3 and ("o", 2 * B - 5) not in done):
                            yield True
                        yield from proj(B)

                def solves(gr):
                    for ch in range(NT):
                        while ("a", ch) not in done or (ch >= 2 and ("o", ch - 2) not in done):
                            yield True
                        yield from solve(ch, gr)

                def prepares():
                    for ch in range(NT):
                        while ch // 2 not in done or (ch >= 3 and ("o", ch - 3) not in done) or (ch >= 2 and (("s", ch - 2, 0) not in done or ("s", ch - 2, 1) not in done)):
                            yield True
                        yield from prepare(ch)

                def outputs():
                    nonlocal t_wo
                    for ch in range(NT):
                        while ("s", ch, 0) not in done or ("s", ch, 1) not in done or "tab" not in done:
                            yield True
                        if ch == 0:
                            t_wo = act(lambda e: e.activation(WO[:, :, :], WO[:, :, :], ACT.Copy, scale=SM[:, 12:13]), [t_wo, t_sm])
                        yield from output(ch)
                        done[("o", ch)] = True

                weave([outputs(), solves(0), solves(1), projections(), prepares(), tables()])
                barrier()
            return t_x_out

        def mixtures(t_in):
            c = ctx.enter_context(ExitStack())

            def s1(name, shape, dt=F32, c=c):
                return sb(name, shape, dt, c)
            NW, NBF, NOB, NXN = 5, 4, 3, 4
            XN = s1("XN", [128, NXN, D])
            XNT = s1("XNT", [128, 4, T])
            GW = s1("GW", [128, 4, E])
            GB = s1("GB", [128, E])
            SW = s1("SW", [128, 3, 4, D])
            W13 = s1("W13", [128, NW, 4, 512])
            W2 = s1("W2", [128, NW, 2, 512])
            shT = s1("shT", [128, 4, 512])
            sth = s1("sth", [128, 2, 512])
            wk = s1("wk", [128, NT, 4])
            slot = s1("slot", [128, E], U32)
            wslot = s1("wslot", [128, E])
            Lm = [line(f"d_m{n}", 16) for n in range(5)]
            Lw = [line(f"d_ew{i}", 16) for i in range(NW)]
            Lb = [line(f"d_eb{i}", 16) for i in range(NBF)]
            Lxn = [line(f"d_exn{i}", 16) for i in range(NXN)]
            Lxb, Lacc = line("d_exb", 16), line("d_eacc", 16)
            Lxi = [line(f"d_exi{i}", 16) for i in range(NT)]
            w13v = a["w13"].rearrange("e (c p) n -> e p c n", p=128)
            w2v = a["w2"].rearrange("e (c p) n -> e p c n", p=128)
            t_ew = {}

            def load_w(y, t_free):
                s, x = y % NW, y % E
                dma(lambda e: e.dma_start(W13[:, s, :, :], w13v[x]), Lw[s], t_free)
                t_ew[y] = dma(lambda e: e.dma_start(W2[:, s, :, :], w2v[x]), Lw[s])

            t_gw = dma(lambda e: e.dma_start(GW[:, :, :], a["gw"].rearrange("(c p) n -> p c n", p=128)), Lm[0])
            t_gb = dma(lambda e: e.dma_start(GB[:, :], a["gb"]), Lm[1])
            t_sw = []
            for j, n in enumerate(("sg", "su", "sd")):
                t_sw.append(dma(lambda e, j=j, n=n: e.dma_start(SW[:, j, :, :], a[n].rearrange("(c p) n -> p c n", p=128)), Lm[2 + j]))
            t_rows = [None]
            t_re = [None] * NT
            t_sth, t_shT = [None, None], [None]
            t_used = {"xn": [None] * NXN, "xnt": None}
            total = (1 if stage < 4 else 2) * E

            def moe(m, t_x0, side=None):
                t_xn, t_xt, t_xs = [None] * NT, [None] * NT, [None] * NT

                def shared(nb4, pairs, downs):
                    while t_xt[4 * nb4 + 3] is None:
                        yield True
                    t_hs = {}
                    for f in range(4):
                        u = f % len(pairs)
                        b0, b1 = pairs[u]
                        for j, b in ((0, b0), (1, b1)):
                            for k in range(4):
                                t = mm(PS[:, b, :], SW[:, j, k, f * 128:(f + 1) * 128], XNT[:, k, nb4 * 512:(nb4 + 1) * 512],
                                       k == 0, k == 3, [t_sw[j], free[b], t_xt[4 * nb4:4 * nb4 + 4]], sig=(k == 3))
                                if k == 1:
                                    yield 3
                            yield 3
                        if f == 3 and nb4 == 3:
                            t_used["xnt"] = t
                        t1 = act(lambda e, u=u, b0=b0: e.activation(sth[:, u, :], PS[:, b0, :], ACT.Tanh, scale=0.5), [t, t_sth[u]])
                        t1 = dve(lambda e, u=u, b0=b0: e.scalar_tensor_tensor(sth[:, u, :], sth[:, u, :], 1.0, PS[:, b0, :], ALU.add, ALU.mult), [t1])
                        t_h = dve(lambda e, u=u, f=f, b1=b1: e.tensor_tensor(shT[:, f, :], sth[:, u, :], PS[:, b1, :], ALU.mult), [t1, t_shT[0]])
                        t_sth[u] = t_h
                        t_hs[f] = free[b0] = free[b1] = t_h
                        yield 3
                    for tl, fs in ((0, (0, 1, 2)), (1, (0, 1, 2)), (0, (3,)), (1, (3,)), (2, (0, 1, 2, 3)), (3, (0, 1, 2, 3))):
                        i = nb4 * 4 + tl
                        b = downs[tl]
                        for f in fs:
                            t = mm(PS[:, b, :], shT[:, f, tl * 128:(tl + 1) * 128], SW[:, 2, f, :], f == 0, f == 3, [t_hs[f], t_sw[2], free[b]], sig=(f == 3))
                            if f == 1:
                                yield 3
                        if fs[-1] == 3:
                            t_xs[i] = dve(lambda e, i=i, b=b: e.scalar_tensor_tensor(X[:, i, :], PS[:, b, :], 0.5, X[:, i, :], ALU.mult, ALU.add), [t, t_xn[i]])
                            free[b] = t_xs[i]
                            route["base"] = dma(lambda e, i=i: e.dma_start(ym[i * 128:(i + 1) * 128, :], X[:, i, :]), Lxb, [t_xs[i]])
                        yield 3
                    t_shT[0] = t

                def norm_tiles(nb4):
                    ii = slice(4 * nb4, 4 * nb4 + 4)
                    t_r = inverse_std(ii, t_x0[ii])
                    for i in range(4 * nb4, 4 * nb4 + 4):
                        s = i % NXN
                        t_xn[i] = normalise(i, XN[:, s, :], [t_r, t_used["xn"][s]])
                        yield
                        t, t_xt[i] = transpose_tile(XN[:, s, :], XNT[:, :, i * 128:(i + 1) * 128], 0, t_xn[i], t_used["xnt"])
                        t_xd[i] = dma(lambda e, i=i, s=s: e.dma_start(xnd[i * 128:(i + 1) * 128, :], XN[:, s, :]), Lxn[s], [t_xn[i], t_rows[0]])
                        t_used["xn"][s] = [t, t_xd[i]]
                        logits(i - 1)
                        yield
                    if nb4 == 3:
                        logits(NT - 1)

                def logits(i):
                    if i < 0:
                        return
                    for k in range(4):
                        t = mm(PS[:, 2, i * E:(i + 1) * E], XNT[:, k, i * 128:(i + 1) * 128], GW[:, k, :], k == 0, k == 3,
                               [t_xt[i], t_gw, free[2]], sig=(k == 3))
                    t_lg[i] = t
                t_xd = [None] * NT
                t_lg = [None] * NT
                route = {}

                def gate(c, nt):
                    def sg(name, shape, dt=F32):
                        return s1(f"{name}_{m}", shape, dt, c)
                    sc = sg("sc", [128, NT, E])
                    sb_ = sg("sbias", [128, NT, E])
                    oh = sg("oh", [128, 4, NT, E])
                    m8 = sg("m8", [128, NT, 4, 8])
                    gsum = sg("gsum", [128, NT, 4])
                    cmp = sg("cmp", [128, NT, 4, 4])
                    cm2 = sg("cm2", [128, NT, 4, 4])
                    cnt = sg("cnt", [128, NT, 4])
                    v8 = sg("v8", [128, NT, 8])
                    i8 = sg("i8", [128, NT, 8], U32)
                    i8f = sg("i8f", [128, NT, 8])
                    ws = sg("ws", [128, NT])
                    msk = sg("msk", [128, NT, E])
                    cum = sg("cum", [128, NT, E])
                    tmp = sg("gtmp", [128, 2, NT, E])
                    pk = sg("pk", [128, 4, NT])
                    op_ = sg("onepos", [128, 2, 4, 128])
                    oe = m8[:, :, :, :].rearrange("p i g n -> p (i g n)").rearrange("p (u k n) -> p u k n", u=2, k=4)
                    yield from nt
                    for y in range(m * E, m * E + NW):
                        load_w(y, None)
                    lg = PS[:, 2, :].rearrange("p (i n) -> p i n", n=E)
                    t1 = act(lambda e: e.activation(sc[:, :, :], lg, ACT.Exp, scale=-1.0), [t_lg[NT - 1]])
                    free[2] = t1
                    t1 = dve(lambda e: e.tensor_scalar(sc[:, :, :], sc[:, :, :], 1.0, None, ALU.add), [t1])
                    t_sc = dve(lambda e: e.reciprocal(sc[:, :, :], sc[:, :, :]), [t1])
                    t1 = dve(lambda e: e.tensor_tensor(sb_[:, :, :], sc[:, :, :], GB[:, :].unsqueeze(1).to_broadcast([128, NT, E]), ALU.add), [t_sc, t_gb])
                    yield
                    for i in range(NT):
                        for gi in range(4):
                            t2 = dve(lambda e, i=i, gi=gi: e.max(m8[:, i, gi, :], sb_[:, i, gi * 8:(gi + 1) * 8]), [t1])
                        if i % 4 == 3:
                            yield
                    t2 = dve(lambda e: e.tensor_tensor(gsum[:, :, :], m8[:, :, :, 0], m8[:, :, :, 1], ALU.add), [t2])
                    gi_ = gsum[:, :, :].unsqueeze(3).to_broadcast([128, NT, 4, 4])
                    gj_ = gsum[:, :, :].unsqueeze(2).to_broadcast([128, NT, 4, 4])
                    cu = CON[:, C_U:C_U + 16].rearrange("p (i j) -> p i j", j=4).unsqueeze(1).to_broadcast([128, NT, 4, 4])
                    cl_ = CON[:, C_L:C_L + 16].rearrange("p (i j) -> p i j", j=4).unsqueeze(1).to_broadcast([128, NT, 4, 4])
                    t3 = dve(lambda e: e.tensor_tensor(cmp[:, :, :, :], gi_, gj_, ALU.is_ge), [t2])
                    t4 = dve(lambda e: e.tensor_tensor(cm2[:, :, :, :], gi_, gj_, ALU.is_gt), [t2])
                    t3 = dve(lambda e: e.tensor_tensor(cmp[:, :, :, :], cmp[:, :, :, :], cu, ALU.mult), [t3])
                    t4 = dve(lambda e: e.tensor_tensor(cm2[:, :, :, :], cm2[:, :, :, :], cl_, ALU.mult), [t4])
                    t3 = dve(lambda e: e.tensor_tensor(cmp[:, :, :, :], cmp[:, :, :, :], cm2[:, :, :, :], ALU.add), [t3, t4])
                    t3 = dve(lambda e: e.tensor_reduce(cnt[:, :, :], cmp[:, :, :, :], AX.X, ALU.add), [t3])
                    t3 = dve(lambda e: e.tensor_scalar(cnt[:, :, :], cnt[:, :, :], 2.0, None, ALU.is_ge), [t3])
                    t3 = dve(lambda e: e.tensor_tensor(
                        sb_[:, :, :].rearrange("p i (g n) -> p i g n", g=4), sb_[:, :, :].rearrange("p i (g n) -> p i g n", g=4),
                        cnt[:, :, :].unsqueeze(3).to_broadcast([128, NT, 4, 8]), ALU.mult), [t3])
                    yield
                    for i in range(NT):
                        t4 = dve(lambda e, i=i: e.max(v8[:, i, :], sb_[:, i, :]), [t3])
                    yield
                    for i in range(NT):
                        t4 = dve(lambda e, i=i: e.max_index(i8[:, i, :], v8[:, i, :], sb_[:, i, :]), [t4])
                    yield
                    t4 = dve(lambda e: e.tensor_copy(i8f[:, :, :], i8[:, :, :]), [t4])
                    io = CON[:, C_IOTA:C_IOTA + 32].unsqueeze(1).to_broadcast([128, NT, E])
                    t5 = []
                    for k in range(4):
                        t5.append(dve(lambda e, k=k: e.tensor_tensor(
                            oh[:, k, :, :], io, i8f[:, :, k:k + 1].to_broadcast([128, NT, E]), ALU.is_equal), [t4]))
                    yield
                    t6 = dve(lambda e: e.tensor_tensor(msk[:, :, :], oh[:, 0, :, :], oh[:, 1, :, :], ALU.add), [t5])
                    t6 = dve(lambda e: e.tensor_tensor(msk[:, :, :], msk[:, :, :], oh[:, 2, :, :], ALU.add), [t6])
                    t_mk = dve(lambda e: e.tensor_tensor(msk[:, :, :], msk[:, :, :], oh[:, 3, :, :], ALU.add), [t6])
                    t6 = dve(lambda e: e.memset(cum[:, 0, :], 0.0))
                    for i in range(1, NT):
                        t6 = dve(lambda e, i=i: e.tensor_tensor(cum[:, i, :], cum[:, i - 1, :], msk[:, i - 1, :], ALU.add), [t6, t_mk])
                    yield
                    mm(PS[:, 3, :], stri, msk[:, :, :].rearrange("p i n -> p (i n)"), True, False, [t_mk, free[3]])
                    t_ps = mm(PS[:, 3, :], ones[:, :], cum[:, :, :].rearrange("p i n -> p (i n)"), False, True, [t6], sig=True)
                    yield
                    pos = PS[:, 3, :].rearrange("p (i n) -> p i n", n=E)
                    t9 = [None, None]
                    for k in range(4):
                        t = dve(lambda e, k=k: e.tensor_tensor(tmp[:, k % 2, :, :], oh[:, k, :, :], pos, ALU.mult), [t_ps, t9[k % 2]])
                        t9[k % 2] = dve(lambda e, k=k: e.tensor_reduce(pk[:, k, :], tmp[:, k % 2, :, :], AX.X, ALU.add), [t])
                        if k == 3:
                            free[3] = t
                        yield
                    t_pk = t9
                    t8 = [t9[0], t9[1]]
                    for k in range(4):
                        t = dve(lambda e, k=k: e.tensor_tensor(tmp[:, k % 2, :, :], oh[:, k, :, :], sc[:, :, :], ALU.mult), [t8[k % 2]])
                        t8[k % 2] = dve(lambda e, k=k: e.tensor_reduce(wk[:, :, k], tmp[:, k % 2, :, :], AX.X, ALU.add), [t])
                        yield
                    t = dve(lambda e: e.tensor_reduce(ws[:, :], wk[:, :, :], AX.X, ALU.add), [t8])
                    t = dve(lambda e: e.tensor_scalar(ws[:, :], ws[:, :], 1e-20, None, ALU.add), [t])
                    t = dve(lambda e: e.reciprocal(ws[:, :], ws[:, :]), [t])
                    t_wk = dve(lambda e: e.tensor_tensor(wk[:, :, :], wk[:, :, :], ws[:, :].unsqueeze(2).to_broadcast([128, NT, 4]), ALU.mult), [t])
                    yield
                    io2 = CON[:, C_IOTA:C_IOTA + 128].unsqueeze(1).to_broadcast([128, 4, 128])
                    t_mp = [None, None]
                    for i in range(NT):
                        u = i % 2
                        t = [dve(lambda e, i=i, u=u: e.tensor_tensor(
                            op_[:, u, :, :], io2, pk[:, :, i].unsqueeze(2).to_broadcast([128, 4, 128]), ALU.is_equal), [t_pk, t_mp[u]])]
                        t.append(dve(lambda e, i=i, u=u: e.tensor_scalar(
                            oe[:, u, :, 0:E], oh[:, :, i, :], CON[:, C_TOK + i:C_TOK + i + 1], None, ALU.mult), [t_mp[u]]))
                        t.append(dve(lambda e, i=i, u=u: e.tensor_tensor(
                            oe[:, u, :, E:2 * E], oh[:, :, i, :], wk[:, i, :].unsqueeze(2).to_broadcast([128, 4, E]), ALU.mult), [t_wk]))
                        yield
                        for k in range(4):
                            t_mp[u] = mm(PS[:, 2, 0:2 * E], op_[:, u, k, :], oe[:, u, k, :], i == 0 and k == 0, i == NT - 1 and k == 3,
                                         [t, free[2]], sig=(k == 3))
                    t = dve(lambda e: e.tensor_scalar(slot[:, :], PS[:, 2, 0:E], float(2 * T), None, ALU.add), [t_mp, t_rows[0]])
                    free[2] = route["map"] = dve(lambda e: e.tensor_copy(wslot[:, :], PS[:, 2, E:2 * E]), [t])
                    yield

                def experts(c):
                    Bf = s1(f"Bf_{m}", [128, NBF, D], F32, c)
                    BT = s1(f"BT_{m}", [128, 2, 4, 128], F32, c)
                    eth = s1(f"eth_{m}", [128, 2, 256], F32, c)
                    hT = s1(f"hT_{m}", [128, 2, 2, 128], F32, c)
                    OB = s1(f"OB_{m}", [128, NOB, D], F32, c)
                    t_b, t_tr, t_bt, t_w13, t_h, t_w2, t_st = {}, {}, {}, {}, {}, {}, {}

                    def load(x):
                        s = x % NBF
                        t_b[x] = dma(lambda e: e.indirect_dma_start(
                            out=Bf[:, s, :], out_offset=None, in_=xnd,
                            in_offset=bass.IndirectOffsetOnAxis(ap=slot[:, x:x + 1], axis=0), bounds_check=T - 1, oob_is_err=False),
                            Lb[s], [route["map"], t_xd[NT - NXN:], t_bf, t_tr.get(x - NBF)], "gpsimd")

                    def turn(x):
                        s, b, u = x % NBF, x % 2, x % 2
                        t_tr[x], t_bt[x] = transpose_tile(Bf[:, s, :], BT[:, u, :, :], b, t_b[x], t_w13.get(x - 2))

                    def hidden(x):
                        u, b, w = x % 2, 2 + x % 2, (m * E + x) % NW
                        for f in range(4):
                            for k in range(4):
                                t = mm(PS[:, b, f * 128:(f + 1) * 128], W13[:, w, k, f * 128:(f + 1) * 128], BT[:, u, k, :], k == 0, k == 3,
                                       [t_bt[x], t_ew[m * E + x], free[b]], sig=(f == 3 and k == 3))
                        t_w13[x] = t
                        t1 = act(lambda e: e.activation(eth[:, u, :], PS[:, b, 0:256], ACT.Tanh, scale=0.5), [t, t_h.get(x - 2)])
                        t1 = dve(lambda e: e.scalar_tensor_tensor(eth[:, u, :], eth[:, u, :], 1.0, PS[:, b, 0:256], ALU.add, ALU.mult), [t1])
                        t_h[x] = dve(lambda e: e.tensor_tensor(
                            hT[:, u, :, :].rearrange("p k n -> p (k n)"), eth[:, u, :], PS[:, b, 256:512], ALU.mult), [t1, t_w2.get(x - 2)])
                        free[b] = t_h[x]

                    def down(x):
                        u, b, w, s = x % 2, 4 + x % 2, (m * E + x) % NW, x % NOB
                        for k in range(2):
                            t = mm(PS[:, b, :], hT[:, u, k, :], W2[:, w, k, :], k == 0, k == 1, [t_h[x], free[b]], sig=(k == 1))
                        t_w2[x] = t
                        if x + NW < E:
                            load_w(m * E + x + NW, t)
                        t1 = act(lambda e: e.activation(OB[:, s, :], PS[:, b, :], ACT.Copy, scale=wslot[:, x:x + 1]), [t, t_st.get(x - NOB)])
                        free[b] = t1
                        t_st[x] = dma(lambda e: e.indirect_dma_start(
                            out=ym, out_offset=bass.IndirectOffsetOnAxis(ap=slot[:, x:x + 1], axis=0), in_=OB[:, s, :], in_offset=None,
                            bounds_check=T - 1, oob_is_err=False, compute_op=ALU.add), Lacc, [t1, route["base"], t_st.get(x - 1)], "gpsimd")

                    t_bf = pool(lambda e: e.memset(Bf[:, :, :], 0.0))
                    for x in range(NBF):
                        load(x)
                    for x in range(-2, E):
                        if x + 2 < E:
                            turn(x + 2)
                            if x + 2 + NBF < E:
                                load(x + 2 + NBF)
                        if 0 <= x + 1 < E:
                            hidden(x + 1)
                        yield
                        if x >= 0:
                            down(x)
                            yield
                    route["acc"] = t_rows[0] = t_st[E - 1]

                ym = (yd, out[0])[m]

                def reload(tiles):
                    for i in tiles:
                        t_re[i] = dma(lambda e, i=i: e.dma_start(X[:, i, :], yd[i * 128:(i + 1) * 128, :]), Lxi[i], [route["acc"]])

                def norms():
                    for nb4 in range(4):
                        while t_x0[4 * nb4 + 3] is None:
                            yield True
                        yield from norm_tiles(nb4)

                def chain():
                    for nb4 in range(4):
                        yield from shared(nb4, ((4, 5), (6, 7)), (4, 5, 6, 7))
                nt, sh = norms(), chain()
                if side is not None:
                    with ExitStack() as c1:
                        front, back = side(c1)
                        if stage == 3:
                            weave([back, front])
                            return None
                        weave([back, front, nt, sh], [back, front])
                    fence(t_x0)
                with ExitStack() as c1:
                    weave([gate(c1, nt), sh])
                fence([route["map"]])
                with ExitStack() as c1:
                    for _ in experts(c1):
                        pass
                fence([route["acc"], free])
                return reload

            def lru(c, reload, t_xi, t_o):
                ring = W13[:, :, :, :].rearrange("p s k n -> p (s k n)")
                xr = ring[:, 0:2 * T].rearrange("p (s k n) -> p s k n", s=2, k=4)
                Ct, St = ring[:, 2 * T:3 * T], ring[:, 3 * T:4 * T]
                xl = ring[:, 4 * T:5 * T].rearrange("p (s n) -> p s n", s=4)
                BW = s1("BW", [128, 2, 4, 128], F32, c)
                CWt = s1("CWt", [128, 2, 512], F32, c)
                DD = s1("DD", [128, 4], F32, c)
                dD = s1("dD", [128, 4, 128], F32, c)
                nmr = s1("nmr", [128, NT], F32, c)
                bu = s1("bu", [128, 2, 512], F32, c)
                r = s1("r", [128, 512], F32, c)
                g = s1("gst", [128, 2, 512], F32, c)
                pr = s1("pr", [128, 2, 512], F32, c)
                LL = [line(f"d_l{i}", 16) for i in range(4)]

                def col(j):
                    return LS[:, j:j + 1]
                t_bw = [dma(lambda e, j=j: e.dma_start(BW[:, j, :, :], a[("bt", "btsw")[j]].rearrange("(c p) n -> p c n", p=128)), LL[0]) for j in range(2)][1]
                t_cw = [dma(lambda e, j=j: e.dma_start(CWt[:, j, :], a[("ct", "ctsw")[j]]), LL[1]) for j in range(2)][1]
                t_dd = dma(lambda e: e.dma_start(DD[:, :], a["dvec"]), LL[2])
                t_tb = [(ln, ln.n) for ln in L_tb]
                reload(range(4))
                t_rot = [dma(lambda e, j=j: e.dma_start((Ct, St)[j], tabs[j]), LL[3], [t_tb]) for j in range(2)][1]
                reload(range(4, NT))
                t_cw = dve(lambda e: e.tensor_scalar(CWt[:, 0, :], CWt[:, 0, :], CON[:, C_SGN:C_SGN + 1], None, ALU.mult), [t_cw])
                t_cw = dve(lambda e: e.tensor_scalar(CWt[:, 1, :], CWt[:, 1, :], -1.0, None, ALU.mult), [t_cw])
                for k in range(4):
                    t_dd = dve(lambda e, k=k: e.tensor_scalar(dD[:, k, :], ident, DD[:, k:k + 1], None, ALU.mult), [t_dd])
                t_xr, t_sl, t_xt = [None] * 4, [None] * 4, {}

                def front():
                    t_sd, t_xl = {}, {}
                    for i in range(-2, NT):
                        n, s = i // 4, i % 4
                        if i + 2 < NT:
                            t = moments(i + 2, t_xi[i + 2])
                            t_sd[i + 2] = act(lambda e, i=i: e.activation(rstd[:, i + 2:i + 3], bmv[:, i + 2, 1:2], ACT.Sqrt, bias=eps[:, :]), [t, t_eps])
                        if 0 <= i + 1 < NT:
                            y = i + 1
                            t = dve(lambda e, y=y: e.reciprocal(rstd[:, y:y + 1], rstd[:, y:y + 1]), [t_sd[y]])
                            t = dve(lambda e, y=y: e.scalar_tensor_tensor(nmr[:, y:y + 1], bmv[:, y, 0:1], -1.0, rstd[:, y:y + 1], ALU.mult, ALU.mult), [t])
                            t_xl[y] = act(lambda e, y=y: e.activation(xl[:, y % 4, :], X[:, y, :], ACT.Identity, bias=nmr[:, y:y + 1], scale=rstd[:, y:y + 1]),
                                          [t, t_sl[y % 4]])
                        if i < 0:
                            yield
                            continue
                        while n > 1 and t_xr[n - 2] is None:
                            yield True
                        t_sl[s], t_xt[i] = transpose_tile(
                            xl[:, s, :], xr[:, n % 2, :, (i % 4) * 128:(i % 4) * 128 + 128], 0, t_xl[i], [t_xr[n - 2] if n > 1 else None])
                        yield

                def back():
                    t_g, t_pr, t_r, t1 = None, None, [None, None], [None, None]
                    late = []

                    def finish():
                        if late:
                            i, b, t = late.pop()
                            free[b] = dve(lambda e: e.tensor_tensor(X[:, i, :], X[:, i, :], PS[:, b, :], ALU.add), [t])
                            t_o[i] = moments(i, free[b])
                    for n in range(4):
                        ns = slice(n * 512, n * 512 + 512)
                        u = n % 2
                        while 4 * n + 3 not in t_xt:
                            yield True
                        finish()
                        for j in range(2):
                            b = (1, 3)[j]
                            for k in range(4):
                                t = mm(PS[:, b, :], BW[:, j, k, :], xr[:, u, k, :], k == 0, k == 3,
                                       [t_bw, [t_xt[i] for i in range(4 * n, 4 * n + 4)], free[b]], sig=(k == 3))
                            tab = (Ct, St)[j]
                            free[b] = t_r[j] = dve(lambda e, j=j, b=b, tab=tab, ns=ns: e.scalar_tensor_tensor(
                                bu[:, j, :], PS[:, b, :], col(3 + j), tab[:, ns], ALU.mult, ALU.mult), [t, t_rot])
                        t = dve(lambda e: e.tensor_tensor(r[:, :], bu[:, 0, :], bu[:, 1, :], ALU.add), [t_r, t_g])
                        init = 0.0 if n == 0 else g[:, 1 - u, 511:512]
                        t_g = dve(lambda e, u=u, init=init: e.tensor_tensor_scan(
                            g[:, u, :], col(2).to_broadcast([128, 512]), r[:, :], init, ALU.mult, ALU.add), [t, t_g])
                        for j, tab in ((0, Ct), (1, St)):
                            t1[j] = (dve, pool)[j](lambda e, j=j, tab=tab, ns=ns, u=u: e.tensor_tensor(pr[:, j, :], g[:, u, :], tab[:, ns], ALU.mult), [t_g, t_pr])
                        yield
                        for i in range(4 * n, 4 * n + 4):
                            b = (1, 3)[i % 2]
                            lt = slice((i % 4) * 128, (i % 4) * 128 + 128)
                            for k in range(4):
                                mm(PS[:, b, k * 128:k * 128 + 128], xr[:, u, k, lt], dD[:, k, :], True, False, [t_dd, free[b]])
                                mm(PS[:, b, k * 128:k * 128 + 128], pr[:, 0, lt], CWt[:, 0, k * 128:k * 128 + 128], False, False, [t1, t_cw])
                                t = mm(PS[:, b, k * 128:k * 128 + 128], pr[:, 1, lt], CWt[:, 1, k * 128:k * 128 + 128], False, True, sig=(k == 3))
                            finish()
                            late.append((i, b, t))
                            yield
                        t_xr[n] = t_pr = t
                    finish()
                return front(), back()

            t_mid = [None] * NT
            t_back = moe(0, t_in)
            if stage == 2:
                t_back(range(NT))
            if stage >= 3:
                moe(1, t_mid, lambda c: lru(c, t_back, t_re, t_mid))

        L_out = line("d_out", 16)
        ov = out.rearrange("b (i p) n -> p (b i) n", p=128)
        t_o = delta_net()
        if stage >= 2:
            mixtures(t_o)
        if stage < 4:
            barrier()
            dma(lambda e: e.dma_start(ov, X[:, :, :]), L_out)
        q["sync"].append(([(ln, ln.n) for ln in lines], None, None))

        block = ctx.enter_context(nc.Block())

        def run(eng, name):
            seen = {}
            for waits, fn, on in q[name]:
                need = {}
                for ln, v in waits:
                    if v > seen.get(ln, 0):
                        need[ln] = max(v, need.get(ln, 0))
                for ln, v in need.items():
                    eng.wait_ge(ln.sem, v)
                    seen[ln] = v
                if fn is not None:
                    ins = fn(eng)
                    if on is not None:
                        ins.then_inc(on.sem, on.by)

        @block.sync
        def _(eng):
            run(eng, "sync")

        @block.scalar
        def _(eng):
            run(eng, "scalar")

        @block.vector
        def _(eng):
            run(eng, "vector")

        @block.tensor
        def _(eng):
            run(eng, "tensor")

        @block.gpsimd
        def _(eng):
            run(eng, "gpsimd")


def layout(i):
    import numpy as _np
    f = lambda n: _np.asarray(i["L0_" + n])
    cat = _np.concatenate
    rows = lambda v: _np.broadcast_to(v, (128,) + v.shape)
    small = _np.zeros((128, 16), _np.float32)
    order = [0, 2, 4, 1, 3, 5]
    heads = lambda v: v.reshape((H, -1) + v.shape[1:])[order].reshape(v.shape)
    small[:, 0:6] = heads(f("attn_a_dt_bias"))
    small[:, 6:12] = heads(f("attn_a_A_log"))
    small[:, 12] = f("attn_a_norm_w")
    br, bi, cr, ci = (f("attn_b_" + n).T for n in ("B_re", "B_im", "C_re", "C_im"))
    lsm = _np.stack([cat([f("attn_b_nu_log")] * 2), cat([f("attn_b_theta_log")] * 2)], 1)
    d = {
        "x": f("attn_a_x"), "consts": shape_constants(), "small": small, "lsm": lsm,
        "wqkvg": cat([f("attn_a_Wq"), f("attn_a_Wk"), heads(f("attn_a_Wv")), heads(f("attn_a_Wg"))]).T,
        "wab": cat([heads(f("attn_a_Wa")), heads(f("attn_a_Wb"))]).T, "wo": heads(f("attn_a_Wo").T),
        "convw": cat([f("attn_a_conv_q_w"), f("attn_a_conv_k_w"), heads(f("attn_a_conv_v_w"))])[:, 0, :],
        "bt": cat([br, bi], 1), "btsw": cat([bi, br], 1), "ct": cat([cr, ci]), "ctsw": cat([ci, cr]),
        "tidx": rows(_np.arange(T, dtype=_np.float32)), "dvec": f("attn_b_D").reshape(4, 128).T, "gw": f("ffn_gate_w").T, "gb": rows(f("ffn_gate_bias")),
        "w13": cat([f("ffn_w1"), f("ffn_w3")], 2), "w2": f("ffn_w2"),
        "sg": f("ffn_shared_gate"), "su": f("ffn_shared_up"), "sd": f("ffn_shared_down"),
    }
    return {k: _np.ascontiguousarray(v) for k, v in d.items()}


def kernel(**inputs):
    import numpy as _np
    import concourse.bacc as _bacc
    from concourse import mybir as _mybir
    from concourse.bass_utils import run_bass_kernel_spmd as _run

    nc = _bacc.Bacc("TRN2", target_bir_lowering=False, num_devices=1)
    arrays, args = {}, {}
    for name, v in layout(inputs).items():
        arrays[f"in_{name}_dram"] = v
        args[name] = nc.dram_tensor(f"in_{name}_dram", v.shape, _mybir.dt.from_np(v.dtype), kind="ExternalInput").ap()
    out = nc.dram_tensor("out_0_dram", (1, 2048, 512), _mybir.dt.float32, kind="ExternalOutput").ap()
    program(nc, args, out)
    r = _run(nc, [arrays], core_ids=[0])
    return r.results[0]["out_0_dram"]
```
